# Optimizing a Trainium2 kernel written in Bass

```python
import numpy as np
import jax
import jax.numpy as jnp

def _softmax(x, axis=-1):
    return jax.nn.softmax(x, axis=axis)

def _gelu(x):
    return jax.nn.gelu(x, approximate=True)

def _silu(x):
    return jax.nn.silu(x)

def _sigmoid(x):
    return jax.nn.sigmoid(x)

def _layernorm(x, axis=-1, eps=1e-05):
    m = jnp.mean(x, axis=axis, keepdims=True)
    v = jnp.var(x, axis=axis, keepdims=True)
    return (x - m) / jnp.sqrt(v + eps)

def _scatter_add(tgt, idx, src, axis=0):
    return tgt.at[idx].add(src)

def _segment_sum(src, seg, n):
    return jax.ops.segment_sum(src, seg, n)
kernel_name = 'mk_flamingo_gated_d4_seqx_r8_8a6472'

def setup_inputs(seed: int=0):
    np.random.seed(seed)
    _w = jnp.asarray

    def _rec_inputs():
        import jax
        import jax.numpy as jnp
        _rk = jax.random.key(seed)
        x = -0.0002928 + 1 * jax.random.normal(jax.random.fold_in(_rk, 1), (4, 512, 128), jnp.float32)
        _lenS = 512 - jax.random.randint(jax.random.fold_in(_rk, 7), (4,), 0, max(1, 512 // 4) + 1, jnp.int32)
        _lenS2 = 77 - jax.random.randint(jax.random.fold_in(_rk, 8), (4,), 0, max(1, 77 // 4) + 1, jnp.int32)
        _ctx_1024P = jax.random.normal(jax.random.fold_in(_rk, 11), (4, 16, 128), jnp.float32)
        _ctx_1024c = jax.random.dirichlet(jax.random.fold_in(_rk, 511), 0.3 * jnp.ones((16,), jnp.float32), (4, 77))
        _ctx_1024t = jnp.einsum('bsk,bkd->bsd', _ctx_1024c, _ctx_1024P)
        _ctx_1024t = _ctx_1024t * jax.lax.rsqrt(jnp.mean(jnp.square(_ctx_1024t)) + 1e-12) * 0.953939
        ctx_1024 = -1.39393e-06 + 0.999914 * (_ctx_1024t + 0.3 * jax.random.normal(jax.random.fold_in(_rk, 611), (4, 77, 128), jnp.float32))
        _validS = jnp.arange(512)[None, :] < _lenS[:, None]
        _validS2 = jnp.arange(77)[None, :] < _lenS2[:, None]
        _causal = jnp.tril(jnp.ones((512, 512), dtype=bool))
        mask_BxSxS2_bk0 = jnp.logical_not(jnp.broadcast_to(_validS2[:, None, :], (4, 512, 77)))
        mask_Bx1x1xS2_bf1 = jnp.ones((4, 1, 1, 77), dtype=bool)
        _g = jax.random.normal(jax.random.fold_in(_rk, 9001), (2, 4), jnp.float32)
        _g = jnp.sign(_g) * jnp.maximum(jnp.abs(_g), 1.0) + (_g == 0) * 1.0
        g_xattn = _g[0]
        g_ffn = _g[1]
        return (x, ctx_1024, mask_BxSxS2_bk0, mask_Bx1x1xS2_bf1, g_xattn, g_ffn)
    x, ctx_1024, mask_BxSxS2_bk0, mask_Bx1x1xS2_bf1, g_xattn, g_ffn = _rec_inputs()

    def _L0_xattn_setup():
        import jax, jax.numpy as jnp
        import numpy as np
        HIDDEN = 128
        HEADS = 16
        HEAD_DIM = HIDDEN // HEADS

        def _split_heads(x):
            b, n, _ = x.shape
            return x.reshape(b, n, HEADS, HEAD_DIM).transpose(0, 2, 1, 3)
        key = jax.random.key(seed)
        ks = jax.random.split(key, 11)
        B, N, D = (2, 256, HIDDEN)
        scale = 1.0 / np.sqrt(D)
        inp = {'q': jax.random.normal(ks[0], (B, N, D), jnp.float32), 'k': jax.random.normal(ks[1], (B, N, D), jnp.float32), 'v': jax.random.normal(ks[2], (B, N, D), jnp.float32), 'Wq': jax.random.normal(ks[3], (D, D), jnp.float32) * scale, 'bq': jnp.zeros((D,), jnp.float32), 'Wk': jax.random.normal(ks[4], (D, D), jnp.float32) * scale, 'bk': jnp.zeros((D,), jnp.float32), 'Wv': jax.random.normal(ks[5], (D, D), jnp.float32) * scale, 'bv': jnp.zeros((D,), jnp.float32), 'Wo': jax.random.normal(ks[6], (D, D), jnp.float32) * scale, 'bo': jnp.zeros((D,), jnp.float32)}
        return inp
    _L0_xattn_all = _L0_xattn_setup()
    _L0_xattn_in = {k: v for k, v in _L0_xattn_all.items() if k in ('Wq', 'bq', 'Wk', 'bk', 'Wv', 'bv', 'Wo', 'bo')}
    del _L0_xattn_all

    def _L0_ffn_setup():
        import jax, jax.numpy as jnp
        import numpy as np
        B, S, H, E = (4, 256, 128, 8)
        key = jax.random.key(seed)
        k1, k2, k3 = jax.random.split(key, 3)
        scale_w = 1.0 / np.sqrt(H)
        return {'x': jax.random.normal(k1, (B, S, H), dtype=jnp.float32), 'router_w': jax.random.normal(k2, (H, E), dtype=jnp.float32) * scale_w, 'router_b': jnp.zeros((E,), dtype=jnp.float32), 'expert_w': jax.random.normal(k3, (E, H, H), dtype=jnp.float32) * scale_w, 'expert_b': jnp.zeros((E, H), dtype=jnp.float32)}
    _L0_ffn_all = _L0_ffn_setup()
    _L0_ffn_in = {k: v for k, v in _L0_ffn_all.items() if k in ('router_w', 'router_b', 'expert_w', 'expert_b')}
    del _L0_ffn_all

    def _L1_xattn_setup():
        import jax, jax.numpy as jnp
        import numpy as np
        EPS = 1e-05
        NEG_BIAS = -1000000000.0
        N_HEADS = 16

        def layer_norm(x, gamma, beta):
            mu = jnp.mean(x, axis=-1, keepdims=True)
            var = jnp.mean(jnp.square(x - mu), axis=-1, keepdims=True)
            return (x - mu) * jax.lax.rsqrt(var + EPS) * gamma + beta

        def split_heads(x, n_heads):
            b, s, d = x.shape
            return x.reshape(b, s, n_heads, d // n_heads).transpose(0, 2, 1, 3)
        key = jax.random.key(seed)
        ks = jax.random.split(key, 12)
        B, S, D = (2, 256, 128)
        inp = {'query_antecedent': jax.random.normal(ks[0], (B, S, D), jnp.float32), 'key_antecedent': jax.random.normal(ks[1], (B, S, D), jnp.float32), 'value_antecedent': jax.random.normal(ks[2], (B, S, D), jnp.float32), 'mask': jnp.tril(jnp.ones((S, S), jnp.bool_))[None].repeat(B, axis=0), 'Wq': jax.random.normal(ks[3], (D, D), jnp.float32) * (1.0 / np.sqrt(D)), 'Wk': jax.random.normal(ks[4], (D, D), jnp.float32) * (1.0 / np.sqrt(D)), 'Wv': jax.random.normal(ks[5], (D, D), jnp.float32) * (1.0 / np.sqrt(D)), 'gq': jnp.ones((D,), jnp.float32), 'bq': jnp.zeros((D,), jnp.float32), 'gk': jnp.ones((D,), jnp.float32), 'bk': jnp.zeros((D,), jnp.float32), 'gv': jnp.ones((D,), jnp.float32), 'bv': jnp.zeros((D,), jnp.float32)}
        return inp
    _L1_xattn_all = _L1_xattn_setup()
    _L1_xattn_in = {k: v for k, v in _L1_xattn_all.items() if k in ('Wq', 'Wk', 'Wv', 'gq', 'bq', 'gk', 'bk', 'gv', 'bv')}
    del _L1_xattn_all

    def _L1_ffn_setup():
        import jax, jax.numpy as jnp
        import numpy as np
        DIM = 128
        NUM_EXPERTS = 8
        HID = 4 * DIM
        key = jax.random.key(seed)
        ks = jax.random.split(key, 9)
        B, T = (4, 128)
        s = 0.02
        return {'x': jax.random.normal(ks[0], (B, T, DIM), dtype=jnp.float32), 'gate_w': jax.random.normal(ks[1], (NUM_EXPERTS, DIM), dtype=jnp.float32) * s, 'wg': jax.random.normal(ks[2], (NUM_EXPERTS, HID, DIM), dtype=jnp.float32) * s, 'bg': jax.random.normal(ks[3], (NUM_EXPERTS, HID), dtype=jnp.float32) * s, 'wi': jax.random.normal(ks[4], (NUM_EXPERTS, HID, DIM), dtype=jnp.float32) * s, 'bi': jax.random.normal(ks[5], (NUM_EXPERTS, HID), dtype=jnp.float32) * s, 'wo': jax.random.normal(ks[6], (NUM_EXPERTS, DIM, HID), dtype=jnp.float32) * s, 'bo': jax.random.normal(ks[7], (NUM_EXPERTS, DIM), dtype=jnp.float32) * s}
    _L1_ffn_all = _L1_ffn_setup()
    _L1_ffn_in = {k: v for k, v in _L1_ffn_all.items() if k in ('gate_w', 'wg', 'bg', 'wi', 'bi', 'wo', 'bo')}
    del _L1_ffn_all

    def _L2_xattn_setup():
        import jax, jax.numpy as jnp
        import numpy as np
        B, L, D_MODEL, H, DK, DV = (4, 256, 128, 16, 64, 64)
        key = jax.random.key(seed)
        ks = jax.random.split(key, 11)
        s = 1.0 / np.sqrt(D_MODEL)
        return {'queries': jax.random.normal(ks[0], (B, L, D_MODEL), jnp.float32), 'keys': jax.random.normal(ks[1], (B, L, D_MODEL), jnp.float32), 'values': jax.random.normal(ks[2], (B, L, D_MODEL), jnp.float32), 'Wq': jax.random.normal(ks[3], (D_MODEL, H * DK), jnp.float32) * s, 'bq': jnp.zeros((H * DK,), jnp.float32), 'Wk': jax.random.normal(ks[4], (D_MODEL, H * DK), jnp.float32) * s, 'bk': jnp.zeros((H * DK,), jnp.float32), 'Wv': jax.random.normal(ks[5], (D_MODEL, H * DV), jnp.float32) * s, 'bv': jnp.zeros((H * DV,), jnp.float32), 'Wo': jax.random.normal(ks[6], (H * DV, D_MODEL), jnp.float32) * s, 'bo': jnp.zeros((D_MODEL,), jnp.float32)}
    _L2_xattn_all = _L2_xattn_setup()
    _L2_xattn_in = {k: v for k, v in _L2_xattn_all.items() if k in ('Wq', 'bq', 'Wk', 'bk', 'Wv', 'bv', 'Wo', 'bo')}
    del _L2_xattn_all

    def _L2_ffn_setup():
        import jax, jax.numpy as jnp
        import numpy as np
        EMB = 128
        HEADS = 16
        SEQ = 256
        LATENT = 64
        N_EXP = 8
        TOP_K = 2
        EXP_DIM = 256
        BATCH = 2
        EPS = 1e-06

        def _rmsnorm(x, g):
            return x * jax.lax.rsqrt(jnp.mean(x * x, axis=-1, keepdims=True) + EPS) * g

        def _mla(h, Wq, Wdkv, Wuk, Wuv, Wo):
            B, S, D = h.shape
            hd = D // HEADS
            q = (h @ Wq).reshape(B, S, HEADS, hd)
            c = h @ Wdkv
            k = (c @ Wuk).reshape(B, S, HEADS, hd)
            v = (c @ Wuv).reshape(B, S, HEADS, hd)
            scores = jnp.einsum('bqhd,bkhd->bhqk', q, k) / jnp.sqrt(jnp.asarray(hd, h.dtype))
            causal = jnp.tril(jnp.ones((S, S), bool))
            scores = jnp.where(causal, scores, jnp.asarray(-1000000000.0, h.dtype))
            a = jax.nn.softmax(scores, axis=-1)
            out = jnp.einsum('bhqk,bkhd->bqhd', a, v).reshape(B, S, D)
            return out @ Wo

        def _moe(h, gate_w, w1, w2):
            B, S, D = h.shape
            t = h.reshape(B * S, D)
            logits = t @ gate_w
            top_v, top_i = jax.lax.top_k(logits, TOP_K)
            gates = jax.nn.softmax(top_v, axis=-1)
            T = t.shape[0]
            combine = jnp.zeros((T, N_EXP), t.dtype).at[jnp.arange(T)[:, None], top_i].add(gates)
            hid = jax.nn.silu(jnp.einsum('td,edh->teh', t, w1))
            ye = jnp.einsum('teh,ehd->ted', hid, w2)
            out = jnp.einsum('te,ted->td', combine, ye)
            return out.reshape(B, S, D)
        key = jax.random.key(seed)
        ks = jax.random.split(key, 12)
        s = 0.02
        return {'x': jax.random.normal(ks[0], (BATCH, SEQ, EMB), jnp.float32), 'g1': jnp.ones((EMB,), jnp.float32), 'Wq': jax.random.normal(ks[1], (EMB, EMB), jnp.float32) * s, 'Wdkv': jax.random.normal(ks[2], (EMB, LATENT), jnp.float32) * s, 'Wuk': jax.random.normal(ks[3], (LATENT, EMB), jnp.float32) * s, 'Wuv': jax.random.normal(ks[4], (LATENT, EMB), jnp.float32) * s, 'Wo': jax.random.normal(ks[5], (EMB, EMB), jnp.float32) * s, 'g2': jnp.ones((EMB,), jnp.float32), 'gate_w': jax.random.normal(ks[6], (EMB, N_EXP), jnp.float32) * s, 'w1': jax.random.normal(ks[7], (N_EXP, EMB, EXP_DIM), jnp.float32) * s, 'w2': jax.random.normal(ks[8], (N_EXP, EXP_DIM, EMB), jnp.float32) * s}
    _L2_ffn_all = _L2_ffn_setup()
    _L2_ffn_in = {k: v for k, v in _L2_ffn_all.items() if k in ('g1', 'Wq', 'Wdkv', 'Wuk', 'Wuv', 'Wo', 'g2', 'gate_w', 'w1', 'w2')}
    del _L2_ffn_all

    def _L3_xattn_setup():
        import math
        import jax, jax.numpy as jnp
        import numpy as np
        D_MODEL = 128
        N_HEADS = 16
        D_K = D_MODEL // N_HEADS

        def _rope(x):
            s, d = (x.shape[2], x.shape[3])
            pos = jnp.arange(s, dtype=x.dtype)[:, None]
            inv = 10000.0 ** (jnp.arange(0, d, 2, dtype=x.dtype) / d)
            theta = pos / inv
            sin = jnp.repeat(jnp.sin(theta), 2, axis=-1)
            cos = jnp.repeat(jnp.cos(theta), 2, axis=-1)
            rot = jnp.stack([-x[..., 1::2], x[..., 0::2]], axis=-1).reshape(x.shape)
            return x * cos + rot * sin
        key = jax.random.key(seed)
        ks = jax.random.split(key, 12)
        b, s, d = (2, 256, D_MODEL)
        sc = 1.0 / math.sqrt(d)
        inp = {'q': jax.random.normal(ks[0], (b, s, d), jnp.float32), 'k': jax.random.normal(ks[1], (b, s, d), jnp.float32), 'v': jax.random.normal(ks[2], (b, s, d), jnp.float32), 'mask': jnp.ones((b, 1, 1, s), dtype=bool), 'w_q': jax.random.normal(ks[3], (d, d), jnp.float32) * sc, 'b_q': jnp.zeros((d,), jnp.float32), 'w_k': jax.random.normal(ks[4], (d, d), jnp.float32) * sc, 'b_k': jnp.zeros((d,), jnp.float32), 'w_v': jax.random.normal(ks[5], (d, d), jnp.float32) * sc, 'b_v': jnp.zeros((d,), jnp.float32), 'w_o': jax.random.normal(ks[6], (d, d), jnp.float32) * sc, 'b_o': jnp.zeros((d,), jnp.float32)}
        return inp
    _L3_xattn_all = _L3_xattn_setup()
    _L3_xattn_in = {k: v for k, v in _L3_xattn_all.items() if k in ('w_q', 'b_q', 'w_k', 'b_k', 'w_v', 'b_v', 'w_o', 'b_o')}
    del _L3_xattn_all

    def _L3_ffn_setup():
        import jax, jax.numpy as jnp
        import numpy as np
        B, S, H = (8, 512, 128)
        NAV = 128
        E = 8
        F = 2 * H
        key = jax.random.key(seed)
        ks = jax.random.split(key, 12)

        def w(k, shape, fan_in):
            return jax.random.normal(k, shape, dtype=jnp.float32) / np.sqrt(fan_in)
        return {'hidden_states': jax.random.normal(ks[0], (B, S, H), dtype=jnp.float32), 'Wp1': w(ks[1], (H, NAV), H), 'bp1': jnp.zeros((NAV,), jnp.float32), 'Wp2': w(ks[2], (NAV, E), NAV), 'bp2': jnp.zeros((E,), jnp.float32), 'W1': w(ks[3], (E, H, F), H), 'b1': jnp.zeros((E, F), jnp.float32), 'W2': w(ks[4], (E, F, H), F), 'b2': jnp.zeros((E, H), jnp.float32), 'Wo': w(ks[5], (H, H), H), 'bo': jnp.zeros((H,), jnp.float32)}
    _L3_ffn_all = _L3_ffn_setup()
    _L3_ffn_in = {k: v for k, v in _L3_ffn_all.items() if k in ('Wp1', 'bp1', 'Wp2', 'bp2', 'W1', 'b1', 'W2', 'b2', 'Wo', 'bo')}
    del _L3_ffn_all
    return {'x': x, 'ctx_1024': ctx_1024, 'mask_BxSxS2_bk0': mask_BxSxS2_bk0, 'mask_Bx1x1xS2_bf1': mask_Bx1x1xS2_bf1, 'g_xattn': g_xattn, 'g_ffn': g_ffn, 'L0_xattn_Wq': _L0_xattn_in['Wq'], 'L0_xattn_bq': _L0_xattn_in['bq'], 'L0_xattn_Wk': _L0_xattn_in['Wk'], 'L0_xattn_bk': _L0_xattn_in['bk'], 'L0_xattn_Wv': _L0_xattn_in['Wv'], 'L0_xattn_bv': _L0_xattn_in['bv'], 'L0_xattn_Wo': _L0_xattn_in['Wo'], 'L0_xattn_bo': _L0_xattn_in['bo'], 'L0_ffn_router_w': _L0_ffn_in['router_w'], 'L0_ffn_router_b': _L0_ffn_in['router_b'], 'L0_ffn_expert_w': _L0_ffn_in['expert_w'], 'L0_ffn_expert_b': _L0_ffn_in['expert_b'], 'L1_xattn_Wq': _L1_xattn_in['Wq'], 'L1_xattn_Wk': _L1_xattn_in['Wk'], 'L1_xattn_Wv': _L1_xattn_in['Wv'], 'L1_xattn_gq': _L1_xattn_in['gq'], 'L1_xattn_bq': _L1_xattn_in['bq'], 'L1_xattn_gk': _L1_xattn_in['gk'], 'L1_xattn_bk': _L1_xattn_in['bk'], 'L1_xattn_gv': _L1_xattn_in['gv'], 'L1_xattn_bv': _L1_xattn_in['bv'], 'L1_ffn_gate_w': _L1_ffn_in['gate_w'], 'L1_ffn_wg': _L1_ffn_in['wg'], 'L1_ffn_bg': _L1_ffn_in['bg'], 'L1_ffn_wi': _L1_ffn_in['wi'], 'L1_ffn_bi': _L1_ffn_in['bi'], 'L1_ffn_wo': _L1_ffn_in['wo'], 'L1_ffn_bo': _L1_ffn_in['bo'], 'L2_xattn_Wq': _L2_xattn_in['Wq'], 'L2_xattn_bq': _L2_xattn_in['bq'], 'L2_xattn_Wk': _L2_xattn_in['Wk'], 'L2_xattn_bk': _L2_xattn_in['bk'], 'L2_xattn_Wv': _L2_xattn_in['Wv'], 'L2_xattn_bv': _L2_xattn_in['bv'], 'L2_xattn_Wo': _L2_xattn_in['Wo'], 'L2_xattn_bo': _L2_xattn_in['bo'], 'L2_ffn_g1': _L2_ffn_in['g1'], 'L2_ffn_Wq': _L2_ffn_in['Wq'], 'L2_ffn_Wdkv': _L2_ffn_in['Wdkv'], 'L2_ffn_Wuk': _L2_ffn_in['Wuk'], 'L2_ffn_Wuv': _L2_ffn_in['Wuv'], 'L2_ffn_Wo': _L2_ffn_in['Wo'], 'L2_ffn_g2': _L2_ffn_in['g2'], 'L2_ffn_gate_w': _L2_ffn_in['gate_w'], 'L2_ffn_w1': _L2_ffn_in['w1'], 'L2_ffn_w2': _L2_ffn_in['w2'], 'L3_xattn_w_q': _L3_xattn_in['w_q'], 'L3_xattn_b_q': _L3_xattn_in['b_q'], 'L3_xattn_w_k': _L3_xattn_in['w_k'], 'L3_xattn_b_k': _L3_xattn_in['b_k'], 'L3_xattn_w_v': _L3_xattn_in['w_v'], 'L3_xattn_b_v': _L3_xattn_in['b_v'], 'L3_xattn_w_o': _L3_xattn_in['w_o'], 'L3_xattn_b_o': _L3_xattn_in['b_o'], 'L3_ffn_Wp1': _L3_ffn_in['Wp1'], 'L3_ffn_bp1': _L3_ffn_in['bp1'], 'L3_ffn_Wp2': _L3_ffn_in['Wp2'], 'L3_ffn_bp2': _L3_ffn_in['bp2'], 'L3_ffn_W1': _L3_ffn_in['W1'], 'L3_ffn_b1': _L3_ffn_in['b1'], 'L3_ffn_W2': _L3_ffn_in['W2'], 'L3_ffn_b2': _L3_ffn_in['b2'], 'L3_ffn_Wo': _L3_ffn_in['Wo'], 'L3_ffn_bo': _L3_ffn_in['bo']}

def reference(x, ctx_1024, mask_BxSxS2_bk0, mask_Bx1x1xS2_bf1, g_xattn, g_ffn, L0_xattn_Wq, L0_xattn_bq, L0_xattn_Wk, L0_xattn_bk, L0_xattn_Wv, L0_xattn_bv, L0_xattn_Wo, L0_xattn_bo, L0_ffn_router_w, L0_ffn_router_b, L0_ffn_expert_w, L0_ffn_expert_b, L1_xattn_Wq, L1_xattn_Wk, L1_xattn_Wv, L1_xattn_gq, L1_xattn_bq, L1_xattn_gk, L1_xattn_bk, L1_xattn_gv, L1_xattn_bv, L1_ffn_gate_w, L1_ffn_wg, L1_ffn_bg, L1_ffn_wi, L1_ffn_bi, L1_ffn_wo, L1_ffn_bo, L2_xattn_Wq, L2_xattn_bq, L2_xattn_Wk, L2_xattn_bk, L2_xattn_Wv, L2_xattn_bv, L2_xattn_Wo, L2_xattn_bo, L2_ffn_g1, L2_ffn_Wq, L2_ffn_Wdkv, L2_ffn_Wuk, L2_ffn_Wuv, L2_ffn_Wo, L2_ffn_g2, L2_ffn_gate_w, L2_ffn_w1, L2_ffn_w2, L3_xattn_w_q, L3_xattn_b_q, L3_xattn_w_k, L3_xattn_b_k, L3_xattn_w_v, L3_xattn_b_v, L3_xattn_w_o, L3_xattn_b_o, L3_ffn_Wp1, L3_ffn_bp1, L3_ffn_Wp2, L3_ffn_bp2, L3_ffn_W1, L3_ffn_b1, L3_ffn_W2, L3_ffn_b2, L3_ffn_Wo, L3_ffn_bo):
    import jax
    import jax.numpy as jnp

    def _L0_xattn_ref(q, k, v, Wq, bq, Wk, bk, Wv, bv, Wo, bo):
        import jax, jax.numpy as jnp
        import numpy as np
        HIDDEN = 128
        HEADS = 16
        HEAD_DIM = HIDDEN // HEADS

        def _split_heads(x):
            b, n, _ = x.shape
            return x.reshape(b, n, HEADS, HEAD_DIM).transpose(0, 2, 1, 3)
        Q = _split_heads(q @ Wq.T + bq)
        K = _split_heads(k @ Wk.T + bk)
        V = _split_heads(v @ Wv.T + bv)
        scale = 1.0 / jnp.sqrt(jnp.asarray(HEAD_DIM, Q.dtype))
        scores = jnp.einsum('bhnd,bhmd->bhnm', Q, K) * scale
        attn = jax.nn.softmax(scores, axis=-1)
        out = jnp.einsum('bhnm,bhmd->bhnd', attn, V)
        b, h, n, d = out.shape
        out = out.transpose(0, 2, 1, 3).reshape(b, n, h * d)
        return out @ Wo.T + bo

    def _L0_ffn_ref(x, router_w, router_b, expert_w, expert_b):
        import jax, jax.numpy as jnp
        import numpy as np
        B, S, H, E = (4, 256, 128, 8)
        b, s, h = x.shape
        xt = x.reshape(b * s, h)
        logits = xt @ router_w + router_b
        probs = jax.nn.softmax(logits, axis=-1)
        gate = jnp.max(probs, axis=-1)
        idx = jnp.argmax(probs, axis=-1)
        out_all = jnp.einsum('th,ehd->ted', xt, expert_w) + expert_b[None, :, :]
        e_out = jnp.take_along_axis(out_all, idx[:, None, None], axis=1)[:, 0, :]
        y = gate[:, None] * e_out
        return y.reshape(b, s, h)

    def _L1_xattn_ref(query_antecedent, key_antecedent, value_antecedent, mask, Wq, Wk, Wv, gq, bq, gk, bk, gv, bv):
        import jax, jax.numpy as jnp
        import numpy as np
        EPS = 1e-05
        NEG_BIAS = -1000000000.0
        N_HEADS = 16

        def layer_norm(x, gamma, beta):
            mu = jnp.mean(x, axis=-1, keepdims=True)
            var = jnp.mean(jnp.square(x - mu), axis=-1, keepdims=True)
            return (x - mu) * jax.lax.rsqrt(var + EPS) * gamma + beta

        def split_heads(x, n_heads):
            b, s, d = x.shape
            return x.reshape(b, s, n_heads, d // n_heads).transpose(0, 2, 1, 3)
        q = layer_norm(query_antecedent @ Wq, gq, bq)
        k = layer_norm(key_antecedent @ Wk, gk, bk)
        v = layer_norm(value_antecedent @ Wv, gv, bv)
        qh, kh, vh = (split_heads(t, N_HEADS) for t in (q, k, v))
        dk = qh.shape[-1]
        sim = jnp.einsum('bhqd,bhkd->bhqk', qh / jnp.sqrt(jnp.float32(dk)), kh)
        bias = NEG_BIAS * (~mask).astype(sim.dtype)[:, None]
        masked = sim + bias
        weights = jax.nn.softmax(masked, axis=-1)
        outh = jnp.einsum('bhqk,bhkd->bhqd', weights, vh)
        B, H, S, dh = outh.shape
        out = outh.transpose(0, 2, 1, 3).reshape(B, S, H * dh)
        return out

    def _L1_ffn_ref(x, gate_w, wg, bg, wi, bi, wo, bo):
        import jax, jax.numpy as jnp
        import numpy as np
        DIM = 128
        NUM_EXPERTS = 8
        HID = 4 * DIM
        B, T, C = x.shape
        E = gate_w.shape[0]
        xt = x.reshape(B * T, C)
        logits = xt @ gate_w.T
        vals, idxs = jax.lax.top_k(logits, 2)
        probs = jax.nn.softmax(vals, axis=1)
        out = jnp.zeros_like(xt)
        for e in range(E):
            w = jnp.sum(jnp.where(idxs == e, probs, 0.0), axis=1)
            h = jax.nn.silu(xt @ wg[e].T + bg[e]) * (xt @ wi[e].T + bi[e])
            y = h @ wo[e].T + bo[e]
            out = out + w[:, None] * y
        return out.reshape(B, T, C)

    def _L2_xattn_ref(queries, keys, values, Wq, bq, Wk, bk, Wv, bv, Wo, bo):
        import jax, jax.numpy as jnp
        import numpy as np
        B, L, D_MODEL, H, DK, DV = (4, 256, 128, 16, 64, 64)
        b, l, _ = queries.shape
        s = keys.shape[1]
        q = (queries @ Wq + bq).reshape(b, l, H, DK)
        k = (keys @ Wk + bk).reshape(b, s, H, DK)
        v = (values @ Wv + bv).reshape(b, s, H, DV)
        scale = 1.0 / np.sqrt(DK)
        scores = jnp.einsum('blhe,bshe->bhls', q, k)
        causal = jnp.triu(jnp.ones((l, s), bool), k=1)
        scores = jnp.where(causal[None, None], -jnp.inf, scores)
        A = jax.nn.softmax(scale * scores, axis=-1)
        out = jnp.einsum('bhls,bshd->blhd', A, v).reshape(b, l, H * DV)
        return out @ Wo + bo

    def _L2_ffn_ref(x, g1, Wq, Wdkv, Wuk, Wuv, Wo, g2, gate_w, w1, w2):
        import jax, jax.numpy as jnp
        import numpy as np
        EMB = 128
        HEADS = 16
        SEQ = 256
        LATENT = 64
        N_EXP = 8
        TOP_K = 2
        EXP_DIM = 256
        BATCH = 2
        EPS = 1e-06

        def _rmsnorm(x, g):
            return x * jax.lax.rsqrt(jnp.mean(x * x, axis=-1, keepdims=True) + EPS) * g

        def _mla(h, Wq, Wdkv, Wuk, Wuv, Wo):
            B, S, D = h.shape
            hd = D // HEADS
            q = (h @ Wq).reshape(B, S, HEADS, hd)
            c = h @ Wdkv
            k = (c @ Wuk).reshape(B, S, HEADS, hd)
            v = (c @ Wuv).reshape(B, S, HEADS, hd)
            scores = jnp.einsum('bqhd,bkhd->bhqk', q, k) / jnp.sqrt(jnp.asarray(hd, h.dtype))
            causal = jnp.tril(jnp.ones((S, S), bool))
            scores = jnp.where(causal, scores, jnp.asarray(-1000000000.0, h.dtype))
            a = jax.nn.softmax(scores, axis=-1)
            out = jnp.einsum('bhqk,bkhd->bqhd', a, v).reshape(B, S, D)
            return out @ Wo

        def _moe(h, gate_w, w1, w2):
            B, S, D = h.shape
            t = h.reshape(B * S, D)
            logits = t @ gate_w
            top_v, top_i = jax.lax.top_k(logits, TOP_K)
            gates = jax.nn.softmax(top_v, axis=-1)
            T = t.shape[0]
            combine = jnp.zeros((T, N_EXP), t.dtype).at[jnp.arange(T)[:, None], top_i].add(gates)
            hid = jax.nn.silu(jnp.einsum('td,edh->teh', t, w1))
            ye = jnp.einsum('teh,ehd->ted', hid, w2)
            out = jnp.einsum('te,ted->td', combine, ye)
            return out.reshape(B, S, D)
        x = x + _mla(_rmsnorm(x, g1), Wq, Wdkv, Wuk, Wuv, Wo)
        x = x + _moe(_rmsnorm(x, g2), gate_w, w1, w2)
        return x

    def _L3_xattn_ref(q, k, v, mask, w_q, b_q, w_k, b_k, w_v, b_v, w_o, b_o):
        import math
        import jax, jax.numpy as jnp
        import numpy as np
        D_MODEL = 128
        N_HEADS = 16
        D_K = D_MODEL // N_HEADS

        def _rope(x):
            s, d = (x.shape[2], x.shape[3])
            pos = jnp.arange(s, dtype=x.dtype)[:, None]
            inv = 10000.0 ** (jnp.arange(0, d, 2, dtype=x.dtype) / d)
            theta = pos / inv
            sin = jnp.repeat(jnp.sin(theta), 2, axis=-1)
            cos = jnp.repeat(jnp.cos(theta), 2, axis=-1)
            rot = jnp.stack([-x[..., 1::2], x[..., 0::2]], axis=-1).reshape(x.shape)
            return x * cos + rot * sin
        b = q.shape[0]
        h, dk = (N_HEADS, D_K)
        qh = (q @ w_q + b_q).reshape(b, -1, h, dk).transpose(0, 2, 1, 3)
        kh = (k @ w_k + b_k).reshape(b, -1, h, dk).transpose(0, 2, 1, 3)
        vh = (v @ w_v + b_v).reshape(b, -1, h, dk).transpose(0, 2, 1, 3)
        qh = _rope(qh)
        kh = _rope(kh)
        scores = jnp.einsum('bhqd,bhkd->bhqk', qh, kh) / math.sqrt(dk)
        scores = jnp.where(mask, scores, jnp.finfo(scores.dtype).min)
        attn = jax.nn.softmax(scores, axis=-1)
        out = jnp.einsum('bhqk,bhkd->bhqd', attn, vh)
        out = out.transpose(0, 2, 1, 3).reshape(b, -1, h * dk)
        return out @ w_o + b_o

    def _L3_ffn_ref(hidden_states, Wp1, bp1, Wp2, bp2, W1, b1, W2, b2, Wo, bo):
        import jax, jax.numpy as jnp
        import numpy as np
        B, S, H = (8, 512, 128)
        NAV = 128
        E = 8
        F = 2 * H
        last = hidden_states[:, -1, :]
        logits = jax.nn.gelu(last @ Wp1 + bp1, approximate=False) @ Wp2 + bp2
        action_probs = jax.nn.softmax(logits, axis=-1)
        sel = jnp.argmax(action_probs, axis=-1)
        w1 = W1[sel]
        w2 = W2[sel]
        h = jax.nn.gelu(jnp.einsum('bsh,bhf->bsf', hidden_states, w1) + b1[sel][:, None, :], approximate=False)
        reasoned = jnp.einsum('bsf,bfh->bsh', h, w2) + b2[sel][:, None, :]
        out = reasoned @ Wo + bo
        return hidden_states + 0.3 * out
    x = x + jnp.tanh(g_xattn[0]) * _L0_xattn_ref(_layernorm(x, axis=-1), ctx_1024, ctx_1024, L0_xattn_Wq, L0_xattn_bq, L0_xattn_Wk, L0_xattn_bk, L0_xattn_Wv, L0_xattn_bv, L0_xattn_Wo, L0_xattn_bo)
    x = x + jnp.tanh(g_ffn[0]) * _L0_ffn_ref(_layernorm(x, axis=-1), L0_ffn_router_w, L0_ffn_router_b, L0_ffn_expert_w, L0_ffn_expert_b)
    x = x + jnp.tanh(g_xattn[1]) * _L1_xattn_ref(_layernorm(x, axis=-1), ctx_1024, ctx_1024, mask_BxSxS2_bk0, L1_xattn_Wq, L1_xattn_Wk, L1_xattn_Wv, L1_xattn_gq, L1_xattn_bq, L1_xattn_gk, L1_xattn_bk, L1_xattn_gv, L1_xattn_bv)
    x = x + jnp.tanh(g_ffn[1]) * _L1_ffn_ref(_layernorm(x, axis=-1), L1_ffn_gate_w, L1_ffn_wg, L1_ffn_bg, L1_ffn_wi, L1_ffn_bi, L1_ffn_wo, L1_ffn_bo)
    x = x + jnp.tanh(g_xattn[2]) * _L2_xattn_ref(_layernorm(x, axis=-1), ctx_1024, ctx_1024, L2_xattn_Wq, L2_xattn_bq, L2_xattn_Wk, L2_xattn_bk, L2_xattn_Wv, L2_xattn_bv, L2_xattn_Wo, L2_xattn_bo)
    x = x + jnp.tanh(g_ffn[2]) * _L2_ffn_ref(_layernorm(x, axis=-1), L2_ffn_g1, L2_ffn_Wq, L2_ffn_Wdkv, L2_ffn_Wuk, L2_ffn_Wuv, L2_ffn_Wo, L2_ffn_g2, L2_ffn_gate_w, L2_ffn_w1, L2_ffn_w2)
    x = x + jnp.tanh(g_xattn[3]) * _L3_xattn_ref(_layernorm(x, axis=-1), ctx_1024, ctx_1024, mask_Bx1x1xS2_bf1, L3_xattn_w_q, L3_xattn_b_q, L3_xattn_w_k, L3_xattn_b_k, L3_xattn_w_v, L3_xattn_b_v, L3_xattn_w_o, L3_xattn_b_o)
    x = x + jnp.tanh(g_ffn[3]) * _L3_ffn_ref(_layernorm(x, axis=-1), L3_ffn_Wp1, L3_ffn_bp1, L3_ffn_Wp2, L3_ffn_bp2, L3_ffn_W1, L3_ffn_b1, L3_ffn_W2, L3_ffn_b2, L3_ffn_Wo, L3_ffn_bo)
    return x

_drawn_inputs = setup_inputs


def setup_inputs(seed=0):
    import zlib

    import numpy as np

    out = dict(_drawn_inputs(seed))
    spreads = {'L0_xattn_bq': (0.0, 0.317),
     'L0_xattn_bk': (0.0, 2.0),
     'L0_xattn_bv': (0.0, 0.1),
     'L0_xattn_bo': (0.0, 0.1),
     'L0_ffn_router_b': (0.0, 0.1),
     'L0_ffn_expert_b': (0.0, 0.469),
     'L1_xattn_gq': (1.0, 0.55),
     'L1_xattn_bq': (0.0, 0.521),
     'L1_xattn_gk': (1.0, 0.569),
     'L1_xattn_bk': (0.0, 2.0),
     'L1_xattn_gv': (1.0, 0.2),
     'L1_xattn_bv': (0.0, 0.1),
     'L2_xattn_bq': (0.0, 0.403),
     'L2_xattn_bk': (0.0, 2.0),
     'L2_xattn_bv': (0.0, 0.1),
     'L2_xattn_bo': (0.0, 0.306),
     'L2_ffn_g1': (1.0, 0.6),
     'L2_ffn_g2': (1.0, 0.6),
     'L3_xattn_b_q': (0.0, 2.0),
     'L3_xattn_b_k': (0.0, 2.0),
     'L3_xattn_b_v': (0.0, 0.304),
     'L3_xattn_b_o': (0.0, 0.8),
     'L3_ffn_bp1': (0.0, 0.296),
     'L3_ffn_bp2': (0.0, 0.305),
     'L3_ffn_b1': (0.0, 2.0),
     'L3_ffn_b2': (0.0, 2.0),
     'L3_ffn_bo': (0.0, 2.0)}
    factors = {'g_ffn': 24.112,
     'L1_ffn_gate_w': 7.612,
     'L1_ffn_wg': 8.0,
     'L1_ffn_bg': 8.0,
     'L1_ffn_wi': 8.0,
     'L1_ffn_bi': 8.0,
     'L1_ffn_wo': 8.0,
     'L1_ffn_bo': 7.671,
     'L2_ffn_Wq': 8.0,
     'L2_ffn_Wdkv': 8.0,
     'L2_ffn_Wuk': 8.0,
     'L2_ffn_Wuv': 8.0,
     'L2_ffn_Wo': 8.0,
     'L2_ffn_gate_w': 3.934,
     'L2_ffn_w1': 3.169,
     'L2_ffn_w2': 3.127,
     'L3_ffn_W1': 2.697}
    for name, (base, spread) in spreads.items():
        noise = np.random.default_rng([zlib.crc32(name.encode()), seed]).standard_normal(out[name].shape)
        drawn = base * np.exp(spread * noise) if base else spread * noise
        out[name] = jnp.asarray(drawn.astype(out[name].dtype))
    for name, factor in factors.items():
        out[name] = (out[name] * factor).astype(out[name].dtype)
    return out
```

```python
import numpy as np
import concourse.bass as bass
from concourse import mybir
from contextlib import ExitStack

F32 = mybir.dt.float32
BF16 = mybir.dt.bfloat16
U8 = mybir.dt.uint8
ALU = mybir.AluOpType
ACT = mybir.ActivationFunctionType
AX = mybir.AxisListType

B, S, D = 4, 512, 128
KEYS = 77
H, HD = 16, 8
HD2 = 64
P = 128
TB = S // P
NT = B * TB
HK = H * KEYS
CK = B * KEYS
NC = -(-HK // P)
LAST = HK - (NC - 1) * P
E = 8
HID1 = 512
HID2 = 256
J1, J2 = HID1 // P, HID2 // P
LAT = 64
VE = HD + 1
BANK = 512
NEG = -3.0e38
SEL = HID2 + J2 + J2 * D + 1
TOP1, TOP2, TOP2N = 8, 19, 18
LN_EPS, RMS_EPS = 1e-5, 1e-6

X0, F0, X1, F1, X2, MLA, MOE, X3, F3 = range(9)
KV1 = 2
ROUNDS = {X0: 1, F0: 1, X1: 2, F1: 1, X2: 1, MLA: 2, MOE: 1, X3: 1, F3: 1}
TURNED = {X0: 1, F0: 1, X1: 2, F1: 1, X2: 1, MLA: 1, MOE: 1, X3: 1, F3: 1}


def before(table, s, kv):
    return sum(B * table[i] for i in range(s)) + (kv if s > X1 else 0)


ROUND0 = {s: before(ROUNDS, s, KV1) + (KV1 if s == X1 else 0) for s in range(9)}
TURN0 = {s: before(TURNED, s, KV1) + (KV1 if s == X1 else 0) for s in range(9)}
X_NEW = {X0: NT, F0: B + NT, X1: NT, F1: B + NT * E, X2: NT, MLA: B, MOE: NT * E, X3: B + NT, F3: B}
XNEW0 = {s: 2 + sum(X_NEW[i] for i in range(s)) for s in range(10)}
LAYER = {X0: 0, X1: 1, X2: 2, X3: 3}
KV_PS0 = {X0: 0, X1: 2, X2: 3, X3: 3 + H}
KV_SB0 = {X0: 0, X2: 2, X3: 2 + H}
FOLD = {X0: 0, X1: 1, X3: 2}
UNIT0 = {F1: 0, MOE: B * E * J1}
BLOCKS = [(i, j) for i in range(TB) for j in range(i + 1)]


class Tile:

    def __init__(self, g, u, k):
        self.k = k
        self.n = k if g is None else g * u + k
        self.group = k // TB if g is None else (g + k // TB if u == TB else None)

    def slot(self, m):
        return self.k % m


def skewed_loop(eng, steps, total, unroll):
    deep = max(lag for _, lag in steps)
    turns = (total - deep) // unroll
    t = 0
    while t < total + deep:
        if t == deep and turns > 1:
            with eng.Fori(0, turns) as g:
                for i in range(unroll):
                    for f, lag in steps:
                        f(Tile(g, unroll, t + i - lag))
            t += turns * unroll
        else:
            for f, lag in steps:
                if 0 <= t - lag < total:
                    f(Tile(None, unroll, t - lag))
            t += 1


class Chain:

    def __init__(self, eng, sem, base=0):
        self.eng, self.sem, self.base, self.k = eng, sem, base, 0

    def link(self, ins):
        self.k += 1
        ins.then_inc(self.sem, 1)
        self.eng.wait_ge(self.sem, self.base + self.k)


GROUPS = {
    "a": [("ident", P), ("hm", H), ("desc", E), ("gates", 8), ("ctxT", CK),
          ("0wq", D), ("0wk", D), ("0wv", D), ("0wo", D), ("0b", 3), ("0bo", D)],
    "b": [("0we", E * D), ("0eb", D), ("0rw", E), ("0rb", E),
          ("1wq", D), ("1wkv", 2 * D), ("1gb", 6), ("1gw", E), ("1bo", D)],
    "c": [("2wqT", 8 * D), ("2wk", 8 * D), ("2wv", 8 * D), ("2wo", 8 * D), ("2b", 24), ("2bo", D), ("2cm", KEYS)],
    "d": [("mwq", D), ("mwd", LAT), ("mwuk", D), ("mwuv", D), ("mwo", D), ("mg", 2), ("mgw", E), ("mcm", P)],
    "e": [("3wq", D), ("3wk", D), ("3wv", D), ("3wo", D), ("3b", 3), ("3bo", D), ("rot", P),
          ("wp1", D), ("bp1", 1), ("wp2", E), ("bp2", E), ("3fwo", D), ("3fbo", D)],
}
PLACE = {}
WIDTH = {}
_at = 0
for _g, _items in GROUPS.items():
    _start = _at
    for _n, _w in _items:
        PLACE[_n] = (_at, _w)
        _at += _w
    WIDTH[_g] = (_start, _at)
PACKED = _at


def build(nc, x_in, packed, w_ffn1, w_moe, w_ffn3, rope, mask1, mask3, out):
    ctx = ExitStack()
    with ctx:
        def sb(name, shape, dt=F32):
            return ctx.enter_context(nc.sbuf_tensor(name, shape, dt))

        def sem(name):
            return ctx.enter_context(nc.semaphore(name))

        W = sb("W", [P, PACKED])

        def w(name, rows=P):
            a, n = PLACE[name]
            return W[0:rows, a:a + n]

        x = sb("x", [P, NT, D])
        FT = sb("FT", [P, B * S])
        xn_s = sb("xn_s", [P, TB, D])
        xnT_s = sb("xnT_s", [P, S])
        q1_s = sb("q1_s", [P, S])
        oT_s = q1_s
        qs = sb("qs", [P, 2, P])
        KBD = sb("KBD", [P, B, HK])
        VW = sb("VW", [P, B, NC, D])
        VBD = sb("VBD", [P, HK])
        att = sb("att", [P, 4, HK])
        PT = sb("PT", [P, 2, NC, P])
        C = sb("C", [P, B * HK])
        U = sb("U", [P, 3 * E * HID1])
        mask_u8 = sb("mask_u8", [P, NT * KEYS], U8)
        mask3_u8 = sb("mask3_u8", [P, CK], U8)
        bo3 = sb("bo3", [P, D])
        identb = sb("identb", [P, P], BF16)
        cmaskb = sb("cmaskb", [P, HK], BF16)
        diagb = sb("diagb", [P, P], BF16)
        tg = sb("tg", [P, 8])
        stats = sb("stats", [P, TB, 6])
        pad = sb("pad", [P, 1])
        mv = sb("mv", [P, TB, 2])
        ve = sb("ve", [P, TB])
        msq = sb("msq", [P, TB])
        rstd = sb("rstd", [P, TB])
        minus_half = sb("minus_half", [P, TB])
        mx = sb("mx", [P, 2, H])
        rs = sb("rs", [P, 2, H])
        ri = sb("ri", [P, 2, H])
        negm = sb("negm", [P, 2, TB])
        rec = sb("rec", [P, TB])
        w_all = sb("w_all", [P, NT, E])
        w_c = sb("w_c", [P, TB, E])
        G = sb("G", [P, 12, TB, E])
        hp_s = sb("hp_s", [P, B])
        m4 = sb("m4", [P, B, E])

        o_s = att[:, :, :].rearrange("p a n -> p (a n)")[:, 4096:4096 + S].rearrange("p (i d) -> p i d", d=D)
        r_s = o_s
        wT_s = att[0:E, 3, 0:S].rearrange("e (i p) -> e i p", p=P)
        mask3_f = att[:, 1, 0:CK]
        kT_s = att[:, 0, 0:CK]
        vT_s = att[:, 0, CK:2 * CK]
        kA_s = att[:, 0, 2 * CK:3 * CK]
        kB_s = att[:, 0, 3 * CK:4 * CK]
        kT2 = att[:, 0:2, :].rearrange("p a n -> p (a n)").rearrange("p (c n) -> p c n", n=CK)
        vT2 = att[:, 2:4, :].rearrange("p a n -> p (a n)").rearrange("p (c n) -> p c n", n=CK)
        VWT = U[:, 4096:4096 + B * HK].rearrange("p (b n) -> p b n", b=B)
        y = U[:, 9100:9100 + NT * D].rearrange("p (t d) -> p t d", d=D)
        cosT = U[:, 11264:11264 + S]
        sinT = U[:, 11264 + S:11264 + 2 * S]
        WG1 = U[:, 0:E * HID1].rearrange("p (e n) -> p e n", e=E)
        WI1 = U[:, E * HID1:2 * E * HID1].rearrange("p (e n) -> p e n", e=E)
        WO1 = U[:, 2 * E * HID1:3 * E * HID1].rearrange("p (e j d) -> p e j d", e=E, d=D)
        bgi = sb("bgi", [P, 2, E, J1])
        W1M = U[:, 0:E * HID2].rearrange("p (e n) -> p e n", e=E)
        W2M = U[:, E * HID2:2 * E * HID2].rearrange("p (e j d) -> p e j d", e=E, d=D)
        W3F = U[:, 4096:4096 + E * SEL].rearrange("p (e n) -> p e n", e=E)
        mneg = C[:, 0:NT * KEYS].rearrange("p (t k) -> p t k", k=KEYS)
        KT = C[:, 0:B * S]
        Vx = C[:, B * S:B * S + NT * H * VE].rearrange("p (t h d) -> p t h d", h=H, d=VE)
        rope_a, rope_b = PT[:, 0, 0:4, :].rearrange("p c n -> p (c n)"), PT[:, 1, 0:4, :].rearrange("p c n -> p (c n)")
        nb3 = C[:, 0:B * HK // 2].bitcast(BF16).rearrange("p (b n) -> p b n", b=B)
        kh = VBD[:, 0:2 * S].rearrange("p (a n) -> p a n", a=2)
        Pm = att[:, :, :].rearrange("p a n -> p (a n)")[:, 0:2 * TB * S].rearrange("p (a i n) -> p a i n", a=2, i=TB)
        q_s = xnT_s
        c_s = q1_s
        sg = att[:, 0, 0:2 * S].rearrange("p (a n) -> p a n", a=2)
        hh = att[:, 2, 0:2 * S].rearrange("p (a n) -> p a n", a=2)
        sel = att[:, 0:2, 0:SEL]
        wide = PT[:, 0, 0:E, :]
        hsum = PT[:, 1, 0, :]

        ps = ctx.enter_context(nc.psum_tensor("ps", [P, 8, BANK], F32))
        flat = ps[:, :, :].rearrange("p b n -> p (b n)")

        ld = {g: sem(f"loaded_{g}") for g in list(GROUPS) + ["x", "f1", "bgi", "moe", "f3", "rope", "m1", "m3"]}
        consts = sem("consts")
        tanh_done = sem("tanh_done")
        bf_done = sem("bf_done")
        s_stats, s_aggr, s_ve, s_rstd, s_xn = map(sem, ("stats_done", "aggregated", "var_eps", "rstd_done", "normed"))
        turned, turned_sb = sem("turned"), sem("turned_copied")
        x_new = sem("x_new")
        gate_chain, exp_gate = sem("gate_chain"), sem("exp_gate")
        router_ps = sem("router_ps")
        w_ready, wT_ps, wT_sb, wb_ps = sem("w_ready"), sem("wT_ps"), sem("wT_sb"), sem("wb_ps")
        q_ps, q_sb = sem("q_ps"), sem("q_sb")
        rot_ps, rope_chain, roped = sem("rot_ps"), sem("rope_chain"), sem("roped")
        y_set, nb_set, mneg_set, scratch = sem("y_set"), sem("nb_set"), sem("mneg_set"), sem("scratch")
        kv_ps, kv_sb, kv_chain = sem("kv_ps"), sem("kv_sb"), sem("kv_chain")
        kbd, vbd, vw_ps, vw_sb, vw_bo = map(sem, ("kbd_done", "vbd_done", "vw_ps", "vw_sb", "vw_bo"))
        fold_ps, fold_act, fold_dve = sem("fold_ps"), sem("fold_act"), sem("fold_dve")
        staged, scores, scores_read, rowmax, shifted = map(sem, ("q_staged", "scores", "scores_read", "rowmax", "shifted"))
        expd, rowsum, recip, probs, probsT_ps, probsT, attn_out = map(
            sem, ("exp_done", "rowsum", "recip", "probs", "probsT_ps", "probsT", "attn_out"))
        m_scores, m_rowmax, m_expd, m_probsT_ps, m_probsT, m_attn, m_rec, m_normed = map(
            sem, ("m_scores", "m_rowmax", "m_expd", "m_probsT_ps", "m_probsT", "m_attn", "m_rec", "m_normed"))
        m_q, ones_set, ot_ps, ot_sb, yo_ps = map(sem, ("m_q", "ones_set", "ot_ps", "ot_sb", "yo_ps"))
        head_k = sem("head_k")
        mla_ps, mla_sb = sem("mla_ps"), sem("mla_sb")
        e0_ps, e0_read, e0_chain = sem("e0_ps"), sem("e0_read"), sem("e0_chain")
        up_ps, silu, gated, down_ps, w_copied = map(sem, ("up_ps", "silu", "gated", "down_ps", "w_copied"))
        pol, pol_sb, sel_done, sel_chain = sem("pol"), sem("pol_sb"), sem("sel_done"), sem("sel_chain")
        h3_ps, h3_sb, r3_ps, r3_sb, o3_ps, fin = map(sem, ("h3_ps", "h3_sb", "r3_ps", "r3_sb", "o3_ps", "fin"))
        stored, scratch_w = sem("stored"), sem("w_staged")

        CREDITS = [(turned, 1), (turned_sb, 1), (vw_ps, 1), (vw_sb, 1), (e0_read, 2), (gated, 2), (down_ps, 2),
                   (m_expd, 4), (m_probsT, 3), (m_normed, 1), (m_scores, 8), (m_probsT_ps, 6), (m_attn, 2),
                   (x_new, 2), (scores, 2), (scores_read, 1), (shifted, 1), (expd, 2), (probs, 2), (probsT_ps, 6),
                   (probsT, 3), (attn_out, 2)]

        def tiles_before(s):
            return LAYER[s] * NT

        def wait(eng, sm, value):
            if isinstance(value, int) and value <= 0:
                return
            eng.wait_ge(sm, value)

        def tok(b, i, n=1):
            return bass.ds(b * TB + i, n)

        def cols(b, n=S):
            return bass.ds(b * n, n)

        def batch(t, b):
            v = t[:, bass.ds(b, 1)]
            return v.rearrange("p b n -> p (b n)") if len(v.shape) == 3 else v.rearrange("p b c n -> p (b c n)")

        def heads(a):
            return a.rearrange("p (h k) -> p h k", k=KEYS)

        def over_keys(a):
            return a.unsqueeze(2).to_broadcast([P, H, KEYS])

        def folded(u):
            h, k = divmod(u, 3)
            return (KBD[:, :, :], C[:, :].rearrange("p (b n) -> p b n", b=B), VWT)[k][:, :, h * KEYS:(h + 1) * KEYS]

        def values_of(b, j, h):
            return Vx[:, tok(b, j), bass.ds(h, 1), :].rearrange("p t h d -> p (t h d)")

        def token_values(b, i):
            return Vx[:, tok(b, i), :, 0:HD].rearrange("p t h d -> p (t h) d")

        def starts(eng, s):
            if s > X0:
                eng.wait_ge(x_new, XNEW0[s])

        block = ctx.enter_context(nc.Block())

        @block.sync
        def _(sp):
            for sm, n in CREDITS:
                sp.sem_inc(sm, n)

            def load(dst, src, g):
                sp.dma_start(dst, src).then_inc(ld[g], 16)

            a, z = WIDTH["a"]
            load(W[:, a:z], packed[:, a:z], "a")
            load(x[:, :, :], x_in.rearrange("(t p) d -> p t d", p=P), "x")
            for g in "bcde":
                a, z = WIDTH[g]
                load(W[:, a:z], packed[:, a:z], g)
                if g == "b":
                    load(mask_u8[:, :].rearrange("p (t k) -> p t k", k=KEYS),
                         mask1.bitcast(U8).rearrange("(t p k) -> p t k", p=P, k=KEYS), "m1")
                    load(U[:, :], w_ffn1[:, 0:3 * E * HID1], "f1")
                    load(bgi[:, :, :, :].rearrange("p a e j -> p (a e j)"), w_ffn1[:, 3 * E * HID1:], "bgi")
            load(mask3_u8[:, :], mask3, "m3")
            sp.wait_ge(x_new, XNEW0[X2])
            load(U[:, 0:2 * E * HID2], w_moe, "moe")
            load(U[:, 11264:11264 + 2 * S], rope, "rope")
            sp.wait_ge(x_new, XNEW0[MLA])
            load(U[:, 4096:4096 + E * SEL], w_ffn3, "f3")
            for b in range(B):
                sp.wait_ge(x_new, XNEW0[F3] + b + 1)
                sp.dma_start(out[b * S:(b + 1) * S, :].rearrange("(t p) d -> p t d", p=P),
                             x[:, b * TB:(b + 1) * TB, :]).then_inc(stored, 16)
            sp.wait_ge(stored, 16 * B)

        @block.tensor
        def _(pe):
            mm = pe.matmul
            ident = w("ident")
            pe.wait_ge(ld["a"], 16)

            def turn(nth, rounds, rows=P):
                pe.wait_ge(s_xn, TB * rounds)
                pe.wait_ge(turned_sb, nth + 1)
                for i in range(TB):
                    t = pe.transpose(ps[:, 7, i * rows:(i + 1) * rows], xn_s[0:rows, i, :], ident[0:rows, 0:rows])
                t.then_inc(turned, 1)

            def prepare(s, after):
                starts(pe, s)
                with pe.Fori(0, B) as b:
                    first = 1 if s == MLA else 0
                    turn(TURN0[s] + b * TURNED[s], ROUND0[s] + b * ROUNDS[s] + first + 1)
                    if after is not None:
                        after(b)

            def turned_copied(s, b):
                pe.wait_ge(turned_sb, TURN0[s] + b * TURNED[s] + 2)

            def route(s, b, weight):
                turned_copied(s, b)
                for i in range(TB):
                    t = mm(ps[:, 6, i * E:(i + 1) * E], xnT_s[:, i * P:(i + 1) * P], weight, start=True, stop=True)
                t.then_inc(router_ps, 1)

            def weighted_bias(n, rows):
                pe.wait_ge(w_ready, n + 1)
                for i in range(TB):
                    t = pe.transpose(ps[0:E, 5, i * P:(i + 1) * P], w_c[:, i, :], ident)
                t.then_inc(wT_ps, 1)
                pe.wait_ge(wT_sb, n + 1)
                for i in range(TB):
                    t = mm(ps[:, 4, i * D:(i + 1) * D], wT_s[:, i, :], rows, start=True, stop=True)
                t.then_inc(wb_ps, 1)

            def fold_values(s, wo):
                n0 = FOLD[s] * B
                with pe.Fori(0, B) as b:
                    pe.wait_ge(vbd, b + n0 + 1)
                    pe.wait_ge(vw_sb, b + n0 + 1)
                    for c in range(NC):
                        m = P if c < NC - 1 else LAST
                        t = mm(ps[0:m, c // 4, (c % 4) * D:(c % 4 + 1) * D], VBD[:, c * P:c * P + m], wo,
                               start=True, stop=True)
                    t.then_inc(vw_ps, 1)

            def keys_values(s):
                starts(pe, s)
                if s in (X0, X3):
                    l = LAYER[s]
                    pe.wait_ge(ld["a" if s == X0 else "e"], 16)
                    mm(ps[:, 0, 0:CK], w(f"{l}wk"), w("ctxT"), start=True, stop=True).then_inc(kv_ps, 1)
                    mm(ps[:, 1, 0:CK], w(f"{l}wv"), w("ctxT"), start=True, stop=True).then_inc(kv_ps, 1)
                    pe.wait_ge(kv_sb, KV_SB0[s] + 2)
                    if s == X3:
                        mm(ps[:, 2, 0:CK], w("rot"), kT_s, start=True, stop=True).then_inc(kv_ps, 1)
                        pe.wait_ge(kbd, 3)
                    fold_values(s, w(f"{l}wo"))
                elif s == X1:
                    for b in range(B):
                        t = mm(ps[0:KEYS, b // 2, (b % 2) * 2 * D:(b % 2 + 1) * 2 * D],
                               w("ctxT")[:, b * KEYS:(b + 1) * KEYS], w("1wkv"), start=True, stop=True)
                    t.then_inc(kv_ps, 1)
                    for r in range(KV1):
                        turn(TURN0[X1] - KV1 + r, ROUND0[X1] - KV1 + r + 1, rows=KEYS)
                    fold_values(s, ident)
                else:
                    pe.wait_ge(ld["c"], 16)
                    for u in range(H):
                        if u >= 6:
                            pe.wait_ge(kv_sb, KV_SB0[X2] + u - 5)
                        wt = w("2wk") if u % 2 == 0 else w("2wv")
                        c = u // 2
                        mm(ps[:, u % 6, 0:CK], wt[:, c * D:(c + 1) * D], w("ctxT"), start=True, stop=True)\
                            .then_inc(kv_ps, 1)
                    pe.wait_ge(kv_sb, KV_SB0[X2] + H)
                    for u in range(3 * H):
                        if u >= 6:
                            pe.wait_ge(fold_act if u % 2 == 0 else fold_dve, (u - 6) // 2 + 1)
                        h, k = divmod(u, 3)
                        c, r = h // 2, HD2 * (h % 2)
                        rows = slice(r, r + HD2)
                        lhs = (w("2wqT")[rows, c * D:(c + 1) * D],
                               w("2b")[rows, c:c + 1].to_broadcast([HD2, P]),
                               w("2wo")[rows, c * D:(c + 1) * D])[k]
                        rhs = (kT2, kT2, vT2)[k][rows, c, :]
                        mm(ps[:, u % 6, 0:CK], lhs, rhs, start=True, stop=True).then_inc(fold_ps, 1)
                    pe.wait_ge(fold_act, 3 * H // 2)
                    pe.wait_ge(fold_dve, 3 * H // 2)
                    for b in range(B):
                        if b >= 2:
                            pe.wait_ge(fold_act, 3 * H // 2 + b - 1)
                        for c in range(NC):
                            m = P if c < NC - 1 else LAST
                            k = 3 * (b % 2) + c // 4
                            t = pe.transpose(ps[0:m, k, (c % 4) * D:(c % 4 + 1) * D], VWT[:, b, c * P:c * P + m],
                                             ident)
                        t.then_inc(fold_ps, 1)

            def cross(s):
                n0 = tiles_before(s)

                def score(t):
                    pe.wait_ge(staged, t.n + n0 + 1)
                    if s in (X1, X2):
                        pe.wait_ge(scores_read, t.n + (LAYER[s] - 1) * NT + 1)
                    else:
                        pe.wait_ge(shifted, t.n + n0 + 1)
                    causal = s == X2 and t.k % TB == 0
                    for c in range(3):
                        a, z = c * BANK, min((c + 1) * BANK, HK)
                        m = mm(flat[:, a:z], qs[:, t.slot(2), :], batch(KBD, t.group)[:, a:z],
                               start=True, stop=not (causal or s == X3))
                        if causal:
                            m = mm(flat[:, a:z], identb[:, :], cmaskb[:, a:z], start=False, stop=True)
                        if s == X3:
                            m = mm(flat[:, a:z], identb[:, :], batch(nb3, t.group)[:, a:z], start=False, stop=True)
                    m.then_inc(scores, 1)

                def weigh(t):
                    pe.wait_ge(probs, t.n + n0 + 3)
                    for k in range(3):
                        pe.wait_ge(probsT, t.n * 3 + 3 * n0 + k + 1)
                        for c in range(4 * k, min(4 * k + 4, NC)):
                            m = P if c < NC - 1 else LAST
                            q = pe.transpose(ps[0:m, 3 + k, (c % 4) * P:(c % 4 + 1) * P],
                                             att[:, 2 + t.slot(2), c * P:c * P + m], ident)
                        q.then_inc(probsT_ps, 1)
                    pe.wait_ge(x_new, t.n + XNEW0[s] + (B if s == X3 else 0) - 1)
                    for k in range(3):
                        pe.wait_ge(probsT, t.n * 3 + 3 * n0 + k + 4)
                        for c in range(4 * k, min(4 * k + 4, NC)):
                            m = P if c < NC - 1 else LAST
                            q = mm(ps[:, 6 + t.slot(2), 0:D], PT[0:m, t.slot(2), c, :],
                                   batch(VW, t.group)[0:m, c * D:(c + 1) * D], start=(c == 0), stop=(c == NC - 1))
                    q.then_inc(attn_out, 1)

                if s != X2:
                    pe.wait_ge(kbd, FOLD[s] + 1)
                if s == X1:
                    pe.wait_ge(vw_sb, (FOLD[s] + 1) * B + 1)
                else:
                    pe.wait_ge(vw_bo, {X0: 1, X2: 2, X3: 3}[s])
                if s == X2:
                    pe.wait_ge(bf_done, 3)
                if s == X3:
                    pe.wait_ge(nb_set, 1)
                skewed_loop(pe, [(score, 0), (weigh, 2)], NT, TB)

            def experts(s, J, wg, wi, wo):
                units = E * J
                u0 = UNIT0[s]
                x0 = XNEW0[s] + (B if s == F1 else 0)
                pe.wait_ge(x_new, x0)

                def chunk(c):
                    def up(u):
                        e, j = divmod(u, J)
                        if s == F1:
                            pe.wait_ge(gated, c * units + u0 + u + 1)
                        else:
                            pe.wait_ge(silu, c * units + u0 + u - 1)
                        t = mm(ps[:, u % 2, :], wg[:, e, j * P:(j + 1) * P], FT[:, cols(c)], start=True, stop=True)
                        if wi is not None:
                            t = mm(ps[:, 2 + u % 2, :], wi[:, e, j * P:(j + 1) * P], FT[:, cols(c)],
                                   start=True, stop=True)
                        t.then_inc(up_ps, 1)

                    def down(u):
                        e, j = divmod(u, J)
                        if s == F1:
                            pe.wait_ge(gated, c * units + u0 + u + 3)
                        else:
                            pe.wait_ge(silu, c * units + u0 + u + 1)
                        if j == 0:
                            pe.wait_ge(x_new, (c * E + e - 1) * TB + x0)
                        for i in range(TB):
                            t = mm(ps[:, 4 + e % 2, i * D:(i + 1) * D], hh[:, u % 2, i * P:(i + 1) * P], wo[:, e, j, :],
                                   start=(j == 0 and i == 0), stop=(j == J - 1 and i == TB - 1))
                        t.then_inc(down_ps, 1)

                    up(0)
                    for u in range(1, units):
                        up(u)
                        down(u - 1)
                    down(units - 1)
                with pe.Fori(0, B) as c:
                    chunk(c)

            keys_values(X0)

            def q0(b):
                turned_copied(X0, b)
                mm(ps[:, 6, :], w("0wq"), xnT_s[:, :], start=True, stop=True).then_inc(q_ps, 1)
            prepare(X0, q0)
            cross(X0)

            pe.wait_ge(ld["b"], 16)

            def experts0(b):
                route(F0, b, w("0rw"))
                weighted_bias(b, w("0eb", E))
                for i in range(TB):
                    pair = 2 * (i % 2)
                    pe.wait_ge(e0_read, b * TB + i + 1)
                    for c in range(2):
                        t = mm(ps[:, pair + c, :], xnT_s[:, i * P:(i + 1) * P], w("0we")[:, c * BANK:(c + 1) * BANK],
                               start=True, stop=True)
                    t.then_inc(e0_ps, 1)
            prepare(F0, experts0)

            keys_values(X1)

            def q1(b):
                turned_copied(X1, b)
                for i in range(TB):
                    t = mm(ps[:, 6, i * D:(i + 1) * D], xnT_s[:, i * P:(i + 1) * P], w("1wq"), start=True, stop=True)
                t.then_inc(q_ps, 1)
                turn(TURN0[X1] + b * 2 + 1, ROUND0[X1] + b * 2 + 2)
            prepare(X1, q1)
            cross(X1)

            def route1(b):
                route(F1, b, w("1gw"))
                weighted_bias(B + b, w("1bo", E))
            prepare(F1, route1)
            pe.wait_ge(ld["f1"], 16)
            experts(F1, J1, WG1, WI1, WO1)

            keys_values(X2)
            prepare(X2, None)
            cross(X2)

            pe.wait_ge(ld["d"], 16)

            def latents(b):
                turned_copied(MLA, b)
                mm(ps[:, 6, :], w("mwq"), xnT_s[:, :], start=True, stop=True).then_inc(mla_ps, 1)
                mm(ps[0:LAT, 5, :], w("mwd"), xnT_s[:, :], start=True, stop=True).then_inc(mla_ps, 1)
                pe.wait_ge(mla_sb, b * 4 + 2)
                mm(ps[:, 4, :], w("mwuk", LAT), c_s[0:LAT, :], start=True, stop=True).then_inc(mla_ps, 1)
                for i in range(TB):
                    t = mm(ps[:, 3, i * D:(i + 1) * D], c_s[0:LAT, i * P:(i + 1) * P], w("mwuv", LAT),
                           start=True, stop=True)
                t.then_inc(mla_ps, 1)
            prepare(MLA, latents)

            pe.wait_ge(mla_sb, 4 * B)
            pe.wait_ge(ones_set, 1)
            pe.wait_ge(bf_done, 3)

            with pe.Fori(0, B) as b:
                def score(t):
                    n = b * H + t.n
                    pe.wait_ge(head_k, n + 1)
                    for i in range(TB):
                        pe.wait_ge(m_expd, n * 4 + i + 1)
                        z = (i + 1) * P
                        mm(ps[:, i, i * P:z], identb[:, :], diagb[:, :], start=True, stop=False, skip_group_check=True)
                        mm(ps[:, i, 0:z], q_s[:, i * P:(i + 1) * P], kh[:, t.slot(2), 0:z], start=False, stop=True,
                           skip_group_check=True).then_inc(m_scores, 1)

                def weigh(t):
                    n = b * H + t.n
                    for k in range(3):
                        pe.wait_ge(m_probsT, n * 3 + k + 1)
                        for c in range(4 * k, min(4 * k + 4, len(BLOCKS))):
                            i, j = BLOCKS[c]
                            if j == 0:
                                pe.wait_ge(m_expd, n * 4 + i + 5)
                            q = pe.transpose(ps[:, 4 + k, (c % 4) * P:(c % 4 + 1) * P],
                                             Pm[:, t.slot(2), i, j * P:(j + 1) * P], ident)
                        q.then_inc(m_probsT_ps, 1)
                    pe.wait_ge(m_normed, n + 1)
                    for c, (i, j) in enumerate(BLOCKS):
                        if c % 4 == 0:
                            pe.wait_ge(m_probsT, n * 3 + c // 4 + 4)
                        q = mm(ps[:, 7, i * VE:(i + 1) * VE], PT[:, t.slot(2), c, :],
                               values_of(b, j, t.n), start=(j == 0), stop=(j == i))
                    q.then_inc(m_attn, 1)

                pe.wait_ge(m_q, b + 1)
                skewed_loop(pe, [(score, 0), (weigh, 1)], H, 2)
                pe.wait_ge(m_normed, b * H + H + 1)
                for i in range(TB):
                    t = pe.transpose(ps[:, 4, i * P:(i + 1) * P], o_s[:, i, :], ident)
                t.then_inc(ot_ps, 1)
                pe.wait_ge(ot_sb, b + 1)
                for i in range(TB):
                    t = mm(ps[:, 5, i * D:(i + 1) * D], oT_s[:, i * P:(i + 1) * P], w("mwo"), start=True, stop=True)
                t.then_inc(yo_ps, 1)
                pe.wait_ge(x_new, b + XNEW0[MLA] + 1)

            prepare(MOE, lambda b: route(MOE, b, w("mgw")))
            pe.wait_ge(ld["moe"], 16)
            experts(MOE, J2, W1M, None, W2M)

            keys_values(X3)

            def q3(b):
                turned_copied(X3, b)
                mm(ps[:, 6, :], w("3wq"), xnT_s[:, :], start=True, stop=True).then_inc(q_ps, 1)
                pe.wait_ge(q_sb, b + B + 1)
                mm(ps[:, 5, :], w("rot"), q1_s[:, :], start=True, stop=True).then_inc(rot_ps, 1)
            prepare(X3, q3)
            cross(X3)

            prepare(F3, None)
            pe.wait_ge(turned_sb, TURN0[F3] + B + 1)
            mm(ps[:, 6, 0:B], w("wp1"), FT[:, S - 1:B * S:S], start=True, stop=True).then_inc(pol, 1)
            pe.wait_ge(pol_sb, 1)
            for b in range(B):
                t = mm(ps[:, 7, b * E:(b + 1) * E], hp_s[:, b:b + 1].to_broadcast([P, P]), w("wp2"),
                       start=True, stop=True)
            t.then_inc(pol, 1)

            def ffn3(t):
                sl = t.slot(2)
                pe.wait_ge(sel_done, t.n + 1)
                for f in range(J2):
                    mm(ps[:, f, :], sel[:, sl, f * P:(f + 1) * P], FT[:, cols(t.n)], start=True, stop=True)\
                        .then_inc(h3_ps, 1)
                for f in range(J2):
                    pe.wait_ge(h3_sb, t.n * J2 + f + 1)
                    a = HID2 + J2 + f * D
                    m = mm(ps[:, 2, :], sel[:, sl, a:a + D], hh[:, f, :], start=(f == 0), stop=(f == J2 - 1))
                m.then_inc(r3_ps, 1)
                pe.wait_ge(r3_sb, t.n + 1)
                pe.wait_ge(x_new, t.n + XNEW0[F3])
                for i in range(TB):
                    m = mm(ps[:, 3, i * D:(i + 1) * D], r_s[:, i, :], w("3fwo"), start=True, stop=True)
                m.then_inc(o3_ps, 1)
            skewed_loop(pe, [(ffn3, 0)], B, 2)

        @block.scalar
        def _(act):
            go = act.activation
            act.wait_ge(ld["a"], 16)
            go(tg[:, :], w("gates"), ACT.Tanh).then_inc(tanh_done, 1)

            def turned_copy(s, b, k, copies):
                act.wait_ge(turned, TURN0[s] + b * TURNED[s] + k + 2)
                for dst, scale, bias in copies:
                    if bias is not None:
                        t = go(dst, ps[:, 7, :], ACT.Identity, scale=scale, bias=bias)
                    elif scale is not None:
                        t = go(dst, ps[:, 7, :], ACT.Copy, scale=scale)
                    else:
                        t = go(dst, ps[:, 7, :], ACT.Copy)
                t.then_inc(turned_sb, 1)

            def copy_vw(b, k0):
                vw = batch(VW, b)
                go(vw[:, 0:4 * D], ps[:, k0, :], ACT.Copy)
                go(vw[:, 4 * D:8 * D], ps[:, k0 + 1, :], ACT.Copy)
                go(vw[:, 8 * D:9 * D], ps[:, k0 + 2, 0:D], ACT.Copy)
                return go(vw[0:LAST, 9 * D:10 * D], ps[0:LAST, k0 + 2, D:2 * D], ACT.Copy)

            def fold_values(s):
                with act.Fori(0, B) as b:
                    act.wait_ge(vw_ps, b + FOLD[s] * B + 2)
                    copy_vw(b, 0).then_inc(vw_sb, 1)

            def keys_values(s):
                starts(act, s)
                if s in (X0, X3):
                    b_ = w(f"{LAYER[s]}b")
                    act.wait_ge(ld["a" if s == X0 else "e"], 16)
                    act.wait_ge(kv_ps, KV_PS0[s] + 1)
                    go(kT_s, ps[:, 0, 0:CK], ACT.Identity, bias=b_[:, 1:2]).then_inc(kv_sb, 1)
                    act.wait_ge(kv_ps, KV_PS0[s] + 2)
                    go(vT_s, ps[:, 1, 0:CK], ACT.Identity, bias=b_[:, 2:3]).then_inc(kv_sb, 1)
                    fold_values(s)
                elif s == X1:
                    act.wait_ge(ld["b"], 16)
                    gb = w("1gb")
                    for r, dst in enumerate((kT_s, vT_s)):
                        act.wait_ge(turned, TURN0[X1] - KV1 + r + 2)
                        go(dst, ps[:, 7, 0:CK], ACT.Identity, scale=gb[:, 2 + 2 * r:3 + 2 * r],
                           bias=gb[:, 3 + 2 * r:4 + 2 * r]).then_inc(turned_sb, 1)
                    fold_values(s)
                else:
                    act.wait_ge(ld["c"], 16)
                    for u in range(H):
                        c = u // 2
                        act.wait_ge(kv_ps, KV_PS0[X2] + u + 1)
                        k = 8 if u % 2 == 0 else 16
                        go((kT2 if u % 2 == 0 else vT2)[:, c, :], ps[:, u % 6, 0:CK], ACT.Identity,
                           bias=w("2b")[:, k + c:k + c + 1]).then_inc(kv_sb, 1)
                    for u in range(0, 3 * H, 2):
                        act.wait_ge(fold_ps, u + 1)
                        go(folded(u), ps[:, u % 6, 0:CK].rearrange("p (b k) -> p b k", k=KEYS), ACT.Copy)\
                            .then_inc(fold_act, 1)
                    for b in range(B):
                        act.wait_ge(fold_ps, 3 * H + b + 1)
                        copy_vw(b, 3 * (b % 2)).then_inc(fold_act, 1)

            def cross(s, scale):
                n0 = tiles_before(s)

                def stage(t):
                    act.wait_ge(scores, t.n + n0 + 1)
                    go(qs[:, t.slot(2), :], FT[:, bass.ds(t.n * P, P)], ACT.Copy).then_inc(staged, 1)

                def exponent(t):
                    act.wait_ge(shifted, t.n + n0 + 2)
                    act.wait_ge(probsT_ps, t.n * 3 + 3 * n0 + 3)
                    go(att[:, 2 + t.slot(2), :], att[:, t.slot(2), :], ACT.Exp, scale=scale).then_inc(expd, 1)

                def evacuate(t):
                    act.wait_ge(attn_out, t.n + n0 + 1)
                    for k in range(3):
                        act.wait_ge(probsT_ps, t.n * 3 + 3 * n0 + k + 7)
                        if k < 2:
                            go(PT[:, t.slot(2), 4 * k:4 * k + 4, :].rearrange("p c n -> p (c n)"), ps[:, 3 + k, :],
                               ACT.Copy).then_inc(probsT, 1)
                        else:
                            go(PT[:, t.slot(2), 8, :], ps[:, 5, 0:P], ACT.Copy)
                            go(PT[0:LAST, t.slot(2), 9, :], ps[0:LAST, 5, P:2 * P], ACT.Copy).then_inc(probsT, 1)

                skewed_loop(act, [(stage, 0), (evacuate, 3), (exponent, 1)], NT, TB)

            def gate_exp(n, chain, src, dst):
                act.wait_ge(gate_chain, chain)
                go(dst, src, ACT.Exp).then_inc(exp_gate, 1)

            def copy_wT(n):
                act.wait_ge(wT_ps, n + 1)
                go(wT_s[:, :, :].rearrange("e i p -> e (i p)"), ps[0:E, 5, :], ACT.Copy).then_inc(wT_sb, 1)

            def hidden(s, J, dst):
                units = E * J
                u0 = UNIT0[s]
                with act.Fori(0, B) as c:
                    for u in range(units):
                        e, j = divmod(u, J)
                        act.wait_ge(up_ps, c * units + u0 + u + 1)
                        if s == F1:
                            act.wait_ge(gated, c * units + u0 + u + 1)
                            go(dst[:, u % 2, :], ps[:, u % 2, :], ACT.Silu, bias=bgi[:, 0, e, j:j + 1]).then_inc(silu, 1)
                        else:
                            act.wait_ge(down_ps, c * units + u0 + u + 1)
                            go(dst[:, u % 2, :], ps[:, u % 2, :], ACT.Silu).then_inc(silu, 1)

            keys_values(X0)

            with act.Fori(0, B) as b:
                turned_copy(X0, b, 0, [(xnT_s[:, :], None, None)])
                act.wait_ge(q_ps, b + 1)
                go(FT[:, cols(b)], ps[:, 6, :], ACT.Identity, bias=w("0b")[:, 0:1]).then_inc(q_sb, 1)
            act.wait_ge(q_sb, B)
            cross(X0, HD ** -0.5)

            starts(act, F0)
            with act.Fori(0, B) as b:
                turned_copy(F0, b, 0, [(xnT_s[:, :], None, None)])
                gate_exp(b, b * TOP1 + 3, G[:, 1, :, :], G[:, 2, :, :])
                copy_wT(b)

            keys_values(X1)
            with act.Fori(0, B) as b:
                turned_copy(X1, b, 0, [(xnT_s[:, :], None, None)])
                turned_copy(X1, b, 1, [(FT[:, cols(b)], w("1gb")[:, 0:1], w("1gb")[:, 1:2])])
            act.wait_ge(turned_sb, TURN0[X1] + 2 * B + 1)
            cross(X1, 1.0)

            starts(act, F1)
            with act.Fori(0, B) as b:
                turned_copy(F1, b, 0, [(xnT_s[:, :], None, None), (FT[:, cols(b)], None, None)])
                gate_exp(B + b, b * TOP2 + B * TOP1 + 12, G[:, 10, :, 0:1], G[:, 11, :, 0:1])
                copy_wT(B + b)
            act.wait_ge(ld["bgi"], 16)
            hidden(F1, J1, sg)

            keys_values(X2)
            with act.Fori(0, B) as b:
                turned_copy(X2, b, 0, [(FT[:, cols(b)], None, None)])
            act.wait_ge(turned_sb, TURN0[X2] + B + 1)
            cross(X2, HD2 ** -0.5)

            starts(act, MLA)
            act.wait_ge(ld["d"], 16)
            with act.Fori(0, B) as b:
                turned_copy(MLA, b, 0, [(xnT_s[:, :], w("mg")[:, 0:1], None)])
                act.wait_ge(mla_ps, b * 4 + 1)
                go(FT[:, cols(b)], ps[:, 6, :], ACT.Copy, scale=HD ** -0.5).then_inc(mla_sb, 1)
                act.wait_ge(mla_ps, b * 4 + 2)
                go(c_s[0:LAT, :], ps[0:LAT, 5, :], ACT.Copy).then_inc(mla_sb, 1)
                act.wait_ge(mla_ps, b * 4 + 3)
                go(KT[:, cols(b)], ps[:, 4, :], ACT.Copy).then_inc(mla_sb, 1)
                act.wait_ge(mla_ps, b * 4 + 4)
                for i in range(TB):
                    t = go(token_values(b, i), ps[:, 3, i * D:(i + 1) * D].rearrange("p (h d) -> p h d", d=HD), ACT.Copy)
                t.then_inc(mla_sb, 1)
            act.wait_ge(mla_sb, 4 * B)

            with act.Fori(0, B) as b:
                act.wait_ge(m_scores, b * (4 * H) + 8)
                go(q_s[:, :], FT[:, cols(b)], ACT.Copy).then_inc(m_q, 1)

                def exponent(t):
                    n = b * H + t.n
                    act.wait_ge(m_probsT_ps, n * 3 + 3)
                    for i in range(TB):
                        act.wait_ge(m_rowmax, n * 4 + i + 1)
                        z = (i + 1) * P
                        go(Pm[:, t.slot(2), i, 0:z], ps[:, i, 0:z], ACT.Exp, bias=negm[:, t.slot(2), i:i + 1])\
                            .then_inc(m_expd, 1)
                skewed_loop(act, [(exponent, 0)], H, 2)
                act.wait_ge(ot_ps, b + 1)
                go(oT_s[:, :], ps[:, 4, :], ACT.Copy).then_inc(ot_sb, 1)

            starts(act, MOE)
            with act.Fori(0, B) as b:
                turned_copy(MOE, b, 0, [(xnT_s[:, :], w("mg")[:, 1:2], None), (FT[:, cols(b)], w("mg")[:, 1:2], None)])
                gate_exp(2 * B + b, b * TOP2N + B * (TOP1 + TOP2) + 12, G[:, 10, :, 0:1], G[:, 11, :, 0:1])
            hidden(MOE, J2, hh)

            keys_values(X3)
            with act.Fori(0, B) as b:
                turned_copy(X3, b, 0, [(xnT_s[:, :], None, None)])
                act.wait_ge(q_ps, b + 2 * B + 1)
                go(q1_s[:, :], ps[:, 6, :], ACT.Identity, bias=w("3b")[:, 0:1]).then_inc(q_sb, 1)
            act.wait_ge(roped, B)
            cross(X3, HD ** -0.5)

            starts(act, F3)
            with act.Fori(0, B) as b:
                turned_copy(F3, b, 0, [(FT[:, cols(b)], None, None)])
            act.wait_ge(pol, 1)
            go(hp_s[:, :], ps[:, 6, 0:B], ACT.Gelu, bias=w("bp1")).then_inc(pol_sb, 1)

            def gelu3(t):
                sl = t.slot(2)
                wait(act, r3_ps, t.n)
                for f in range(J2):
                    act.wait_ge(h3_ps, t.n * J2 + f + 1)
                    go(hh[:, f, :], ps[:, f, :], ACT.Gelu, bias=sel[:, sl, HID2 + f:HID2 + f + 1]).then_inc(h3_sb, 1)
                act.wait_ge(r3_ps, t.n + 1)
                wait(act, o3_ps, t.n)
                go(r_s[:, :, :].rearrange("p i d -> p (i d)"), ps[:, 2, :], ACT.Identity, bias=sel[:, sl, SEL - 1:SEL])\
                    .then_inc(r3_sb, 1)
            skewed_loop(act, [(gelu3, 0)], B, 2)

        @block.gpsimd
        def _(pool):
            tt = pool.tensor_tensor
            pool.memset(minus_half[:, :], -0.5).then_inc(consts, 1)
            pool.wait_ge(consts, 1)

            def root(n):
                pool.wait_ge(s_ve, n + 1)
                tt(rstd[:, :], ve[:, :], minus_half[:, :], ALU.pow).then_inc(s_rstd, 1)

            def roots(s):
                with pool.Fori(0, B) as b:
                    for k in range(ROUNDS[s]):
                        root(b * ROUNDS[s] + ROUND0[s] + k)

            def block_values(s):
                starts(pool, s)
                if s == X1:
                    pool.wait_ge(turned_sb, TURN0[X1] + 1)
                else:
                    pool.wait_ge(kv_sb, KV_SB0[s] + 2)
                with pool.Fori(0, B) as b:
                    pool.wait_ge(vw_ps, b + FOLD[s] * B + 1)
                    tt(heads(VBD[:, :]), vT_s[:, bass.ds(b * KEYS, KEYS)].unsqueeze(1).to_broadcast([P, H, KEYS]),
                       over_keys(w("hm")), ALU.mult).then_inc(vbd, 1)

            def cross(s):
                n0 = tiles_before(s)

                def normalize(t):
                    pool.wait_ge(recip, t.n + n0 + 1)
                    p = heads(att[:, 2 + t.slot(2), :])
                    tt(p, p, over_keys(ri[:, t.slot(2), :]), ALU.mult).then_inc(probs, 1)
                skewed_loop(pool, [(normalize, 0)], NT, TB)

            pool.wait_ge(ld["a"], 16)
            block_values(X0)
            roots(X0)
            cross(X0)
            pool.wait_ge(ld["m1"], 16)
            pool.tensor_scalar(C[:, 0:NT * KEYS], mask_u8[:, :], 1.0e9, -1.0e9, ALU.mult, ALU.add).then_inc(mneg_set, 1)
            roots(F0)
            for r in range(KV1):
                root(ROUND0[X1] - KV1 + r)
            block_values(X1)
            roots(X1)
            cross(X1)
            roots(F1)
            roots(X2)
            cross(X2)
            starts(pool, MLA)
            pool.memset(Vx[:, :, :, HD:VE], 1.0).then_inc(ones_set, 1)
            roots(MLA)
            pool.wait_ge(mla_sb, 4 * B)
            with pool.Fori(0, B) as b:
                def keys_of_head(t):
                    n = b * H + t.n
                    pool.wait_ge(m_scores, n * 4 + 4)
                    tt(kh[:, t.slot(2), :], KT[:, cols(b)], w("hm")[:, bass.ds(t.n, 1)].to_broadcast([P, S]), ALU.mult)\
                        .then_inc(head_k, 1)
                skewed_loop(pool, [(keys_of_head, 0)], H, 2)
            starts(pool, MOE)
            pool.wait_ge(ld["m3"], 16)
            for b in range(B):
                t = pool.tensor_scalar(heads(nb3[:, b, :]),
                                       mask3_u8[:, b * KEYS:(b + 1) * KEYS].unsqueeze(1).to_broadcast([P, H, KEYS]),
                                       -NEG, NEG, ALU.mult, ALU.add)
            t.then_inc(nb_set, 1)
            roots(MOE)
            block_values(X3)
            roots(X3)
            cross(X3)
            roots(F3)

        @block.vector
        def _(dve):
            v = nc.vector
            tt, ts, stt = v.tensor_tensor, v.tensor_scalar, v.scalar_tensor_tensor

            def norm(n, n_turn, src, dst, rms=None, rows=P):
                v.memset(pad[:, :], 0.0)
                for i in range(TB):
                    v.bn_stats(stats[0:rows, i, :], src(i)).then_inc(s_stats, 1)
                dve.wait_ge(s_stats, TB * (n + 1))
                v.memset(pad[:, :], 0.0)
                for i in range(TB):
                    v.bn_aggr(mv[0:rows, i, :], stats[0:rows, i, :]).then_inc(s_aggr, 1)
                dve.wait_ge(s_aggr, TB * (n + 1))
                mean, var = mv[0:rows, :, 0], mv[0:rows, :, 1]
                if rms is not None:
                    tt(msq[0:rows, :], mean, mean, ALU.mult).then_inc(scratch, 1)
                    dve.wait_ge(scratch, rms)
                    stt(ve[0:rows, :], msq[0:rows, :], RMS_EPS, var, ALU.add, ALU.add).then_inc(s_ve, 1)
                else:
                    ts(ve[0:rows, :], var, LN_EPS, None, ALU.add).then_inc(s_ve, 1)
                dve.wait_ge(s_rstd, n + 1)
                if n_turn is not None:
                    dve.wait_ge(turned, n_turn + 1)
                for i in range(TB):
                    if rms is not None:
                        ts(dst(i), src(i), rstd[0:rows, i:i + 1], None, ALU.mult).then_inc(s_xn, 1)
                    else:
                        ts(dst(i), src(i), mv[0:rows, i, 0:1], rstd[0:rows, i:i + 1], ALU.subtract, ALU.mult)\
                            .then_inc(s_xn, 1)

            def row(t, b, i):
                return t[:, tok(b, i), :].rearrange("p t d -> p (t d)")

            def xn_of(i):
                return xn_s[:, i, :]

            def norm_rms(b, n, n_turn, nth):
                norm(n, n_turn, lambda i: row(y, b, i), xn_of, rms=nth + 1)

            def block_keys(s):
                starts(dve, s)
                dst = KBD[:, :, :].rearrange("p b (h k) -> p b h k", k=KEYS)
                if s == X1:
                    dve.wait_ge(turned_sb, TURN0[X1])
                elif s == X0:
                    dve.wait_ge(kv_sb, 1)
                for b in range(B):
                    t = tt(dst[:, b], kT_s[:, b * KEYS:(b + 1) * KEYS].unsqueeze(1).to_broadcast([P, H, KEYS]),
                           over_keys(w("hm")), ALU.mult)
                t.then_inc(kbd, 1)

            def add_output_bias(s, n):
                if s == X2:
                    dve.wait_ge(fold_act, 3 * H // 2 + B)
                else:
                    dve.wait_ge(vw_sb, (FOLD[s] + 1) * B + 1)
                tt(VW[:, :, 0, :], VW[:, :, 0, :], w(f"{LAYER[s]}bo").unsqueeze(1).to_broadcast([P, B, D]), ALU.add)\
                    .then_inc(vw_bo, 1)

            def cross(s):
                n0 = tiles_before(s)

                def shift(t):
                    a = heads(att[:, t.slot(2), :])
                    dve.wait_ge(scores, t.n + n0 + 3)
                    dve.wait_ge(expd, t.n + n0 + 1)
                    src = heads(flat[:, 0:HK])
                    if s == X1:
                        m = mneg[:, bass.ds(t.n, 1), :].to_broadcast([P, H, KEYS])
                        stt(a, src, HD ** -0.5, m, ALU.mult, ALU.add).then_inc(scores_read, 1)
                    if s == X2:
                        tt(att[:, t.slot(2), :], flat[:, 0:HK], batch(C[:, :].rearrange("p (b n) -> p b n", b=B), t.group), ALU.add)\
                            .then_inc(scores_read, 1)
                    if s in (X1, X2):
                        src = a
                        dve.wait_ge(scores_read, t.n + (LAYER[s] - 1) * NT + 2)
                    v.tensor_reduce(mx[:, t.slot(2), :], src, AX.X, ALU.max).then_inc(rowmax, 1)
                    dve.wait_ge(rowmax, t.n + n0 + 1)
                    tt(a, src, over_keys(mx[:, t.slot(2), :]), ALU.subtract).then_inc(shifted, 1)

                def total(t):
                    dve.wait_ge(expd, t.n + n0 + 3)
                    v.tensor_reduce(rs[:, t.slot(2), :], heads(att[:, 2 + t.slot(2), :]), AX.X, ALU.add)\
                        .then_inc(rowsum, 1)
                    dve.wait_ge(rowsum, t.n + n0 + 1)
                    dve.wait_ge(probs, t.n + n0 + 1)
                    v.reciprocal(ri[:, t.slot(2), :], rs[:, t.slot(2), :]).then_inc(recip, 1)

                def update(t):
                    dve.wait_ge(attn_out, t.n + n0 + 3)
                    xt = x[:, bass.ds(t.n, 1), :].rearrange("p t d -> p (t d)")
                    stt(xt, ps[:, 6 + t.slot(2), 0:D], tg[:, LAYER[s]:LAYER[s] + 1], xt, ALU.mult, ALU.add)\
                        .then_inc(x_new, 1)

                skewed_loop(dve, [(shift, 0), (total, 1), (update, 2)], NT, TB)

            def gate(s, b, n, base, tanh):
                c = Chain(dve, gate_chain, base)
                g = lambda k: G[:, k, :, :]
                one = lambda k: G[:, 3, :, k:k + 1]
                wide_ = lambda a: a.to_broadcast([P, TB, E])
                desc = w("desc").unsqueeze(1).to_broadcast([P, TB, E])
                lg = ps[:, 6, 0:TB * E].rearrange("p (i e) -> p i e", e=E)
                dve.wait_ge(router_ps, n + 1)

                def first_largest(src, k, m, m2):
                    c.link(v.tensor_reduce(one(m), src, AX.X, ALU.max))
                    c.link(tt(g(k), src, wide_(one(m)), ALU.subtract))
                    c.link(stt(g(k + 1), g(k), 0.0, desc, ALU.is_ge, ALU.mult))
                    c.link(v.tensor_reduce(one(m2), g(k + 1), AX.X, ALU.max))
                    c.link(tt(g(k + 1), g(k + 1), wide_(one(m2)), ALU.is_equal))
                    return g(k + 1)

                if s == F0:
                    c.link(tt(g(0), lg, w("0rb").unsqueeze(1).to_broadcast([P, TB, E]), ALU.add))
                    c.link(v.tensor_reduce(one(0), g(0), AX.X, ALU.max))
                    c.link(tt(g(1), g(0), wide_(one(0)), ALU.subtract))
                    c.link(stt(g(5), g(1), 0.0, desc, ALU.is_ge, ALU.mult))
                    c.link(v.tensor_reduce(one(1), g(5), AX.X, ALU.max))
                    c.link(tt(g(5), g(5), wide_(one(1)), ALU.is_equal))
                    dve.wait_ge(exp_gate, n + 1)
                    c.link(v.tensor_reduce(one(2), g(2), AX.X, ALU.add))
                    c.link(v.reciprocal(one(3), one(2)))
                    stt(w_c[:, :, :], g(5), tanh, wide_(one(3)), ALU.mult, ALU.mult).then_inc(w_ready, 1)
                    dve.wait_ge(w_ready, n + 1)
                    assert c.k == TOP1, c.k
                    return
                c.link(v.tensor_copy(g(0), lg))
                oh1 = first_largest(g(0), 4, 0, 1)
                c.link(stt(g(6), oh1, NEG, g(0), ALU.mult, ALU.add))
                c.link(v.tensor_reduce(one(2), g(6), AX.X, ALU.max))
                c.link(tt(g(7), g(6), wide_(one(2)), ALU.subtract))
                c.link(stt(g(8), g(7), 0.0, desc, ALU.is_ge, ALU.mult))
                c.link(v.tensor_reduce(one(3), g(8), AX.X, ALU.max))
                c.link(tt(G[:, 10, :, 0:1], one(2), one(0), ALU.subtract))
                c.link(tt(g(8), g(8), wide_(one(3)), ALU.is_equal))
                dve.wait_ge(exp_gate, n + 1)
                ex = G[:, 11, :, 0:1]
                c.link(ts(one(4), ex, 1.0, None, ALU.add))
                c.link(v.reciprocal(one(5), one(4)))
                if tanh is not None:
                    c.link(ts(one(5), one(5), tanh, None, ALU.mult))
                c.link(tt(one(6), ex, one(5), ALU.mult))
                c.link(tt(g(7), oh1, wide_(one(5)), ALU.mult))
                c.link(tt(g(8), g(8), wide_(one(6)), ALU.mult))
                tt(w_c[:, :, :], g(7), g(8), ALU.add).then_inc(w_ready, 1)
                dve.wait_ge(w_ready, n + 1)
                v.tensor_copy(w_all[:, tok(b, 0, TB), :], w_c[:, :, :]).then_inc(w_copied, 1)
                assert c.k == (TOP2 if s == F1 else TOP2N), c.k

            def add_weighted_bias(s, b, n):
                dve.wait_ge(wb_ps, n + 1)
                xb = x[:, tok(b, 0, TB), :]
                tt(xb, xb, ps[:, 4, :].rearrange("p (i d) -> p i d", d=D), ALU.add).then_inc(x_new, 1)

            def experts(s, J, acc):
                units = E * J
                u0 = UNIT0[s]
                x0 = XNEW0[s] + (B if s == F1 else 0)
                w0 = 0 if s == F1 else B
                dve.wait_ge(w_copied, 2 * B if s == MOE else B)
                with dve.Fori(0, B) as c:
                    dve.wait_ge(x_new, c * (E * TB) + x0)
                    v.tensor_copy(w_c[:, :, :], w_all[:, tok(c, 0, TB), :]).then_inc(scratch_w, 1)
                    dve.wait_ge(scratch_w, c + w0 + 1)

                    def gate_unit(u):
                        e, j = divmod(u, J)
                        dve.wait_ge(silu, c * units + u0 + u + 1)
                        dve.wait_ge(down_ps, c * units + u0 + u + 1)
                        stt(hh[:, u % 2, :], ps[:, 2 + u % 2, :], bgi[:, 1, e, j:j + 1], sg[:, u % 2, :],
                            ALU.add, ALU.mult).then_inc(gated, 1)

                    def add_expert(e):
                        dve.wait_ge(down_ps, c * units + u0 + (e + 1) * J + 2)
                        if e >= 1:
                            dve.wait_ge(x_new, (c * E + e) * TB + x0)
                        for i in range(TB):
                            a = row(acc, c, i)
                            stt(a, ps[:, 4 + e % 2, i * D:(i + 1) * D], w_c[:, i, e:e + 1], a, ALU.mult, ALU.add)\
                                .then_inc(x_new, 1)
                    for e in range(E):
                        for j in range(J):
                            if s == F1:
                                gate_unit(e * J + j)
                            if j == 0 and e > 0:
                                add_expert(e - 1)
                    add_expert(E - 1)

            dve.wait_ge(ld["a"], 16)
            v.tensor_copy(identb[:, :], w("ident")).then_inc(bf_done, 1)
            block_keys(X0)
            dve.wait_ge(ld["x"], 16)
            with dve.Fori(0, B) as b:
                norm(b, TURN0[X0] + b, lambda i: row(x, b, i), xn_of)
            add_output_bias(X0, 1)
            dve.wait_ge(tanh_done, 1)
            cross(X0)

            starts(dve, F0)
            dve.wait_ge(ld["b"], 16)
            with dve.Fori(0, B) as b:
                norm(ROUND0[F0] + b, TURN0[F0] + b, lambda i: row(x, b, i), xn_of)
                gate(F0, b, b, b * TOP1, tg[:, 4:5])
                add_weighted_bias(F0, b, b)
                c = Chain(dve, e0_chain, b * TB)
                for i in range(TB):
                    dve.wait_ge(e0_ps, b * TB + i + 1)
                    pair = 2 * (i % 2)
                    ys = flat[:, pair * BANK:(pair + 2) * BANK].rearrange("p (e d) -> p e d", d=D)
                    tt(wide, ys, w_c[:, i, :].unsqueeze(2).to_broadcast([P, E, D]), ALU.mult).then_inc(e0_read, 1)
                    dve.wait_ge(e0_read, b * TB + i + 3)
                    c.link(v.tensor_reduce(hsum, wide.rearrange("p e d -> p d e"), AX.X, ALU.add))
                    dve.wait_ge(x_new, b * (TB + 1) + XNEW0[F0] + i + 1)
                    tt(row(x, b, i), row(x, b, i), hsum, ALU.add).then_inc(x_new, 1)

            starts(dve, X1)
            dve.wait_ge(kv_ps, KV_PS0[X1] + 1)
            for r in range(KV1):
                norm(ROUND0[X1] - KV1 + r, TURN0[X1] - KV1 + r,
                     lambda i: ps[0:KEYS, i // 2, (2 * (i % 2) + r) * D:(2 * (i % 2) + r + 1) * D],
                     lambda i: xn_s[0:KEYS, i, :], rows=KEYS)
            block_keys(X1)
            with dve.Fori(0, B) as b:
                norm(ROUND0[X1] + b * 2, TURN0[X1] + b * 2, lambda i: row(x, b, i), xn_of)
                dve.wait_ge(q_ps, b + B + 1)
                norm(ROUND0[X1] + b * 2 + 1, TURN0[X1] + b * 2 + 1, lambda i: ps[:, 6, i * D:(i + 1) * D], xn_of)
            dve.wait_ge(mneg_set, 1)
            cross(X1)

            starts(dve, F1)
            with dve.Fori(0, B) as b:
                norm(ROUND0[F1] + b, TURN0[F1] + b, lambda i: row(x, b, i), xn_of)
                gate(F1, b, B + b, b * TOP2 + B * TOP1, tg[:, 5:6])
                add_weighted_bias(F1, b, B + b)
            dve.wait_ge(ld["bgi"], 16)
            experts(F1, J1, x)

            starts(dve, X2)
            dve.wait_ge(ld["c"], 16)
            for u in range(1, 3 * H, 2):
                dve.wait_ge(fold_ps, u + 1)
                v.tensor_copy(folded(u), ps[:, u % 6, 0:CK].rearrange("p (b k) -> p b k", k=KEYS)).then_inc(fold_dve, 1)
            dve.wait_ge(ld["d"], 16)
            v.tensor_copy(heads(cmaskb[:, :]), w("2cm").unsqueeze(1).to_broadcast([P, H, KEYS])).then_inc(bf_done, 1)
            v.tensor_copy(diagb[:, :], w("mcm")).then_inc(bf_done, 1)
            with dve.Fori(0, B) as b:
                norm(ROUND0[X2] + b, TURN0[X2] + b, lambda i: row(x, b, i), xn_of)
            add_output_bias(X2, 2)
            dve.wait_ge(fold_dve, 3 * H // 2)
            cross(X2)

            starts(dve, MLA)
            with dve.Fori(0, B) as b:
                norm(ROUND0[MLA] + b * 2, None, lambda i: row(x, b, i), lambda i: row(y, b, i))
                dve.wait_ge(s_xn, TB * (ROUND0[MLA] + b * 2 + 1))
                norm_rms(b, ROUND0[MLA] + b * 2 + 1, TURN0[MLA] + b, b)
            with dve.Fori(0, B) as b:
                def maxima(t):
                    n = b * H + t.n
                    for i in range(TB):
                        dve.wait_ge(m_scores, n * 4 + i + 9)
                        v.tensor_reduce(negm[:, t.slot(2), i:i + 1], ps[:, i, 0:(i + 1) * P], AX.X, ALU.max, negate=True)\
                            .then_inc(m_rowmax, 1)

                def evacuate(t):
                    n = b * H + t.n
                    dve.wait_ge(m_attn, n + 1)
                    for k in range(3):
                        dve.wait_ge(m_probsT_ps, n * 3 + k + 7)
                        m = min(4, len(BLOCKS) - 4 * k)
                        v.tensor_copy(PT[:, t.slot(2), 4 * k:4 * k + m, :].rearrange("p c n -> p (c n)"),
                                      ps[:, 4 + k, 0:m * P]).then_inc(m_probsT, 1)

                def divide(t):
                    n = b * H + t.n
                    dve.wait_ge(m_attn, n + 3)
                    o = ps[:, 7, 0:TB * VE].rearrange("p (i d) -> p i d", d=VE)
                    v.reciprocal(rec[:, :].unsqueeze(2), o[:, :, HD:VE]).then_inc(m_rec, 1)
                    dve.wait_ge(m_rec, n + 1)
                    tt(o_s[:, :, bass.ds(t.n * HD, HD)], o[:, :, 0:HD], rec[:, :].unsqueeze(2).to_broadcast([P, TB, HD]),
                       ALU.mult).then_inc(m_normed, 1)
                skewed_loop(dve, [(maxima, 0), (evacuate, 1), (divide, 1)], H, 2)
                dve.wait_ge(yo_ps, b + 1)
                yb = y[:, tok(b, 0, TB), :]
                tt(yb, yb, ps[:, 5, :].rearrange("p (i d) -> p i d", d=D), ALU.add).then_inc(x_new, 1)

            starts(dve, MOE)
            with dve.Fori(0, B) as b:
                norm_rms(b, ROUND0[MOE] + b, TURN0[MOE] + b, B + b)
                gate(MOE, b, 2 * B + b, b * TOP2N + B * (TOP1 + TOP2), None)
            experts(MOE, J2, y)

            starts(dve, X3)
            dve.wait_ge(ld["e"], 16)
            dve.wait_ge(ld["m3"], 16)
            dve.wait_ge(ld["rope"], 16)
            dve.wait_ge(kv_ps, KV_PS0[X3] + 3)
            c = Chain(dve, kv_chain)
            perb = lambda a: a.rearrange("p (b k) -> p b k", k=KEYS)
            table = lambda a: a[:, 0:KEYS].unsqueeze(1).to_broadcast([P, B, KEYS])
            c.link(v.tensor_copy(mask3_f[:, :], mask3_u8[:, :]))
            c.link(tt(perb(kA_s), perb(kT_s), table(cosT), ALU.mult))
            c.link(tt(perb(kB_s), perb(ps[:, 2, 0:CK]), table(sinT), ALU.mult))
            c.link(tt(kA_s, kA_s, kB_s, ALU.add))
            c.link(tt(kT_s, kA_s, mask3_f[:, :], ALU.mult))
            block_keys(X3)
            with dve.Fori(0, B) as b:
                xb, yb = x[:, tok(b, 0, TB), :], y[:, tok(b, 0, TB), :]
                stt(xb, yb, tg[:, 6:7], xb, ALU.mult, ALU.add).then_inc(x_new, 1)
                dve.wait_ge(x_new, b + XNEW0[X3] + 1)
                norm(ROUND0[X3] + b, TURN0[X3] + b, lambda i: row(x, b, i), xn_of)
                dve.wait_ge(rot_ps, b + 1)
                c = Chain(dve, rope_chain, b * 2)
                c.link(tt(rope_a, q1_s[:, :], cosT, ALU.mult))
                c.link(tt(rope_b, ps[:, 5, :], sinT, ALU.mult))
                tt(FT[:, cols(b)], rope_a, rope_b, ALU.add).then_inc(roped, 1)
            add_output_bias(X3, 3)
            cross(X3)

            starts(dve, F3)
            ts(bo3[:, :], w("3fbo"), 0.3, None, ALU.mult).then_inc(y_set, 1)
            dve.wait_ge(y_set, 1)
            with dve.Fori(0, B) as b:
                norm(ROUND0[F3] + b, TURN0[F3] + b, lambda i: row(x, b, i), xn_of)
                dve.wait_ge(s_xn, TB * (ROUND0[F3] + b + 1))
                tt(y[:, tok(b, 0, TB), :], xn_s[:, :, :], bo3[:, :].unsqueeze(1).to_broadcast([P, TB, D]), ALU.add)\
                    .then_inc(y_set, 1)
            dve.wait_ge(y_set, B + 1)
            dve.wait_ge(pol, 2)
            c = Chain(dve, sel_chain)
            lg = ps[:, 7, 0:B * E].rearrange("p (b e) -> p b e", e=E)
            of = lambda a: a.unsqueeze(1).to_broadcast([P, B, E])
            one = lambda k: G[:, 3, :, k:k + 1]
            c.link(tt(G[:, 0, :, :], lg, of(w("bp2")), ALU.add))
            c.link(v.tensor_reduce(one(0), G[:, 0, :, :], AX.X, ALU.max))
            c.link(tt(G[:, 1, :, :], G[:, 0, :, :], one(0).to_broadcast([P, B, E]), ALU.subtract))
            c.link(stt(G[:, 5, :, :], G[:, 1, :, :], 0.0, of(w("desc")), ALU.is_ge, ALU.mult))
            c.link(v.tensor_reduce(one(1), G[:, 5, :, :], AX.X, ALU.max))
            c.link(tt(m4[:, :, :], G[:, 5, :, :], one(1).to_broadcast([P, B, E]), ALU.is_equal))
            dve.wait_ge(ld["f3"], 16)

            def select(t):
                wait(dve, r3_ps, t.n - 1)
                wait(dve, r3_sb, t.n - 1)
                d = sel[:, t.slot(2), :]
                for e in range(E):
                    m = m4[:, t.n, e:e + 1]
                    if e == 0:
                        ins = ts(d, W3F[:, e, :], m, None, ALU.mult)
                    else:
                        ins = stt(d, W3F[:, e, :], m, d, ALU.mult, ALU.add)
                    if e < E - 1:
                        c.link(ins)
                ins.then_inc(sel_done, 1)

            def finish(t):
                dve.wait_ge(o3_ps, t.n + 1)
                xb, yb = x[:, t.n * TB:(t.n + 1) * TB, :], y[:, t.n * TB:(t.n + 1) * TB, :]
                c.link(stt(yb, ps[:, 3, :].rearrange("p (i d) -> p i d", d=D), 0.3, yb, ALU.mult, ALU.add))
                stt(xb, yb, tg[:, 7:8], xb, ALU.mult, ALU.add).then_inc(x_new, 1)
            skewed_loop(dve, [(select, 0), (finish, 1)], B, 2)


def _columns(v):
    return v.reshape(-1, P).T


def _rows(v, n=P):
    out = np.zeros((P, v.size), v.dtype)
    out[:n] = v
    return out


def _pad(a):
    out = np.zeros((P, a.shape[1]), a.dtype)
    out[:a.shape[0]] = a
    return out


def _pack(i):
    f = np.float32
    ident = np.eye(P, dtype=f)
    rot = np.zeros((P, P), f)
    for k in range(0, P, 2):
        rot[k + 1, k] = -1.0
        rot[k, k + 1] = 1.0
    causal = np.where(np.arange(KEYS)[None, :] > np.arange(P)[:, None], f(-1e30), f(0)).astype(f)
    diag = np.where(np.arange(P)[None, :] > np.arange(P)[:, None], f(-1e30), f(0)).astype(f)
    two = lambda a: a.reshape(8, P, D).transpose(1, 0, 2).reshape(P, 8 * D)
    v = {
        "ident": ident,
        "hm": (np.arange(P)[:, None] // HD == np.arange(H)[None, :]).astype(f),
        "desc": np.tile(np.arange(E, 0, -1, dtype=f), (P, 1)),
        "gates": _rows(np.concatenate([i["g_xattn"], i["g_ffn"]])),
        "ctxT": i["ctx_1024"].reshape(CK, D).T,
        "0wq": i["L0_xattn_Wq"].T, "0wk": i["L0_xattn_Wk"].T, "0wv": i["L0_xattn_Wv"].T, "0wo": i["L0_xattn_Wo"].T,
        "0b": np.stack([i["L0_xattn_bq"], i["L0_xattn_bk"], i["L0_xattn_bv"]], 1),
        "0bo": _rows(i["L0_xattn_bo"], KEYS),
        "0we": i["L0_ffn_expert_w"].transpose(1, 0, 2).reshape(P, E * D),
        "0eb": _pad(i["L0_ffn_expert_b"]), "0rw": i["L0_ffn_router_w"], "0rb": _rows(i["L0_ffn_router_b"]),
        "1wq": i["L1_xattn_Wq"], "1wkv": np.concatenate([i["L1_xattn_Wk"], i["L1_xattn_Wv"]], 1),
        "1gb": np.stack([i["L1_xattn_" + k] for k in ("gq", "bq", "gk", "bk", "gv", "bv")], 1),
        "1gw": i["L1_ffn_gate_w"].T, "1bo": _pad(i["L1_ffn_bo"]),
        "2wqT": two(i["L2_xattn_Wq"].T), "2wk": i["L2_xattn_Wk"], "2wv": i["L2_xattn_Wv"], "2wo": two(i["L2_xattn_Wo"]),
        "2b": np.concatenate([_columns(i["L2_xattn_" + k]) for k in ("bq", "bk", "bv")], 1),
        "2bo": _rows(i["L2_xattn_bo"], KEYS), "2cm": causal,
        "mwq": i["L2_ffn_Wq"], "mwd": i["L2_ffn_Wdkv"], "mwuk": _pad(i["L2_ffn_Wuk"]), "mwuv": _pad(i["L2_ffn_Wuv"]),
        "mwo": i["L2_ffn_Wo"], "mg": np.stack([i["L2_ffn_g1"], i["L2_ffn_g2"]], 1), "mgw": i["L2_ffn_gate_w"],
        "mcm": diag,
        "3wq": i["L3_xattn_w_q"], "3wk": i["L3_xattn_w_k"], "3wv": i["L3_xattn_w_v"], "3wo": i["L3_xattn_w_o"],
        "3b": np.stack([i["L3_xattn_b_q"], i["L3_xattn_b_k"], i["L3_xattn_b_v"]], 1),
        "3bo": _rows(i["L3_xattn_b_o"], KEYS), "rot": rot,
        "wp1": i["L3_ffn_Wp1"], "bp1": i["L3_ffn_bp1"][:, None], "wp2": i["L3_ffn_Wp2"], "bp2": _rows(i["L3_ffn_bp2"]),
        "3fwo": i["L3_ffn_Wo"], "3fbo": _rows(i["L3_ffn_bo"]),
    }
    order = [n for items in GROUPS.values() for n, _ in items]
    for n in order:
        assert v[n].shape == (P, PLACE[n][1]), (n, v[n].shape)
    return np.ascontiguousarray(np.concatenate([v[n] for n in order], 1))


def _rope():
    f = np.float32
    inv = (f(10000.0) ** (np.arange(0, HD, 2, dtype=f) / f(HD))).astype(f)
    theta = (np.arange(S, dtype=f)[:, None] / inv).astype(f)
    theta = np.tile(np.repeat(theta, 2, axis=1), (1, H)).T
    return np.ascontiguousarray(np.concatenate([np.cos(theta), np.sin(theta)], 1).astype(f))


def kernel(**inputs):
    import concourse.bacc as _bacc
    from concourse.bass_utils import run_bass_kernel_spmd as _run

    i = {k: np.asarray(a) for k, a in inputs.items()}

    def up(a):
        return a.transpose(2, 0, 1).reshape(D, -1)

    def down(a):
        e, h, d = a.shape
        return a.reshape(e, h // P, P, d).transpose(2, 0, 1, 3).reshape(P, -1)

    def cols_of(a):
        e, h = a.shape
        return a.reshape(e, h // P, P).transpose(2, 0, 1)

    arrays = {
        "x": i["x"].reshape(B * S, D),
        "packed": _pack(i),
        "ffn1": np.concatenate([up(i["L1_ffn_wg"]), up(i["L1_ffn_wi"]), down(i["L1_ffn_wo"].transpose(0, 2, 1)),
                                cols_of(i["L1_ffn_bg"]).reshape(P, -1), cols_of(i["L1_ffn_bi"]).reshape(P, -1)], 1),
        "moe": np.concatenate([i["L2_ffn_w1"].transpose(1, 0, 2).reshape(D, -1), down(i["L2_ffn_w2"])], 1),
        "ffn3": np.concatenate([i["L3_ffn_W1"].transpose(1, 0, 2), cols_of(i["L3_ffn_b1"]),
                                down(i["L3_ffn_W2"]).reshape(P, E, J2 * D), i["L3_ffn_b2"].T[:, :, None]],
                               2).reshape(P, -1),
        "rope": _rope(),
        "mask1": np.ascontiguousarray(i["mask_BxSxS2_bk0"]).reshape(-1).view(np.uint32),
        "mask3": np.ascontiguousarray(np.broadcast_to(i["mask_Bx1x1xS2_bf1"].reshape(1, CK), (P, CK))).view(np.uint8),
    }
    arrays = {f"in_{k}": np.ascontiguousarray(a) for k, a in arrays.items()}
    nc = _bacc.Bacc("TRN2", target_bir_lowering=False, num_devices=1)
    args = {k: nc.dram_tensor(k, a.shape, mybir.dt.from_np(a.dtype), kind="ExternalInput").ap()
            for k, a in arrays.items()}
    out = nc.dram_tensor("out_x", (B * S, D), F32, kind="ExternalOutput").ap()
    build(nc, args["in_x"], args["in_packed"], args["in_ffn1"], args["in_moe"], args["in_ffn3"], args["in_rope"],
          args["in_mask1"], args["in_mask3"], out)
    r = _run(nc, [arrays], core_ids=[0])
    return r.results[0]["out_x"].reshape(B, S, D)
```

```python
import numpy as np
import concourse.bass as bass
from concourse import mybir
from contextlib import ExitStack

F32 = mybir.dt.float32
BF16 = mybir.dt.bfloat16
F16 = mybir.dt.float16
U8 = mybir.dt.uint8
ALU = mybir.AluOpType
ACT = mybir.ActivationFunctionType
AX = mybir.AxisListType

B, S, D = 4, 512, 128
KEYS = 77
H, HD = 16, 8
HD2 = 64
P = 128
TB = S // P
NT = B * TB
HK = H * KEYS
CK = B * KEYS
NC = -(-HK // P)
LAST = HK - (NC - 1) * P
E = 8
HID1 = 512
HID2 = 256
J1, J2 = HID1 // P, HID2 // P
LAT = 64
VE = HD + 1
PIECES = 3
PSCALE = 1024.0
BANK = 512
NEG = -3.0e38
SEL = HID2 + J2 + J2 * D + 1
TOP1, TOP2, TOP2N = 8, 19, 18
LN_EPS, RMS_EPS = 1e-5, 1e-6

X0, F0, X1, F1, X2, MLA, MOE, X3, F3 = range(9)
KV1 = 2
ROUNDS = {X0: 1, F0: 1, X1: 2, F1: 1, X2: 1, MLA: 2, MOE: 1, X3: 1, F3: 1}
TURNED = {X0: 1, F0: 1, X1: 2, F1: 1, X2: 1, MLA: 1, MOE: 1, X3: 1, F3: 1}


def before(table, s, kv):
    return sum(B * table[i] for i in range(s)) + (kv if s > X1 else 0)


ROUND0 = {s: before(ROUNDS, s, KV1) + (KV1 if s == X1 else 0) for s in range(9)}
TURN0 = {s: before(TURNED, s, KV1) + (KV1 if s == X1 else 0) for s in range(9)}
X_NEW = {X0: NT, F0: B + NT, X1: NT, F1: B + NT * E, X2: NT, MLA: B, MOE: NT * E, X3: B + NT, F3: B}
XNEW0 = {s: 2 + sum(X_NEW[i] for i in range(s)) for s in range(10)}
LAYER = {X0: 0, X1: 1, X2: 2, X3: 3}
KV_PS0 = {X0: 0, X1: 2, X2: 3, X3: 3 + H}
KV_SB0 = {X0: 0, X2: 2, X3: 2 + H}
FOLD = {X0: 0, X1: 1, X3: 2}
UNIT0 = {F1: 0, MOE: B * E * J1}
BLOCKS = [(i, j) for i in range(TB) for j in range(i + 1)]


class Tile:

    def __init__(self, g, u, k):
        self.k = k
        self.n = k if g is None else g * u + k
        self.group = k // TB if g is None else (g + k // TB if u == TB else None)

    def slot(self, m):
        return self.k % m


def skewed_loop(eng, steps, total, unroll):
    deep = max(lag for _, lag in steps)
    turns = (total - deep) // unroll
    t = 0
    while t < total + deep:
        if t == deep and turns > 1:
            with eng.Fori(0, turns) as g:
                for i in range(unroll):
                    for f, lag in steps:
                        f(Tile(g, unroll, t + i - lag))
            t += turns * unroll
        else:
            for f, lag in steps:
                if 0 <= t - lag < total:
                    f(Tile(None, unroll, t - lag))
            t += 1


class Chain:

    def __init__(self, eng, sem, base=0):
        self.eng, self.sem, self.base, self.k = eng, sem, base, 0

    def link(self, ins):
        self.k += 1
        ins.then_inc(self.sem, 1)
        self.eng.wait_ge(self.sem, self.base + self.k)


GROUPS = {
    "a": [("ident", P), ("hm", H), ("desc", E), ("gates", 8), ("ctxT", CK),
          ("0wq", D), ("0wk", D), ("0wv", D), ("0wo", D), ("0b", 3), ("0bo", D)],
    "b": [("0we", E * D), ("0eb", D), ("0rw", E), ("0rb", E),
          ("1wq", D), ("1wkv", 2 * D), ("1gb", 6), ("1gw", E), ("1bo", D)],
    "c": [("2wqT", 8 * D), ("2wk", 8 * D), ("2wv", 8 * D), ("2wo", 8 * D), ("2b", 24), ("2bo", D), ("2cm", KEYS)],
    "d": [("mwq", D), ("mwd", LAT), ("mwuk", D), ("mwuv", D), ("mwo", D), ("mg", 2), ("mgw", E), ("mcm", P)],
    "e": [("3wq", D), ("3wk", D), ("3wv", D), ("3wo", D), ("3b", 3), ("3bo", D), ("rot", P),
          ("wp1", D), ("bp1", 1), ("wp2", E), ("bp2", E), ("3fwo", D), ("3fbo", D)],
}
PLACE = {}
WIDTH = {}
_at = 0
for _g, _items in GROUPS.items():
    _start = _at
    for _n, _w in _items:
        PLACE[_n] = (_at, _w)
        _at += _w
    WIDTH[_g] = (_start, _at)
PACKED = _at


def build(nc, x_in, packed, w_ffn1, w_moe, w_ffn3, rope, mask1, mask3, out):
    ctx = ExitStack()
    with ctx:
        def sb(name, shape, dt=F32):
            return ctx.enter_context(nc.sbuf_tensor(name, shape, dt))

        def sem(name):
            return ctx.enter_context(nc.semaphore(name))

        W = sb("W", [P, PACKED])

        def w(name, rows=P):
            a, n = PLACE[name]
            return W[0:rows, a:a + n]

        x = sb("x", [P, NT, D])
        FT = sb("FT", [P, B * S])
        xn_s = sb("xn_s", [P, TB, D])
        xnT_s = sb("xnT_s", [P, S])
        q1_s = sb("q1_s", [P, S])
        oT_s = q1_s
        qs = sb("qs", [P, 2, P])
        KBD = sb("KBD", [P, B, HK])
        VW = sb("VW", [P, B, NC, D])
        VBD = sb("VBD", [P, HK])
        att = sb("att", [P, 4, HK])
        PT = sb("PT", [P, 2, NC, P])
        C = sb("C", [P, B * HK])
        U = sb("U", [P, 3 * E * HID1])
        mask_u8 = sb("mask_u8", [P, NT * KEYS], U8)
        mask3_u8 = sb("mask3_u8", [P, CK], U8)
        bo3 = sb("bo3", [P, D])
        identb = sb("identb", [P, P], BF16)
        cmaskb = sb("cmaskb", [P, HK], BF16)
        diagb = sb("diagb", [P, P], BF16)
        tg = sb("tg", [P, 8])
        stats = sb("stats", [P, NT, 6])
        mv = sb("mv", [P, NT, 2])
        ve = sb("ve", [P, NT])
        msq = sb("msq", [P, NT])
        rstd = sb("rstd", [P, NT])
        minus_half = sb("minus_half", [P, TB])
        mx = sb("mx", [P, 2, H])
        rs = sb("rs", [P, 2, H])
        ri = sb("ri", [P, 2, H])
        negm = sb("negm", [P, 2, TB])
        rec = sb("rec", [P, TB])
        o_sum = sb("o_sum", [P, TB, VE])
        w_all = sb("w_all", [P, NT, E])
        w_c = sb("w_c", [P, TB, E])
        G3 = sb("G3", [P, 6, B, E])
        hp_s = sb("hp_s", [P, B])
        m4 = sb("m4", [P, B, E])

        o_s = att[:, :, :].rearrange("p a n -> p (a n)")[:, 4096:4096 + S].rearrange("p (i d) -> p i d", d=D)
        r_s = o_s
        wT_s = att[:, :, :].rearrange("p a n -> p (a n)")[0:E, 2 * HK:2 * HK + B * S].rearrange("e (i p) -> e i p", p=P)
        G = att[:, :, :].rearrange("p a n -> p (a n)")[:, 0:12 * NT * E].rearrange("p (k t e) -> p k t e", k=12, e=E)
        xn_at = (xn_s, PT[:, 1, 4:8, :])
        VBD_at = (VBD[:, :], att[:, 2, :])
        mask3_f = att[:, 1, 0:CK]
        kT_s = att[:, 0, 0:CK]
        vT_s = att[:, 0, CK:2 * CK]
        kA_s = att[:, 0, 2 * CK:3 * CK]
        kB_s = att[:, 0, 3 * CK:4 * CK]
        kT2 = att[:, 0:2, :].rearrange("p a n -> p (a n)").rearrange("p (c n) -> p c n", n=CK)
        vT2 = att[:, 2:4, :].rearrange("p a n -> p (a n)").rearrange("p (c n) -> p c n", n=CK)
        VWT = U[:, 4096:4096 + B * HK].rearrange("p (b n) -> p b n", b=B)
        y = U[:, 9100:9100 + NT * D].rearrange("p (t d) -> p t d", d=D)
        cosT = U[:, 11264:11264 + S]
        sinT = U[:, 11264 + S:11264 + 2 * S]
        WG1 = U[:, 0:E * HID1].rearrange("p (e n) -> p e n", e=E)
        WI1 = U[:, E * HID1:2 * E * HID1].rearrange("p (e n) -> p e n", e=E)
        WO1 = U[:, 2 * E * HID1:3 * E * HID1].rearrange("p (e j d) -> p e j d", e=E, d=D)
        bgi = sb("bgi", [P, 2, E, J1])
        W1M = U[:, 0:E * HID2].rearrange("p (e n) -> p e n", e=E)
        W2M = U[:, E * HID2:2 * E * HID2].rearrange("p (e j d) -> p e j d", e=E, d=D)
        W3F = U[:, 4096:4096 + E * SEL].rearrange("p (e n) -> p e n", e=E)
        mneg = C[:, 0:NT * KEYS].rearrange("p (t k) -> p t k", k=KEYS)
        KT = C[:, 0:B * S]
        VP = KBD[:, :, :].rearrange("p b n -> p (b n)")[:, 0:NT * H * PIECES * VE // 2].bitcast(BF16)\
            .rearrange("p (t h c d) -> p t h c d", h=H, c=PIECES, d=VE)
        v_rest = VBD[:, 0:S]
        PH = PT[:, :, :, :].rearrange("p a c n -> p (a c n)").bitcast(F16)\
            .rearrange("p (a l c n) -> p a l c n", a=2, l=2, n=P)
        rope_a, rope_b = PT[:, 0, 0:4, :].rearrange("p c n -> p (c n)"), PT[:, 1, 0:4, :].rearrange("p c n -> p (c n)")
        nb3 = C[:, 0:B * HK // 2].bitcast(BF16).rearrange("p (b n) -> p b n", b=B)
        kh = VBD[:, 0:2 * S].rearrange("p (a n) -> p a n", a=2)
        Pm = att[:, :, :].rearrange("p a n -> p (a n)")[:, 0:2 * TB * S].rearrange("p (a i n) -> p a i n", a=2, i=TB)
        q_s = xnT_s
        c_s = q1_s
        sg = att[:, 0, 0:2 * S].rearrange("p (a n) -> p a n", a=2)
        hh = att[:, 2, 0:2 * S].rearrange("p (a n) -> p a n", a=2)
        sel = att[:, 0:2, 0:SEL]
        wide = PT[:, :, 0:E, :]
        hsum = PT[:, :, E, :]

        ps = ctx.enter_context(nc.psum_tensor("ps", [P, 8, BANK], F32))
        flat = ps[:, :, :].rearrange("p b n -> p (b n)")

        ld = {g: sem(f"loaded_{g}") for g in list(GROUPS) + ["x", "f1", "bgi", "moe", "f3", "rope", "m1", "m3"]}
        consts = sem("consts")
        tanh_done = sem("tanh_done")
        bf_done = sem("bf_done")
        s_stats, s_aggr, s_ve, s_rstd, s_xn = map(sem, ("stats_done", "aggregated", "var_eps", "rstd_done", "normed"))
        turned, turned_sb = sem("turned"), sem("turned_copied")
        x_new = sem("x_new")
        gate_chain, exp_gate = sem("gate_chain"), sem("exp_gate")
        router_ps = sem("router_ps")
        w_ready, wT_ps, wT_sb, wb_ps = sem("w_ready"), sem("wT_ps"), sem("wT_sb"), sem("wb_ps")
        q_ps, q_sb = sem("q_ps"), sem("q_sb")
        rot_ps, rope_chain, roped = sem("rot_ps"), sem("rope_chain"), sem("roped")
        y_set, nb_set, mneg_set, scratch = sem("y_set"), sem("nb_set"), sem("mneg_set"), sem("scratch")
        kv_ps, kv_sb, kv_chain = sem("kv_ps"), sem("kv_sb"), sem("kv_chain")
        kbd, vbd, vw_ps, vw_sb, vw_bo = map(sem, ("kbd_done", "vbd_done", "vw_ps", "vw_sb", "vw_bo"))
        fold_ps, fold_act, fold_dve = sem("fold_ps"), sem("fold_act"), sem("fold_dve")
        staged, scores, scores_read, rowmax, shifted = map(sem, ("q_staged", "scores", "scores_read", "rowmax", "shifted"))
        expd, rowsum, recip, probs, probsT_ps, probsT, attn_out = map(
            sem, ("exp_done", "rowsum", "recip", "probs", "probsT_ps", "probsT", "attn_out"))
        m_scores, m_rowmax, m_expd, m_probsT_ps, m_probsT, m_attn, m_rec, m_normed = map(
            sem, ("m_scores", "m_rowmax", "m_expd", "m_probsT_ps", "m_probsT", "m_attn", "m_rec", "m_normed"))
        m_q, ones_set, ot_ps, ot_sb, yo_ps = map(sem, ("m_q", "ones_set", "ot_ps", "ot_sb", "yo_ps"))
        head_k = sem("head_k")
        m_high, m_summed = sem("m_high"), sem("m_summed")
        v_chain, v_split = sem("v_chain"), sem("v_split")
        mla_ps, mla_sb = sem("mla_ps"), sem("mla_sb")
        e0_staged, e0_ps, e0_read, e0_summed = map(sem, ("e0_staged", "e0_ps", "e0_read", "e0_summed"))
        up_ps, silu, gated, down_ps = map(sem, ("up_ps", "silu", "gated", "down_ps"))
        pol, pol_sb, sel_done, sel_chain = sem("pol"), sem("pol_sb"), sem("sel_done"), sem("sel_chain")
        h3_ps, h3_sb, r3_ps, r3_sb, o3_ps, fin = map(sem, ("h3_ps", "h3_sb", "r3_ps", "r3_sb", "o3_ps", "fin"))
        stored, scratch_w = sem("stored"), sem("w_staged")

        CREDITS = [(turned, 1), (turned_sb, 1), (vw_ps, 2), (vw_sb, 1), (e0_ps, 2), (e0_read, 2), (e0_summed, 2), (gated, 2), (down_ps, 2),
                   (m_expd, 4), (m_probsT, 3), (m_normed, 1), (m_summed, 1), (m_scores, 8), (m_probsT_ps, 6), (m_attn, 2),
                   (x_new, 2), (scores, 2), (scores_read, 1), (shifted, 1), (expd, 2), (probs, 2), (probsT_ps, 6),
                   (probsT, 3), (attn_out, 2)]

        def tiles_before(s):
            return LAYER[s] * NT

        def wait(eng, sm, value):
            if isinstance(value, int) and value <= 0:
                return
            eng.wait_ge(sm, value)

        def tok(b, i, n=1):
            return bass.ds(b * TB + i, n)

        def cols(b, n=S):
            return bass.ds(b * n, n)

        def batch(t, b):
            v = t[:, bass.ds(b, 1)]
            return v.rearrange("p b n -> p (b n)") if len(v.shape) == 3 else v.rearrange("p b c n -> p (b c n)")

        def heads(a):
            return a.rearrange("p (h k) -> p h k", k=KEYS)

        def over_keys(a):
            return a.unsqueeze(2).to_broadcast([P, H, KEYS])

        def folded(u):
            h, k = divmod(u, 3)
            return (KBD[:, :, :], C[:, :].rearrange("p (b n) -> p b n", b=B), VWT)[k][:, :, h * KEYS:(h + 1) * KEYS]

        def values_of(b, j, h):
            return VP[:, tok(b, j), bass.ds(h, 1), :, :].rearrange("p t h c d -> p (t h c d)")

        def starts(eng, s):
            if s > X0:
                eng.wait_ge(x_new, XNEW0[s])

        block = ctx.enter_context(nc.Block())

        @block.sync
        def _(sp):
            for sm, n in CREDITS:
                sp.sem_inc(sm, n)

            def load(dst, src, g):
                sp.dma_start(dst, src).then_inc(ld[g], 16)

            a, z = WIDTH["a"]
            load(W[:, a:z], packed[:, a:z], "a")
            load(x[:, :, :], x_in.rearrange("(t p) d -> p t d", p=P), "x")
            for g in "bcde":
                a, z = WIDTH[g]
                load(W[:, a:z], packed[:, a:z], g)
                if g == "b":
                    load(mask_u8[:, :].rearrange("p (t k) -> p t k", k=KEYS),
                         mask1.bitcast(U8).rearrange("(t p k) -> p t k", p=P, k=KEYS), "m1")
                    load(U[:, :], w_ffn1[:, 0:3 * E * HID1], "f1")
                    load(bgi[:, :, :, :].rearrange("p a e j -> p (a e j)"), w_ffn1[:, 3 * E * HID1:], "bgi")
            load(mask3_u8[:, :], mask3, "m3")
            sp.wait_ge(x_new, XNEW0[X2])
            load(U[:, 0:2 * E * HID2], w_moe, "moe")
            load(U[:, 11264:11264 + 2 * S], rope, "rope")
            sp.wait_ge(x_new, XNEW0[MLA])
            load(U[:, 4096:4096 + E * SEL], w_ffn3, "f3")
            for b in range(B):
                sp.wait_ge(x_new, XNEW0[F3] + b + 1)
                sp.dma_start(out[b * S:(b + 1) * S, :].rearrange("(t p) d -> p t d", p=P),
                             x[:, b * TB:(b + 1) * TB, :]).then_inc(stored, 16)
            sp.wait_ge(stored, 16 * B)

        @block.tensor
        def _(pe):
            mm = pe.matmul
            ident = w("ident")
            pe.wait_ge(ld["a"], 16)

            def turn(nth, rounds, rows=P):
                pe.wait_ge(s_xn, TB * rounds)
                pe.wait_ge(turned_sb, nth + 1)
                for i in range(TB):
                    t = pe.transpose(ps[:, 7, i * rows:(i + 1) * rows], xn_at[nth % 2][0:rows, i, :],
                                     ident[0:rows, 0:rows])
                t.then_inc(turned, 1)

            def prepare(s, after):
                starts(pe, s)
                first = B if s == MLA else 0
                for b in range(B):
                    turn(TURN0[s] + b, ROUND0[s] + first + b + 1)
                    if after is not None:
                        after(b)

            def turned_copied(s, b):
                pe.wait_ge(turned_sb, TURN0[s] + b + 2)

            def route(s, b, weight):
                turned_copied(s, b)
                for i in range(TB):
                    t = mm(ps[:, 6, (b * TB + i) * E:(b * TB + i + 1) * E], xnT_s[:, i * P:(i + 1) * P], weight, start=True, stop=True)
                t.then_inc(router_ps, 1)

            def weighted_bias(n, rows):
                pe.wait_ge(w_ready, n + 1)
                for b in range(B):
                    for i in range(TB):
                        t = pe.transpose(ps[0:E, 2 + b, i * P:(i + 1) * P], w_all[:, b * TB + i, :], ident)
                    t.then_inc(wT_ps, 1)
                for b in range(B):
                    pe.wait_ge(wT_sb, n * B + b + 1)
                    for i in range(TB):
                        t = mm(ps[:, 2 + b, i * D:(i + 1) * D], wT_s[:, b * TB + i, :], rows, start=True, stop=True)
                    t.then_inc(wb_ps, 1)

            def fold_values(s, wo, b):
                n = FOLD[s] * B + b
                pe.wait_ge(vbd, n + 1)
                pe.wait_ge(vw_sb, n + 1)
                for c in range(NC):
                    m = P if c < NC - 1 else LAST
                    t = mm(ps[0:m, c // 4, (c % 4) * D:(c % 4 + 1) * D], VBD_at[b % 2][:, c * P:c * P + m], wo,
                           start=True, stop=True)
                t.then_inc(vw_ps, 1)

            def keys_values(s):
                starts(pe, s)
                if s in (X0, X3):
                    l = LAYER[s]
                    pe.wait_ge(ld["a" if s == X0 else "e"], 16)
                    mm(ps[:, 0, 0:CK], w(f"{l}wk"), w("ctxT"), start=True, stop=True).then_inc(kv_ps, 1)
                    mm(ps[:, 1, 0:CK], w(f"{l}wv"), w("ctxT"), start=True, stop=True).then_inc(kv_ps, 1)
                    pe.wait_ge(kv_sb, KV_SB0[s] + 2)
                    if s == X3:
                        mm(ps[:, 2, 0:CK], w("rot"), kT_s, start=True, stop=True).then_inc(kv_ps, 1)
                        pe.wait_ge(kv_chain, 3)
                    for b in range(2):
                        fold_values(s, w(f"{l}wo"), b)
                elif s == X1:
                    for b in range(B):
                        t = mm(ps[0:KEYS, b // 2, (b % 2) * 2 * D:(b % 2 + 1) * 2 * D],
                               w("ctxT")[:, b * KEYS:(b + 1) * KEYS], w("1wkv"), start=True, stop=True)
                    t.then_inc(kv_ps, 1)
                    for r in range(KV1):
                        turn(TURN0[X1] - KV1 + r, ROUND0[X1] - KV1 + r + 1, rows=KEYS)
                    for b in range(2):
                        fold_values(s, ident, b)
                else:
                    pe.wait_ge(ld["c"], 16)
                    for u in range(H):
                        if u >= 6:
                            pe.wait_ge(kv_sb, KV_SB0[X2] + u - 5)
                        wt = w("2wk") if u % 2 == 0 else w("2wv")
                        c = u // 2
                        mm(ps[:, u % 6, 0:CK], wt[:, c * D:(c + 1) * D], w("ctxT"), start=True, stop=True)\
                            .then_inc(kv_ps, 1)
                    pe.wait_ge(kv_sb, KV_SB0[X2] + H)
                    for u in range(3 * H):
                        if u >= 6:
                            pe.wait_ge(fold_act if u % 2 == 0 else fold_dve, (u - 6) // 2 + 1)
                        h, k = divmod(u, 3)
                        c, r = h // 2, HD2 * (h % 2)
                        rows = slice(r, r + HD2)
                        lhs = (w("2wqT")[rows, c * D:(c + 1) * D],
                               w("2b")[rows, c:c + 1].to_broadcast([HD2, P]),
                               w("2wo")[rows, c * D:(c + 1) * D])[k]
                        rhs = (kT2, kT2, vT2)[k][rows, c, :]
                        mm(ps[:, u % 6, 0:CK], lhs, rhs, start=True, stop=True).then_inc(fold_ps, 1)
                    pe.wait_ge(fold_act, 3 * H // 2)
                    pe.wait_ge(fold_dve, 3 * H // 2)
                    for b in range(B):
                        if b >= 2:
                            pe.wait_ge(fold_act, 3 * H // 2 + b - 1)
                        for c in range(NC):
                            m = P if c < NC - 1 else LAST
                            k = 3 * (b % 2) + c // 4
                            t = pe.transpose(ps[0:m, k, (c % 4) * D:(c % 4 + 1) * D], VWT[:, b, c * P:c * P + m],
                                             ident)
                        t.then_inc(fold_ps, 1)

            def cross(s):
                n0 = tiles_before(s)

                def score(t):
                    pe.wait_ge(staged, t.n + n0 + 1)
                    if s in (X1, X2):
                        pe.wait_ge(scores_read, t.n + (LAYER[s] - 1) * NT + 1)
                    else:
                        pe.wait_ge(shifted, t.n + n0 + 1)
                    causal = s == X2 and t.k % TB == 0
                    for c in range(3):
                        a, z = c * BANK, min((c + 1) * BANK, HK)
                        m = mm(flat[:, a:z], qs[:, t.slot(2), :], batch(KBD, t.group)[:, a:z],
                               start=True, stop=not (causal or s == X3))
                        if causal:
                            m = mm(flat[:, a:z], identb[:, :], cmaskb[:, a:z], start=False, stop=True)
                        if s == X3:
                            m = mm(flat[:, a:z], identb[:, :], batch(nb3, t.group)[:, a:z], start=False, stop=True)
                    m.then_inc(scores, 1)

                def turn_probs(t):
                    pe.wait_ge(probs, t.n + n0 + 3)
                    for k in range(3):
                        pe.wait_ge(probsT, t.n * 3 + 3 * n0 + k + 1)
                        for c in range(4 * k, min(4 * k + 4, NC)):
                            m = P if c < NC - 1 else LAST
                            q = pe.transpose(ps[0:m, 3 + k, (c % 4) * P:(c % 4 + 1) * P],
                                             att[:, 2 + t.slot(2), c * P:c * P + m], ident)
                        q.then_inc(probsT_ps, 1)

                def product(t):
                    pe.wait_ge(x_new, t.n + XNEW0[s] + (B if s == X3 else 0) - 1)
                    for k in range(3):
                        pe.wait_ge(probsT, t.n * 3 + 3 * n0 + k + 4)
                        for c in range(4 * k, min(4 * k + 4, NC)):
                            m = P if c < NC - 1 else LAST
                            q = mm(ps[:, 6 + t.slot(2), 0:D], PT[0:m, t.slot(2), c, :],
                                   batch(VW, t.group)[0:m, c * D:(c + 1) * D], start=(c == 0), stop=(c == NC - 1))
                    q.then_inc(attn_out, 1)

                if s != X2:
                    pe.wait_ge(kbd, FOLD[s] + 1)
                if s == X1:
                    pe.wait_ge(vw_sb, (FOLD[s] + 1) * B + 1)
                else:
                    pe.wait_ge(vw_bo, {X0: 1, X2: 2, X3: 3}[s])
                if s == X2:
                    pe.wait_ge(bf_done, 3)
                if s == X3:
                    pe.wait_ge(nb_set, 1)
                skewed_loop(pe, [(score, 0), (product, 3), (turn_probs, 2)], NT, TB)

            def experts(s, J, wg, wi, wo):
                units = E * J
                u0 = UNIT0[s]
                x0 = XNEW0[s] + (B if s == F1 else 0)
                pe.wait_ge(x_new, x0)

                def chunk(c):
                    def up(u):
                        e, j = divmod(u, J)
                        if s == F1:
                            pe.wait_ge(gated, c * units + u0 + u + 1)
                        else:
                            pe.wait_ge(silu, c * units + u0 + u - 1)
                        t = mm(ps[:, u % 2, :], wg[:, e, j * P:(j + 1) * P], FT[:, cols(c)], start=True, stop=True)
                        if wi is not None:
                            t = mm(ps[:, 2 + u % 2, :], wi[:, e, j * P:(j + 1) * P], FT[:, cols(c)],
                                   start=True, stop=True)
                        t.then_inc(up_ps, 1)

                    def down(u):
                        e, j = divmod(u, J)
                        if s == F1:
                            pe.wait_ge(gated, c * units + u0 + u + 3)
                        else:
                            pe.wait_ge(silu, c * units + u0 + u + 1)
                        if j == 0:
                            pe.wait_ge(x_new, (c * E + e - 1) * TB + x0)
                        for i in range(TB):
                            t = mm(ps[:, 4 + e % 2, i * D:(i + 1) * D], hh[:, u % 2, i * P:(i + 1) * P], wo[:, e, j, :],
                                   start=(j == 0 and i == 0), stop=(j == J - 1 and i == TB - 1))
                        t.then_inc(down_ps, 1)

                    up(0)
                    for u in range(1, units):
                        up(u)
                        down(u - 1)
                    down(units - 1)
                with pe.Fori(0, B) as c:
                    chunk(c)

            keys_values(X0)

            def q0(b):
                turned_copied(X0, b)
                mm(ps[:, 6, :], w("0wq"), xnT_s[:, :], start=True, stop=True).then_inc(q_ps, 1)
            prepare(X0, q0)
            for b in range(2, B):
                fold_values(X0, w("0wo"), b)
            cross(X0)

            pe.wait_ge(ld["b"], 16)

            prepare(F0, lambda b: route(F0, b, w("0rw")))
            weighted_bias(0, w("0eb", E))

            def experts0(t):
                pe.wait_ge(e0_staged, t.n + 1)
                pe.wait_ge(e0_read, t.n + 1)
                for c in range(2):
                    m = mm(ps[:, 6 * t.slot(2) + c, :], qs[:, t.slot(2), :], w("0we")[:, c * BANK:(c + 1) * BANK],
                           start=True, stop=True)
                m.then_inc(e0_ps, 1)
            skewed_loop(pe, [(experts0, 0)], NT, TB)

            keys_values(X1)

            def q1(b):
                turned_copied(X1, b)
                for i in range(TB):
                    t = mm(ps[:, 3 + b, i * D:(i + 1) * D], xnT_s[:, i * P:(i + 1) * P], w("1wq"), start=True, stop=True)
                t.then_inc(q_ps, 1)
            prepare(X1, q1)
            for b in range(2, B):
                fold_values(X1, ident, b)
            for b in range(B):
                turn(TURN0[X1] + B + b, ROUND0[X1] + B + b + 1)
            cross(X1)

            prepare(F1, lambda b: route(F1, b, w("1gw")))
            weighted_bias(1, w("1bo", E))
            pe.wait_ge(ld["f1"], 16)
            experts(F1, J1, WG1, WI1, WO1)

            keys_values(X2)
            prepare(X2, None)
            cross(X2)

            pe.wait_ge(ld["d"], 16)

            def latents(b):
                turned_copied(MLA, b)
                mm(ps[:, 6, :], w("mwq"), xnT_s[:, :], start=True, stop=True).then_inc(mla_ps, 1)
                mm(ps[0:LAT, 5, :], w("mwd"), xnT_s[:, :], start=True, stop=True).then_inc(mla_ps, 1)
                pe.wait_ge(mla_sb, b * 3 + 2)
                mm(ps[:, 4, :], w("mwuk", LAT), c_s[0:LAT, :], start=True, stop=True).then_inc(mla_ps, 1)
                for i in range(TB):
                    t = mm(ps[:, b, i * D:(i + 1) * D], c_s[0:LAT, i * P:(i + 1) * P], w("mwuv", LAT),
                           start=True, stop=True)
                t.then_inc(mla_ps, 1)
            prepare(MLA, latents)

            pe.wait_ge(mla_sb, 3 * B)
            pe.wait_ge(v_split, B)
            pe.wait_ge(ones_set, 2)
            pe.wait_ge(bf_done, 3)

            with pe.Fori(0, B) as b:
                def score(t):
                    n = b * H + t.n
                    pe.wait_ge(head_k, n + 1)
                    for i in range(TB):
                        pe.wait_ge(m_expd, n * 4 + i + 1)
                        z = (i + 1) * P
                        mm(ps[:, i, i * P:z], identb[:, :], diagb[:, :], start=True, stop=False, skip_group_check=True)
                        mm(ps[:, i, 0:z], q_s[:, i * P:(i + 1) * P], kh[:, t.slot(2), 0:z], start=False, stop=True,
                           skip_group_check=True).then_inc(m_scores, 1)

                def turn_probs(t):
                    n = b * H + t.n
                    for k in range(3):
                        pe.wait_ge(m_probsT, n * 3 + k + 1)
                        for c in range(4 * k, min(4 * k + 4, len(BLOCKS))):
                            i, j = BLOCKS[c]
                            if j == 0:
                                pe.wait_ge(m_expd, n * 4 + i + 5)
                            q = pe.transpose(ps[:, 4 + k, (c % 4) * P:(c % 4 + 1) * P],
                                             Pm[:, t.slot(2), i, j * P:(j + 1) * P], ident)
                        q.then_inc(m_probsT_ps, 1)

                def weigh(t):
                    n = b * H + t.n
                    pe.wait_ge(m_summed, n + 1)
                    for c, (i, j) in enumerate(BLOCKS):
                        if c % 4 == 0:
                            pe.wait_ge(m_probsT, n * 3 + c // 4 + 4)
                        for half in range(2):
                            q = mm(ps[:, 7, i * PIECES * VE:(i + 1) * PIECES * VE], PH[:, t.slot(2), half, c, :],
                                   values_of(b, j, t.n), start=(j == 0 and half == 0), stop=(j == i and half == 1))
                    q.then_inc(m_attn, 1)

                pe.wait_ge(m_q, b + 1)
                skewed_loop(pe, [(score, 0), (turn_probs, 1), (weigh, 2)], H, 2)
                pe.wait_ge(m_normed, b * H + H + 1)
                for i in range(TB):
                    t = pe.transpose(ps[:, 4, i * P:(i + 1) * P], o_s[:, i, :], ident)
                t.then_inc(ot_ps, 1)
                pe.wait_ge(ot_sb, b + 1)
                for i in range(TB):
                    t = mm(ps[:, 5, i * D:(i + 1) * D], oT_s[:, i * P:(i + 1) * P], w("mwo"), start=True, stop=True)
                t.then_inc(yo_ps, 1)
                pe.wait_ge(x_new, b + XNEW0[MLA] + 1)

            prepare(MOE, lambda b: route(MOE, b, w("mgw")))
            pe.wait_ge(ld["moe"], 16)
            experts(MOE, J2, W1M, None, W2M)

            keys_values(X3)

            def q3(b):
                turned_copied(X3, b)
                mm(ps[:, 6, :], w("3wq"), xnT_s[:, :], start=True, stop=True).then_inc(q_ps, 1)
                pe.wait_ge(q_sb, b + B + 1)
                if b >= 3:
                    pe.wait_ge(roped, b - 2)
                mm(ps[:, 3 + b % 3, :], w("rot"), FT[:, b * S:(b + 1) * S], start=True, stop=True).then_inc(rot_ps, 1)
            prepare(X3, q3)
            for b in range(2, B):
                fold_values(X3, w("3wo"), b)
            cross(X3)

            prepare(F3, None)
            pe.wait_ge(turned_sb, TURN0[F3] + B + 1)
            mm(ps[:, 6, 0:B], w("wp1"), FT[:, S - 1:B * S:S], start=True, stop=True).then_inc(pol, 1)
            pe.wait_ge(pol_sb, 1)
            for b in range(B):
                t = mm(ps[:, 7, b * E:(b + 1) * E], hp_s[:, b:b + 1].to_broadcast([P, P]), w("wp2"),
                       start=True, stop=True)
            t.then_inc(pol, 1)

            def ffn3(t):
                sl = t.slot(2)
                pe.wait_ge(sel_done, t.n + 1)
                for f in range(J2):
                    mm(ps[:, f, :], sel[:, sl, f * P:(f + 1) * P], FT[:, cols(t.n)], start=True, stop=True)\
                        .then_inc(h3_ps, 1)
                for f in range(J2):
                    pe.wait_ge(h3_sb, t.n * J2 + f + 1)
                    a = HID2 + J2 + f * D
                    m = mm(ps[:, 2, :], sel[:, sl, a:a + D], hh[:, f, :], start=(f == 0), stop=(f == J2 - 1))
                m.then_inc(r3_ps, 1)
                pe.wait_ge(r3_sb, t.n + 1)
                pe.wait_ge(x_new, t.n + XNEW0[F3])
                for i in range(TB):
                    m = mm(ps[:, 3, i * D:(i + 1) * D], r_s[:, i, :], w("3fwo"), start=True, stop=True)
                m.then_inc(o3_ps, 1)
            skewed_loop(pe, [(ffn3, 0)], B, 2)

        @block.scalar
        def _(act):
            go = act.activation
            act.wait_ge(ld["a"], 16)
            go(tg[:, :], w("gates"), ACT.Tanh).then_inc(tanh_done, 1)

            def turned_copy(s, b, k, copies):
                act.wait_ge(turned, TURN0[s] + k * B + b + 2)
                for dst, scale, bias in copies:
                    if bias is not None:
                        t = go(dst, ps[:, 7, :], ACT.Identity, scale=scale, bias=bias)
                    elif scale is not None:
                        t = go(dst, ps[:, 7, :], ACT.Copy, scale=scale)
                    else:
                        t = go(dst, ps[:, 7, :], ACT.Copy)
                t.then_inc(turned_sb, 1)

            def copy_vw(b, k0):
                vw = VW[:, b, :, :].rearrange("p c n -> p (c n)")
                go(vw[:, 0:4 * D], ps[:, k0, :], ACT.Copy)
                go(vw[:, 4 * D:8 * D], ps[:, k0 + 1, :], ACT.Copy)
                go(vw[:, 8 * D:9 * D], ps[:, k0 + 2, 0:D], ACT.Copy)
                return go(vw[0:LAST, 9 * D:10 * D], ps[0:LAST, k0 + 2, D:2 * D], ACT.Copy)

            def fold_values(s, b):
                n = b + FOLD[s] * B
                act.wait_ge(vw_ps, n + 3)
                copy_vw(b, 0).then_inc(vw_sb, 1)

            def keys_values(s):
                starts(act, s)
                if s in (X0, X3):
                    b_ = w(f"{LAYER[s]}b")
                    act.wait_ge(ld["a" if s == X0 else "e"], 16)
                    act.wait_ge(kv_ps, KV_PS0[s] + 1)
                    go(kT_s, ps[:, 0, 0:CK], ACT.Identity, bias=b_[:, 1:2]).then_inc(kv_sb, 1)
                    act.wait_ge(kv_ps, KV_PS0[s] + 2)
                    go(vT_s, ps[:, 1, 0:CK], ACT.Identity, bias=b_[:, 2:3]).then_inc(kv_sb, 1)
                    for b in range(2):
                        fold_values(s, b)
                elif s == X1:
                    act.wait_ge(ld["b"], 16)
                    gb = w("1gb")
                    for r, dst in enumerate((kT_s, vT_s)):
                        act.wait_ge(turned, TURN0[X1] - KV1 + r + 2)
                        go(dst, ps[:, 7, 0:CK], ACT.Identity, scale=gb[:, 2 + 2 * r:3 + 2 * r],
                           bias=gb[:, 3 + 2 * r:4 + 2 * r]).then_inc(turned_sb, 1)
                    for b in range(2):
                        fold_values(s, b)
                else:
                    act.wait_ge(ld["c"], 16)
                    for u in range(H):
                        c = u // 2
                        act.wait_ge(kv_ps, KV_PS0[X2] + u + 1)
                        k = 8 if u % 2 == 0 else 16
                        go((kT2 if u % 2 == 0 else vT2)[:, c, :], ps[:, u % 6, 0:CK], ACT.Identity,
                           bias=w("2b")[:, k + c:k + c + 1]).then_inc(kv_sb, 1)
                    for u in range(0, 3 * H, 2):
                        act.wait_ge(fold_ps, u + 1)
                        go(folded(u), ps[:, u % 6, 0:CK].rearrange("p (b k) -> p b k", k=KEYS), ACT.Copy)\
                            .then_inc(fold_act, 1)
                    for b in range(B):
                        act.wait_ge(fold_ps, 3 * H + b + 1)
                        copy_vw(b, 3 * (b % 2)).then_inc(fold_act, 1)

            def cross(s, scale):
                n0 = tiles_before(s)

                def stage(t):
                    act.wait_ge(scores, t.n + n0 + 1)
                    go(qs[:, t.slot(2), :], FT[:, bass.ds(t.n * P, P)], ACT.Copy).then_inc(staged, 1)

                def exponent(t):
                    act.wait_ge(shifted, t.n + n0 + 2)
                    act.wait_ge(probsT_ps, t.n * 3 + 3 * n0 + 3)
                    go(att[:, 2 + t.slot(2), :], att[:, t.slot(2), :], ACT.Exp, scale=scale).then_inc(expd, 1)

                def evacuate(t):
                    act.wait_ge(attn_out, t.n + n0 + 1)
                    for k in range(3):
                        act.wait_ge(probsT_ps, t.n * 3 + 3 * n0 + k + 7)
                        if k < 2:
                            go(PT[:, t.slot(2), 4 * k:4 * k + 4, :].rearrange("p c n -> p (c n)"), ps[:, 3 + k, :],
                               ACT.Copy).then_inc(probsT, 1)
                        else:
                            go(PT[:, t.slot(2), 8, :], ps[:, 5, 0:P], ACT.Copy)
                            go(PT[0:LAST, t.slot(2), 9, :], ps[0:LAST, 5, P:2 * P], ACT.Copy).then_inc(probsT, 1)

                skewed_loop(act, [(stage, 0), (evacuate, 3), (exponent, 1)], NT, TB)

            def gate_exp(n, chain, src, dst):
                act.wait_ge(gate_chain, chain)
                go(dst, src, ACT.Exp).then_inc(exp_gate, 1)

            def copy_wT(n):
                for b in range(B):
                    act.wait_ge(wT_ps, n * B + b + 1)
                    go(wT_s[:, b * TB:(b + 1) * TB, :].rearrange("e i p -> e (i p)"), ps[0:E, 2 + b, :], ACT.Copy)\
                        .then_inc(wT_sb, 1)

            def hidden(s, J, dst):
                units = E * J
                u0 = UNIT0[s]
                with act.Fori(0, B) as c:
                    for u in range(units):
                        e, j = divmod(u, J)
                        act.wait_ge(up_ps, c * units + u0 + u + 1)
                        if s == F1:
                            act.wait_ge(gated, c * units + u0 + u + 1)
                            go(dst[:, u % 2, :], ps[:, u % 2, :], ACT.Silu, bias=bgi[:, 0, e, j:j + 1]).then_inc(silu, 1)
                        else:
                            act.wait_ge(down_ps, c * units + u0 + u + 1)
                            go(dst[:, u % 2, :], ps[:, u % 2, :], ACT.Silu).then_inc(silu, 1)

            keys_values(X0)
            for b in range(B):
                turned_copy(X0, b, 0, [(xnT_s[:, :], None, None)])
                act.wait_ge(q_ps, b + 1)
                go(FT[:, cols(b)], ps[:, 6, :], ACT.Identity, bias=w("0b")[:, 0:1]).then_inc(q_sb, 1)
            for b in range(2, B):
                fold_values(X0, b)
            act.wait_ge(q_sb, B)
            cross(X0, HD ** -0.5)

            starts(act, F0)
            for b in range(B):
                turned_copy(F0, b, 0, [(xnT_s[:, :], None, None), (FT[:, cols(b)], None, None)])
            gate_exp(0, 3, G[:, 1, :, :], G[:, 2, :, :])
            copy_wT(0)

            def stage0(t):
                act.wait_ge(e0_ps, t.n + 1)
                go(qs[:, t.slot(2), :], FT[:, bass.ds(t.n * P, P)], ACT.Copy).then_inc(e0_staged, 1)
            act.wait_ge(turned_sb, TURN0[F0] + B + 1)
            skewed_loop(act, [(stage0, 0)], NT, TB)

            keys_values(X1)
            for b in range(B):
                turned_copy(X1, b, 0, [(xnT_s[:, :], None, None)])
            for b in range(2, B):
                fold_values(X1, b)
            for b in range(B):
                turned_copy(X1, b, 1, [(FT[:, cols(b)], w("1gb")[:, 0:1], w("1gb")[:, 1:2])])
            act.wait_ge(turned_sb, TURN0[X1] + 2 * B + 1)
            cross(X1, 1.0)

            starts(act, F1)
            for b in range(B):
                turned_copy(F1, b, 0, [(xnT_s[:, :], None, None), (FT[:, cols(b)], None, None)])
            gate_exp(1, TOP1 + 12, G[:, 10, :, 0:1], G[:, 11, :, 0:1])
            copy_wT(1)
            act.wait_ge(ld["bgi"], 16)
            hidden(F1, J1, sg)

            keys_values(X2)
            for b in range(B):
                turned_copy(X2, b, 0, [(FT[:, cols(b)], None, None)])
            act.wait_ge(turned_sb, TURN0[X2] + B + 1)
            cross(X2, HD2 ** -0.5)

            starts(act, MLA)
            act.wait_ge(ld["d"], 16)
            for b in range(B):
                turned_copy(MLA, b, 0, [(xnT_s[:, :], w("mg")[:, 0:1], None)])
                act.wait_ge(mla_ps, b * 4 + 1)
                go(FT[:, cols(b)], ps[:, 6, :], ACT.Copy, scale=HD ** -0.5).then_inc(mla_sb, 1)
                act.wait_ge(mla_ps, b * 4 + 2)
                go(c_s[0:LAT, :], ps[0:LAT, 5, :], ACT.Copy).then_inc(mla_sb, 1)
                act.wait_ge(mla_ps, b * 4 + 3)
                go(KT[:, cols(b)], ps[:, 4, :], ACT.Copy).then_inc(mla_sb, 1)
            act.wait_ge(mla_sb, 3 * B)

            with act.Fori(0, B) as b:
                act.wait_ge(m_scores, b * (4 * H) + 8)
                go(q_s[:, :], FT[:, cols(b)], ACT.Copy).then_inc(m_q, 1)

                def exponent(t):
                    n = b * H + t.n
                    act.wait_ge(m_probsT_ps, n * 3 + 3)
                    for i in range(TB):
                        act.wait_ge(m_rowmax, n * 4 + i + 1)
                        z = (i + 1) * P
                        go(Pm[:, t.slot(2), i, 0:z], ps[:, i, 0:z], ACT.Exp, bias=negm[:, t.slot(2), i:i + 1])\
                            .then_inc(m_expd, 1)

                def high_half(t):
                    n = b * H + t.n
                    act.wait_ge(m_attn, n + 1)
                    for k in range(3):
                        act.wait_ge(m_probsT_ps, n * 3 + k + 7)
                        m = min(4, len(BLOCKS) - 4 * k)
                        go(PH[:, t.slot(2), 0, 4 * k:4 * k + m, :].rearrange("p c n -> p (c n)"), ps[:, 4 + k, 0:m * P],
                           ACT.Copy, scale=PSCALE).then_inc(m_high, 1)
                skewed_loop(act, [(high_half, 1), (exponent, 0)], H, 2)
                act.wait_ge(ot_ps, b + 1)
                go(oT_s[:, :], ps[:, 4, :], ACT.Copy).then_inc(ot_sb, 1)

            starts(act, MOE)
            for b in range(B):
                turned_copy(MOE, b, 0, [(xnT_s[:, :], w("mg")[:, 1:2], None), (FT[:, cols(b)], w("mg")[:, 1:2], None)])
            gate_exp(2, TOP1 + TOP2 + 12, G[:, 10, :, 0:1], G[:, 11, :, 0:1])
            hidden(MOE, J2, hh)

            keys_values(X3)
            for b in range(B):
                turned_copy(X3, b, 0, [(xnT_s[:, :], None, None)])
                act.wait_ge(q_ps, b + 2 * B + 1)
                go(FT[:, cols(b)], ps[:, 6, :], ACT.Identity, bias=w("3b")[:, 0:1]).then_inc(q_sb, 1)
            for b in range(2, B):
                fold_values(X3, b)
            act.wait_ge(roped, B)
            cross(X3, HD ** -0.5)

            starts(act, F3)
            for b in range(B):
                turned_copy(F3, b, 0, [(FT[:, cols(b)], None, None)])
            act.wait_ge(pol, 1)
            go(hp_s[:, :], ps[:, 6, 0:B], ACT.Gelu, bias=w("bp1")).then_inc(pol_sb, 1)

            def gelu3(t):
                sl = t.slot(2)
                wait(act, r3_ps, t.n)
                for f in range(J2):
                    act.wait_ge(h3_ps, t.n * J2 + f + 1)
                    go(hh[:, f, :], ps[:, f, :], ACT.Gelu, bias=sel[:, sl, HID2 + f:HID2 + f + 1]).then_inc(h3_sb, 1)
                act.wait_ge(r3_ps, t.n + 1)
                wait(act, o3_ps, t.n)
                go(r_s[:, :, :].rearrange("p i d -> p (i d)"), ps[:, 2, :], ACT.Identity, bias=sel[:, sl, SEL - 1:SEL])\
                    .then_inc(r3_sb, 1)
            skewed_loop(act, [(gelu3, 0)], B, 2)

        @block.gpsimd
        def _(pool):
            tt = pool.tensor_tensor
            pool.memset(minus_half[:, :], -0.5).then_inc(consts, 1)
            pool.wait_ge(consts, 1)

            def root(n, b):
                pool.wait_ge(s_ve, n + 1)
                at = slice(b * TB, (b + 1) * TB)
                tt(rstd[:, at], ve[:, at], minus_half[:, :], ALU.pow).then_inc(s_rstd, 1)

            def roots(s, k=0):
                for b in range(B):
                    root(ROUND0[s] + k * B + b, b)

            def block_values(s, b):
                pool.wait_ge(vw_ps, b + FOLD[s] * B + 1)
                tt(heads(VBD_at[b % 2]), vT_s[:, b * KEYS:(b + 1) * KEYS].unsqueeze(1).to_broadcast([P, H, KEYS]),
                   over_keys(w("hm")), ALU.mult).then_inc(vbd, 1)

            def values_and_roots(s):
                starts(pool, s)
                if s == X1:
                    for r in range(KV1):
                        root(ROUND0[X1] - KV1 + r, r)
                    pool.wait_ge(turned_sb, TURN0[X1] + 1)
                else:
                    pool.wait_ge(kv_sb, KV_SB0[s] + 2)
                for b in range(2):
                    block_values(s, b)
                roots(s)
                for b in range(2, B):
                    block_values(s, b)

            def cross(s):
                n0 = tiles_before(s)

                def normalize(t):
                    pool.wait_ge(recip, t.n + n0 + 1)
                    p = heads(att[:, 2 + t.slot(2), :])
                    tt(p, p, over_keys(ri[:, t.slot(2), :]), ALU.mult).then_inc(probs, 1)
                skewed_loop(pool, [(normalize, 0)], NT, TB)

            pool.wait_ge(ld["a"], 16)
            values_and_roots(X0)
            cross(X0)
            pool.wait_ge(ld["m1"], 16)
            pool.tensor_scalar(C[:, 0:NT * KEYS], mask_u8[:, :], 1.0e9, -1.0e9, ALU.mult, ALU.add).then_inc(mneg_set, 1)
            roots(F0)
            values_and_roots(X1)
            roots(X1, 1)
            cross(X1)
            roots(F1)
            roots(X2)
            cross(X2)
            starts(pool, MLA)
            pool.memset(VP[:, :, :, 0, HD:VE], 1.0).then_inc(ones_set, 1)
            pool.memset(VP[:, :, :, 1:PIECES, HD:VE], 0.0).then_inc(ones_set, 1)
            roots(MLA)
            roots(MLA, 1)
            pool.wait_ge(mla_sb, 3 * B)
            pool.wait_ge(v_split, B)
            with pool.Fori(0, B) as b:
                def keys_of_head(t):
                    n = b * H + t.n
                    pool.wait_ge(m_scores, n * 4 + 4)
                    tt(kh[:, t.slot(2), :], KT[:, cols(b)], w("hm")[:, bass.ds(t.n, 1)].to_broadcast([P, S]), ALU.mult)\
                        .then_inc(head_k, 1)
                skewed_loop(pool, [(keys_of_head, 0)], H, 2)
            starts(pool, MOE)
            pool.wait_ge(ld["m3"], 16)
            for b in range(B):
                t = pool.tensor_scalar(heads(nb3[:, b, :]),
                                       mask3_u8[:, b * KEYS:(b + 1) * KEYS].unsqueeze(1).to_broadcast([P, H, KEYS]),
                                       -NEG, NEG, ALU.mult, ALU.add)
            t.then_inc(nb_set, 1)
            roots(MOE)
            values_and_roots(X3)
            cross(X3)
            roots(F3)

        @block.vector
        def _(dve):
            v = nc.vector
            tt, ts, stt = v.tensor_tensor, v.tensor_scalar, v.scalar_tensor_tensor

            def moments(n, src, b, rms=None, rows=P):
                for i in range(TB):
                    v.bn_stats(stats[0:rows, b * TB + i, :], src(i)).then_inc(s_stats, 1)
                dve.wait_ge(s_stats, TB * (n + 1))
                for i in range(TB):
                    v.bn_aggr(mv[0:rows, b * TB + i, :], stats[0:rows, b * TB + i, :]).then_inc(s_aggr, 1)
                dve.wait_ge(s_aggr, TB * (n + 1))
                at = slice(b * TB, (b + 1) * TB)
                mean, var = mv[0:rows, at, 0], mv[0:rows, at, 1]
                if rms is not None:
                    tt(msq[0:rows, at], mean, mean, ALU.mult).then_inc(scratch, 1)
                    dve.wait_ge(scratch, rms)
                    stt(ve[0:rows, at], msq[0:rows, at], RMS_EPS, var, ALU.add, ALU.add).then_inc(s_ve, 1)
                else:
                    ts(ve[0:rows, at], var, LN_EPS, None, ALU.add).then_inc(s_ve, 1)

            def normed(n, n_turn, src, dst, b, rms=False, rows=P):
                dve.wait_ge(s_rstd, n + 1)
                if n_turn is not None:
                    wait(dve, turned, n_turn)
                for i in range(TB):
                    k = b * TB + i
                    if rms:
                        ts(dst(i), src(i), rstd[0:rows, k:k + 1], None, ALU.mult).then_inc(s_xn, 1)
                    else:
                        ts(dst(i), src(i), mv[0:rows, k, 0:1], rstd[0:rows, k:k + 1], ALU.subtract, ALU.mult)\
                            .then_inc(s_xn, 1)

            def xn_of(nth, rows=P):
                return lambda i: xn_at[nth % 2][0:rows, i, :]

            def rows_of(t, b):
                return lambda i: t[:, b * TB + i, :]

            def norm_x(s):
                for b in range(B):
                    moments(ROUND0[s] + b, rows_of(x, b), b)
                for b in range(B):
                    normed(ROUND0[s] + b, TURN0[s] + b, rows_of(x, b), xn_of(TURN0[s] + b), b)

            def norm_y(s, n, rms0):
                for b in range(B):
                    moments(n + b, rows_of(y, b), b, rms=rms0 + b + 1)
                for b in range(B):
                    normed(n + b, TURN0[s] + b, rows_of(y, b), xn_of(TURN0[s] + b), b, rms=True)

            def row(t, b, i):
                return t[:, tok(b, i), :].rearrange("p t d -> p (t d)")

            def block_keys(s):
                starts(dve, s)
                dst = KBD[:, :, :].rearrange("p b (h k) -> p b h k", k=KEYS)
                if s == X1:
                    dve.wait_ge(turned_sb, TURN0[X1])
                elif s == X0:
                    dve.wait_ge(kv_sb, 1)
                for b in range(B):
                    t = tt(dst[:, b], kT_s[:, b * KEYS:(b + 1) * KEYS].unsqueeze(1).to_broadcast([P, H, KEYS]),
                           over_keys(w("hm")), ALU.mult)
                t.then_inc(kbd, 1)

            def add_output_bias(s, n):
                if s == X2:
                    dve.wait_ge(fold_act, 3 * H // 2 + B)
                else:
                    dve.wait_ge(vw_sb, (FOLD[s] + 1) * B + 1)
                tt(VW[:, :, 0, :], VW[:, :, 0, :], w(f"{LAYER[s]}bo").unsqueeze(1).to_broadcast([P, B, D]), ALU.add)\
                    .then_inc(vw_bo, 1)

            def cross(s):
                n0 = tiles_before(s)

                def shift(t):
                    a = heads(att[:, t.slot(2), :])
                    dve.wait_ge(scores, t.n + n0 + 3)
                    dve.wait_ge(expd, t.n + n0 + 1)
                    src = heads(flat[:, 0:HK])
                    if s == X1:
                        m = mneg[:, bass.ds(t.n, 1), :].to_broadcast([P, H, KEYS])
                        stt(a, src, HD ** -0.5, m, ALU.mult, ALU.add).then_inc(scores_read, 1)
                    if s == X2:
                        tt(att[:, t.slot(2), :], flat[:, 0:HK], batch(C[:, :].rearrange("p (b n) -> p b n", b=B), t.group), ALU.add)\
                            .then_inc(scores_read, 1)
                    if s in (X1, X2):
                        src = a
                        dve.wait_ge(scores_read, t.n + (LAYER[s] - 1) * NT + 2)
                    v.tensor_reduce(mx[:, t.slot(2), :], src, AX.X, ALU.max).then_inc(rowmax, 1)
                    dve.wait_ge(rowmax, t.n + n0 + 1)
                    tt(a, src, over_keys(mx[:, t.slot(2), :]), ALU.subtract).then_inc(shifted, 1)

                def total(t):
                    dve.wait_ge(expd, t.n + n0 + 3)
                    v.tensor_reduce(rs[:, t.slot(2), :], heads(att[:, 2 + t.slot(2), :]), AX.X, ALU.add)\
                        .then_inc(rowsum, 1)
                    dve.wait_ge(rowsum, t.n + n0 + 1)
                    dve.wait_ge(probs, t.n + n0 + 1)
                    v.reciprocal(ri[:, t.slot(2), :], rs[:, t.slot(2), :]).then_inc(recip, 1)

                def update(t):
                    dve.wait_ge(attn_out, t.n + n0 + 3)
                    xt = x[:, bass.ds(t.n, 1), :].rearrange("p t d -> p (t d)")
                    stt(xt, ps[:, 6 + t.slot(2), 0:D], tg[:, LAYER[s]:LAYER[s] + 1], xt, ALU.mult, ALU.add)\
                        .then_inc(x_new, 1)

                skewed_loop(dve, [(shift, 0), (total, 1), (update, 3)], NT, TB)

            def gate(s, n, base, tanh):
                c = Chain(dve, gate_chain, base)
                g = lambda k: G[:, k, :, :]
                one = lambda k: G[:, 3, :, k:k + 1]
                wide_ = lambda a: a.to_broadcast([P, NT, E])
                desc = w("desc").unsqueeze(1).to_broadcast([P, NT, E])
                lg = ps[:, 6, 0:NT * E].rearrange("p (i e) -> p i e", e=E)
                dve.wait_ge(router_ps, (n + 1) * B)

                def first_largest(src, k, m, m2):
                    c.link(v.tensor_reduce(one(m), src, AX.X, ALU.max))
                    c.link(tt(g(k), src, wide_(one(m)), ALU.subtract))
                    c.link(stt(g(k + 1), g(k), 0.0, desc, ALU.is_ge, ALU.mult))
                    c.link(v.tensor_reduce(one(m2), g(k + 1), AX.X, ALU.max))
                    c.link(tt(g(k + 1), g(k + 1), wide_(one(m2)), ALU.is_equal))
                    return g(k + 1)

                if s == F0:
                    c.link(tt(g(0), lg, w("0rb").unsqueeze(1).to_broadcast([P, NT, E]), ALU.add))
                    c.link(v.tensor_reduce(one(0), g(0), AX.X, ALU.max))
                    c.link(tt(g(1), g(0), wide_(one(0)), ALU.subtract))
                    c.link(stt(g(5), g(1), 0.0, desc, ALU.is_ge, ALU.mult))
                    c.link(v.tensor_reduce(one(1), g(5), AX.X, ALU.max))
                    c.link(tt(g(5), g(5), wide_(one(1)), ALU.is_equal))
                    dve.wait_ge(exp_gate, n + 1)
                    c.link(v.tensor_reduce(one(2), g(2), AX.X, ALU.add))
                    c.link(v.reciprocal(one(3), one(2)))
                    stt(w_all[:, :, :], g(5), tanh, wide_(one(3)), ALU.mult, ALU.mult).then_inc(w_ready, 1)
                    dve.wait_ge(w_ready, n + 1)
                    assert c.k == TOP1, c.k
                    return
                c.link(v.tensor_copy(g(0), lg))
                oh1 = first_largest(g(0), 4, 0, 1)
                c.link(stt(g(6), oh1, NEG, g(0), ALU.mult, ALU.add))
                c.link(v.tensor_reduce(one(2), g(6), AX.X, ALU.max))
                c.link(tt(g(7), g(6), wide_(one(2)), ALU.subtract))
                c.link(stt(g(8), g(7), 0.0, desc, ALU.is_ge, ALU.mult))
                c.link(v.tensor_reduce(one(3), g(8), AX.X, ALU.max))
                c.link(tt(G[:, 10, :, 0:1], one(2), one(0), ALU.subtract))
                c.link(tt(g(8), g(8), wide_(one(3)), ALU.is_equal))
                dve.wait_ge(exp_gate, n + 1)
                ex = G[:, 11, :, 0:1]
                c.link(ts(one(4), ex, 1.0, None, ALU.add))
                c.link(v.reciprocal(one(5), one(4)))
                if tanh is not None:
                    c.link(ts(one(5), one(5), tanh, None, ALU.mult))
                c.link(tt(one(6), ex, one(5), ALU.mult))
                c.link(tt(g(7), oh1, wide_(one(5)), ALU.mult))
                c.link(tt(g(8), g(8), wide_(one(6)), ALU.mult))
                tt(w_all[:, :, :], g(7), g(8), ALU.add).then_inc(w_ready, 1)
                dve.wait_ge(w_ready, n + 1)
                assert c.k == (TOP2 if s == F1 else TOP2N), c.k

            def add_weighted_bias(n):
                for b in range(B):
                    dve.wait_ge(wb_ps, n * B + b + 1)
                    xb = x[:, tok(b, 0, TB), :]
                    tt(xb, xb, ps[:, 2 + b, :].rearrange("p (i d) -> p i d", d=D), ALU.add).then_inc(x_new, 1)

            def experts(s, J, acc):
                units = E * J
                u0 = UNIT0[s]
                x0 = XNEW0[s] + (B if s == F1 else 0)
                w0 = 0 if s == F1 else B
                dve.wait_ge(w_ready, 3 if s == MOE else 2)
                with dve.Fori(0, B) as c:
                    dve.wait_ge(x_new, c * (E * TB) + x0)
                    v.tensor_copy(w_c[:, :, :], w_all[:, tok(c, 0, TB), :]).then_inc(scratch_w, 1)
                    dve.wait_ge(scratch_w, c + w0 + 1)

                    def gate_unit(u):
                        e, j = divmod(u, J)
                        dve.wait_ge(silu, c * units + u0 + u + 1)
                        dve.wait_ge(down_ps, c * units + u0 + u + 1)
                        stt(hh[:, u % 2, :], ps[:, 2 + u % 2, :], bgi[:, 1, e, j:j + 1], sg[:, u % 2, :],
                            ALU.add, ALU.mult).then_inc(gated, 1)

                    def add_expert(e):
                        dve.wait_ge(down_ps, c * units + u0 + (e + 1) * J + 2)
                        if e >= 1:
                            dve.wait_ge(x_new, (c * E + e) * TB + x0)
                        for i in range(TB):
                            a = row(acc, c, i)
                            stt(a, ps[:, 4 + e % 2, i * D:(i + 1) * D], w_c[:, i, e:e + 1], a, ALU.mult, ALU.add)\
                                .then_inc(x_new, 1)
                    for e in range(E):
                        for j in range(J):
                            if s == F1:
                                gate_unit(e * J + j)
                            if j == 0 and e > 0:
                                add_expert(e - 1)
                    add_expert(E - 1)

            dve.wait_ge(ld["a"], 16)
            v.tensor_copy(identb[:, :], w("ident")).then_inc(bf_done, 1)
            dve.wait_ge(ld["x"], 16)
            norm_x(X0)
            block_keys(X0)
            add_output_bias(X0, 1)
            dve.wait_ge(tanh_done, 1)
            cross(X0)

            starts(dve, F0)
            dve.wait_ge(ld["b"], 16)
            norm_x(F0)
            gate(F0, 0, 0, tg[:, 4:5])
            add_weighted_bias(0)

            def weigh_experts(t):
                dve.wait_ge(e0_ps, t.n + 3)
                dve.wait_ge(e0_summed, t.n + 1)
                ys = flat[:, 6 * BANK * t.slot(2):(6 * t.slot(2) + 2) * BANK].rearrange("p (e d) -> p e d", d=D)
                wt = w_all[:, bass.ds(t.n, 1), :].rearrange("p t e -> p (t e)").unsqueeze(2).to_broadcast([P, E, D])
                tt(wide[:, t.slot(2)], ys, wt, ALU.mult).then_inc(e0_read, 1)

            def sum_experts(t):
                dve.wait_ge(e0_read, t.n + 3)
                dve.wait_ge(x_new, t.n + XNEW0[F0] + B - 1)
                v.tensor_reduce(hsum[:, t.slot(2), :], wide[:, t.slot(2)].rearrange("p e d -> p d e"), AX.X, ALU.add)\
                    .then_inc(e0_summed, 1)

            def add_experts(t):
                dve.wait_ge(e0_summed, t.n + 3)
                xt = x[:, bass.ds(t.n, 1), :].rearrange("p t d -> p (t d)")
                tt(xt, xt, hsum[:, t.slot(2), :], ALU.add).then_inc(x_new, 1)
            dve.wait_ge(x_new, XNEW0[F0] + B)
            skewed_loop(dve, [(weigh_experts, 0), (sum_experts, 1), (add_experts, 2)], NT, TB)

            starts(dve, X1)
            dve.wait_ge(kv_ps, KV_PS0[X1] + 1)
            kv = [lambda i, r=r: ps[0:KEYS, i // 2, (2 * (i % 2) + r) * D:(2 * (i % 2) + r + 1) * D] for r in range(KV1)]
            n0, t0 = ROUND0[X1], TURN0[X1]
            for r in range(KV1):
                moments(n0 - KV1 + r, kv[r], r, rows=KEYS)
            for r in range(KV1):
                normed(n0 - KV1 + r, t0 - KV1 + r, kv[r], xn_of(t0 - KV1 + r, KEYS), r, rows=KEYS)
            dve.wait_ge(s_xn, TB * n0)
            norm_x(X1)
            block_keys(X1)
            for b in range(B):
                dve.wait_ge(q_ps, b + B + 1)
                moments(n0 + B + b, lambda i: ps[:, 3 + b, i * D:(i + 1) * D], b)
            for b in range(B):
                normed(n0 + B + b, t0 + B + b, lambda i: ps[:, 3 + b, i * D:(i + 1) * D], xn_of(t0 + B + b), b)
            dve.wait_ge(mneg_set, 1)
            cross(X1)

            starts(dve, F1)
            norm_x(F1)
            gate(F1, 1, TOP1, tg[:, 5:6])
            add_weighted_bias(1)
            dve.wait_ge(ld["bgi"], 16)
            experts(F1, J1, x)

            starts(dve, X2)
            for b in range(B):
                moments(ROUND0[X2] + b, rows_of(x, b), b)
            dve.wait_ge(ld["c"], 16)
            for u in range(1, 3 * H, 2):
                dve.wait_ge(fold_ps, u + 1)
                v.tensor_copy(folded(u), ps[:, u % 6, 0:CK].rearrange("p (b k) -> p b k", k=KEYS)).then_inc(fold_dve, 1)
            dve.wait_ge(ld["d"], 16)
            v.tensor_copy(heads(cmaskb[:, :]), w("2cm").unsqueeze(1).to_broadcast([P, H, KEYS])).then_inc(bf_done, 1)
            v.tensor_copy(diagb[:, :], w("mcm")).then_inc(bf_done, 1)
            for b in range(B):
                normed(ROUND0[X2] + b, TURN0[X2] + b, rows_of(x, b), xn_of(TURN0[X2] + b), b)
            add_output_bias(X2, 2)
            dve.wait_ge(fold_dve, 3 * H // 2)
            cross(X2)

            starts(dve, MLA)
            n0 = ROUND0[MLA]
            for b in range(B):
                moments(n0 + b, rows_of(x, b), b)
            for b in range(B):
                normed(n0 + b, None, rows_of(x, b), rows_of(y, b), b)
            dve.wait_ge(s_xn, TB * (n0 + B))
            norm_y(MLA, n0 + B, 0)

            c = Chain(dve, v_chain)
            for b in range(B):
                dve.wait_ge(mla_ps, b * 4 + 4)
                heads_of = lambda a: a.rearrange("p (t h d) -> p t h d", h=H, d=HD)
                piece = lambda k: VP[:, b * TB:(b + 1) * TB, :, k, 0:HD]
                c.link(v.tensor_copy(piece(0), heads_of(ps[:, b, :])))
                c.link(tt(heads_of(v_rest), heads_of(ps[:, b, :]), piece(0), ALU.subtract))
                c.link(v.tensor_copy(piece(1), heads_of(v_rest)))
                tt(piece(2), heads_of(v_rest), piece(1), ALU.subtract).then_inc(v_split, 1)
                dve.wait_ge(v_split, b + 1)
            with dve.Fori(0, B) as b:
                def maxima(t):
                    n = b * H + t.n
                    for i in range(TB):
                        dve.wait_ge(m_scores, n * 4 + i + 9)
                        v.tensor_reduce(negm[:, t.slot(2), i:i + 1], ps[:, i, 0:(i + 1) * P], AX.X, ALU.max, negate=True)\
                            .then_inc(m_rowmax, 1)

                def low_half(t):
                    n = b * H + t.n
                    for k in range(3):
                        dve.wait_ge(m_high, n * 3 + k + 1)
                        m = min(4, len(BLOCKS) - 4 * k)
                        high, low = (PH[:, t.slot(2), half, 4 * k:4 * k + m, :].rearrange("p c n -> p (c n)")
                                     for half in range(2))
                        stt(low, ps[:, 4 + k, 0:m * P], PSCALE, high, ALU.mult, ALU.subtract).then_inc(m_probsT, 1)

                def divide(t):
                    n = b * H + t.n
                    dve.wait_ge(m_attn, n + 3)
                    dve.wait_ge(m_normed, n + 1)
                    o = ps[:, 7, 0:TB * PIECES * VE].rearrange("p (i c d) -> p i d c", c=PIECES, d=VE)
                    v.tensor_reduce(o_sum[:, :, :], o, AX.X, ALU.add).then_inc(m_summed, 1)
                    dve.wait_ge(m_summed, n + 2)
                    v.reciprocal(rec[:, :].unsqueeze(2), o_sum[:, :, HD:VE]).then_inc(m_rec, 1)
                    dve.wait_ge(m_rec, n + 1)
                    tt(o_s[:, :, bass.ds(t.n * HD, HD)], o_sum[:, :, 0:HD],
                       rec[:, :].unsqueeze(2).to_broadcast([P, TB, HD]), ALU.mult).then_inc(m_normed, 1)
                skewed_loop(dve, [(divide, 3), (maxima, 0), (low_half, 1)], H, 2)
                dve.wait_ge(yo_ps, b + 1)
                yb = y[:, tok(b, 0, TB), :]
                tt(yb, yb, ps[:, 5, :].rearrange("p (i d) -> p i d", d=D), ALU.add).then_inc(x_new, 1)

            starts(dve, MOE)
            norm_y(MOE, ROUND0[MOE], B)
            gate(MOE, 2, TOP1 + TOP2, None)
            experts(MOE, J2, y)

            starts(dve, X3)
            dve.wait_ge(ld["e"], 16)
            dve.wait_ge(ld["m3"], 16)
            dve.wait_ge(ld["rope"], 16)
            dve.wait_ge(kv_ps, KV_PS0[X3] + 3)
            c = Chain(dve, kv_chain)
            perb = lambda a: a.rearrange("p (b k) -> p b k", k=KEYS)
            table = lambda a: a[:, 0:KEYS].unsqueeze(1).to_broadcast([P, B, KEYS])
            c.link(v.tensor_copy(mask3_f[:, :], mask3_u8[:, :]))
            c.link(tt(perb(kA_s), perb(kT_s), table(cosT), ALU.mult))
            c.link(tt(perb(kB_s), perb(ps[:, 2, 0:CK]), table(sinT), ALU.mult))
            c.link(tt(kA_s, kA_s, kB_s, ALU.add))
            c.link(tt(kT_s, kA_s, mask3_f[:, :], ALU.mult))
            for b in range(B):
                xb, yb = x[:, tok(b, 0, TB), :], y[:, tok(b, 0, TB), :]
                stt(xb, yb, tg[:, 6:7], xb, ALU.mult, ALU.add).then_inc(x_new, 1)
            dve.wait_ge(x_new, XNEW0[X3] + B)
            norm_x(X3)
            block_keys(X3)
            c = Chain(dve, rope_chain)
            for b in range(B):
                dve.wait_ge(rot_ps, b + 1)
                c.link(tt(rope_a, FT[:, cols(b)], cosT, ALU.mult))
                c.link(tt(rope_b, ps[:, 3 + b % 3, :], sinT, ALU.mult))
                tt(FT[:, cols(b)], rope_a, rope_b, ALU.add).then_inc(roped, 1)
                dve.wait_ge(roped, b + 1)
            add_output_bias(X3, 3)
            cross(X3)

            starts(dve, F3)
            ts(bo3[:, :], w("3fbo"), 0.3, None, ALU.mult).then_inc(y_set, 1)
            dve.wait_ge(y_set, 1)
            for b in range(B):
                moments(ROUND0[F3] + b, rows_of(x, b), b)
            for b in range(B):
                dve.wait_ge(y_set, max(b, 1))
                nth = TURN0[F3] + b
                normed(ROUND0[F3] + b, nth, rows_of(x, b), xn_of(nth), b)
                dve.wait_ge(s_xn, TB * (ROUND0[F3] + b + 1))
                tt(y[:, b * TB:(b + 1) * TB, :], xn_at[nth % 2][:, :, :],
                   bo3[:, :].unsqueeze(1).to_broadcast([P, TB, D]), ALU.add).then_inc(y_set, 1)
            dve.wait_ge(y_set, B + 1)
            dve.wait_ge(pol, 2)
            c = Chain(dve, sel_chain)
            lg = ps[:, 7, 0:B * E].rearrange("p (b e) -> p b e", e=E)
            of = lambda a: a.unsqueeze(1).to_broadcast([P, B, E])
            one = lambda k: G3[:, 3, :, k:k + 1]
            c.link(tt(G3[:, 0, :, :], lg, of(w("bp2")), ALU.add))
            c.link(v.tensor_reduce(one(0), G3[:, 0, :, :], AX.X, ALU.max))
            c.link(tt(G3[:, 1, :, :], G3[:, 0, :, :], one(0).to_broadcast([P, B, E]), ALU.subtract))
            c.link(stt(G3[:, 5, :, :], G3[:, 1, :, :], 0.0, of(w("desc")), ALU.is_ge, ALU.mult))
            c.link(v.tensor_reduce(one(1), G3[:, 5, :, :], AX.X, ALU.max))
            c.link(tt(m4[:, :, :], G3[:, 5, :, :], one(1).to_broadcast([P, B, E]), ALU.is_equal))
            dve.wait_ge(ld["f3"], 16)

            def select(t):
                wait(dve, r3_ps, t.n - 1)
                wait(dve, r3_sb, t.n - 1)
                d = sel[:, t.slot(2), :]
                for e in range(E):
                    m = m4[:, t.n, e:e + 1]
                    if e == 0:
                        ins = ts(d, W3F[:, e, :], m, None, ALU.mult)
                    else:
                        ins = stt(d, W3F[:, e, :], m, d, ALU.mult, ALU.add)
                    if e < E - 1:
                        c.link(ins)
                ins.then_inc(sel_done, 1)

            def finish(t):
                dve.wait_ge(o3_ps, t.n + 1)
                xb, yb = x[:, t.n * TB:(t.n + 1) * TB, :], y[:, t.n * TB:(t.n + 1) * TB, :]
                c.link(stt(yb, ps[:, 3, :].rearrange("p (i d) -> p i d", d=D), 0.3, yb, ALU.mult, ALU.add))
                stt(xb, yb, tg[:, 7:8], xb, ALU.mult, ALU.add).then_inc(x_new, 1)
            skewed_loop(dve, [(select, 0), (finish, 1)], B, 2)


def _columns(v):
    return v.reshape(-1, P).T


def _rows(v, n=P):
    out = np.zeros((P, v.size), v.dtype)
    out[:n] = v
    return out


def _pad(a):
    out = np.zeros((P, a.shape[1]), a.dtype)
    out[:a.shape[0]] = a
    return out


def _pack(i):
    f = np.float32
    ident = np.eye(P, dtype=f)
    rot = np.zeros((P, P), f)
    for k in range(0, P, 2):
        rot[k + 1, k] = -1.0
        rot[k, k + 1] = 1.0
    causal = np.where(np.arange(KEYS)[None, :] > np.arange(P)[:, None], f(-1e30), f(0)).astype(f)
    diag = np.where(np.arange(P)[None, :] > np.arange(P)[:, None], f(-1e30), f(0)).astype(f)
    two = lambda a: a.reshape(8, P, D).transpose(1, 0, 2).reshape(P, 8 * D)
    v = {
        "ident": ident,
        "hm": (np.arange(P)[:, None] // HD == np.arange(H)[None, :]).astype(f),
        "desc": np.tile(np.arange(E, 0, -1, dtype=f), (P, 1)),
        "gates": _rows(np.concatenate([i["g_xattn"], i["g_ffn"]])),
        "ctxT": i["ctx_1024"].reshape(CK, D).T,
        "0wq": i["L0_xattn_Wq"].T, "0wk": i["L0_xattn_Wk"].T, "0wv": i["L0_xattn_Wv"].T, "0wo": i["L0_xattn_Wo"].T,
        "0b": np.stack([i["L0_xattn_bq"], i["L0_xattn_bk"], i["L0_xattn_bv"]], 1),
        "0bo": _rows(i["L0_xattn_bo"], KEYS),
        "0we": i["L0_ffn_expert_w"].transpose(1, 0, 2).reshape(P, E * D),
        "0eb": _pad(i["L0_ffn_expert_b"]), "0rw": i["L0_ffn_router_w"], "0rb": _rows(i["L0_ffn_router_b"]),
        "1wq": i["L1_xattn_Wq"], "1wkv": np.concatenate([i["L1_xattn_Wk"], i["L1_xattn_Wv"]], 1),
        "1gb": np.stack([i["L1_xattn_" + k] for k in ("gq", "bq", "gk", "bk", "gv", "bv")], 1),
        "1gw": i["L1_ffn_gate_w"].T, "1bo": _pad(i["L1_ffn_bo"]),
        "2wqT": two(i["L2_xattn_Wq"].T), "2wk": i["L2_xattn_Wk"], "2wv": i["L2_xattn_Wv"], "2wo": two(i["L2_xattn_Wo"]),
        "2b": np.concatenate([_columns(i["L2_xattn_" + k]) for k in ("bq", "bk", "bv")], 1),
        "2bo": _rows(i["L2_xattn_bo"], KEYS), "2cm": causal,
        "mwq": i["L2_ffn_Wq"], "mwd": i["L2_ffn_Wdkv"], "mwuk": _pad(i["L2_ffn_Wuk"]), "mwuv": _pad(i["L2_ffn_Wuv"]),
        "mwo": i["L2_ffn_Wo"], "mg": np.stack([i["L2_ffn_g1"], i["L2_ffn_g2"]], 1), "mgw": i["L2_ffn_gate_w"],
        "mcm": diag,
        "3wq": i["L3_xattn_w_q"], "3wk": i["L3_xattn_w_k"], "3wv": i["L3_xattn_w_v"], "3wo": i["L3_xattn_w_o"],
        "3b": np.stack([i["L3_xattn_b_q"], i["L3_xattn_b_k"], i["L3_xattn_b_v"]], 1),
        "3bo": _rows(i["L3_xattn_b_o"], KEYS), "rot": rot,
        "wp1": i["L3_ffn_Wp1"], "bp1": i["L3_ffn_bp1"][:, None], "wp2": i["L3_ffn_Wp2"], "bp2": _rows(i["L3_ffn_bp2"]),
        "3fwo": i["L3_ffn_Wo"], "3fbo": _rows(i["L3_ffn_bo"]),
    }
    order = [n for items in GROUPS.values() for n, _ in items]
    for n in order:
        assert v[n].shape == (P, PLACE[n][1]), (n, v[n].shape)
    return np.ascontiguousarray(np.concatenate([v[n] for n in order], 1))


def _rope():
    f = np.float32
    inv = (f(10000.0) ** (np.arange(0, HD, 2, dtype=f) / f(HD))).astype(f)
    theta = (np.arange(S, dtype=f)[:, None] / inv).astype(f)
    theta = np.tile(np.repeat(theta, 2, axis=1), (1, H)).T
    return np.ascontiguousarray(np.concatenate([np.cos(theta), np.sin(theta)], 1).astype(f))


def kernel(**inputs):
    import concourse.bacc as _bacc
    from concourse.bass_utils import run_bass_kernel_spmd as _run

    i = {k: np.asarray(a) for k, a in inputs.items()}

    def up(a):
        return a.transpose(2, 0, 1).reshape(D, -1)

    def down(a):
        e, h, d = a.shape
        return a.reshape(e, h // P, P, d).transpose(2, 0, 1, 3).reshape(P, -1)

    def cols_of(a):
        e, h = a.shape
        return a.reshape(e, h // P, P).transpose(2, 0, 1)

    arrays = {
        "x": i["x"].reshape(B * S, D),
        "packed": _pack(i),
        "ffn1": np.concatenate([up(i["L1_ffn_wg"]), up(i["L1_ffn_wi"]), down(i["L1_ffn_wo"].transpose(0, 2, 1)),
                                cols_of(i["L1_ffn_bg"]).reshape(P, -1), cols_of(i["L1_ffn_bi"]).reshape(P, -1)], 1),
        "moe": np.concatenate([i["L2_ffn_w1"].transpose(1, 0, 2).reshape(D, -1), down(i["L2_ffn_w2"])], 1),
        "ffn3": np.concatenate([i["L3_ffn_W1"].transpose(1, 0, 2), cols_of(i["L3_ffn_b1"]),
                                down(i["L3_ffn_W2"]).reshape(P, E, J2 * D), i["L3_ffn_b2"].T[:, :, None]],
                               2).reshape(P, -1),
        "rope": _rope(),
        "mask1": np.ascontiguousarray(i["mask_BxSxS2_bk0"]).reshape(-1).view(np.uint32),
        "mask3": np.ascontiguousarray(np.broadcast_to(i["mask_Bx1x1xS2_bf1"].reshape(1, CK), (P, CK))).view(np.uint8),
    }
    arrays = {f"in_{k}": np.ascontiguousarray(a) for k, a in arrays.items()}
    nc = _bacc.Bacc("TRN2", target_bir_lowering=False, num_devices=1)
    args = {k: nc.dram_tensor(k, a.shape, mybir.dt.from_np(a.dtype), kind="ExternalInput").ap()
            for k, a in arrays.items()}
    out = nc.dram_tensor("out_x", (B * S, D), F32, kind="ExternalOutput").ap()
    build(nc, args["in_x"], args["in_packed"], args["in_ffn1"], args["in_moe"], args["in_ffn3"], args["in_rope"],
          args["in_mask1"], args["in_mask3"], out)
    r = _run(nc, [arrays], core_ids=[0])
    return r.results[0]["out_x"].reshape(B, S, D)
```

```python
import numpy as np
import concourse.bass as bass
from concourse import mybir
from contextlib import ExitStack

F32 = mybir.dt.float32
BF16 = mybir.dt.bfloat16
F16 = mybir.dt.float16
I32 = mybir.dt.int32
U8 = mybir.dt.uint8
ALU = mybir.AluOpType
ACT = mybir.ActivationFunctionType
AX = mybir.AxisListType

B, S, D = 4, 512, 128
KEYS = 77
H, HD = 16, 8
HD2 = 64
P = 128
TB = S // P
NT = B * TB
HK = H * KEYS
CK = B * KEYS
NC = -(-HK // P)
LAST = HK - (NC - 1) * P
E = 8
HID1 = 512
HID2 = 256
J1, J2 = HID1 // P, HID2 // P
LAT = 64
VE = HD + 1
PIECES = 3
PSCALE = 1024.0
BANK = 512
NEG = -3.0e38
SEL = HID2 + J2 + J2 * D + 1
TOP1, TOP2, TOP2N = 8, 19, 18
LN_EPS, RMS_EPS = 1e-5, 1e-6

X0, F0, X1, F1, X2, MLA, MOE, X3, F3 = range(9)
KV1 = 2
ROUNDS = {X0: 1, F0: 1, X1: 2, F1: 1, X2: 1, MLA: 2, MOE: 1, X3: 1, F3: 1}
TURNED = {X0: 1, F0: 1, X1: 2, F1: 1, X2: 1, MLA: 1, MOE: 1, X3: 1, F3: 1}


def before(table, s, kv):
    return sum(B * table[i] for i in range(s)) + (kv if s > X1 else 0)


ROUND0 = {s: before(ROUNDS, s, KV1) + (KV1 if s == X1 else 0) for s in range(9)}
TURN0 = {s: before(TURNED, s, KV1) + (KV1 if s == X1 else 0) for s in range(9)}
X_NEW = {X0: NT, F0: B + NT, X1: NT, F1: B + NT * E, X2: NT, MLA: B, MOE: NT * E, X3: B + NT, F3: B}
XNEW0 = {s: 2 + sum(X_NEW[i] for i in range(s)) for s in range(10)}
LAYER = {X0: 0, X1: 1, X2: 2, X3: 3}
KV_PS0 = {X0: 0, X1: 2, X2: 3, X3: 3 + H}
KV_SB0 = {X0: 0, X2: 2, X3: 2 + H}
FOLD = {X0: 0, X1: 1, X3: 2}
WARM = {F1: 10, MLA: 18, MOE: 10, F3: 10}
WARM_FOLD = 4
EARLY = 3
UNIT0 = {F1: 0, MOE: B * E * J1}
BLOCKS = [(i, j) for i in range(TB) for j in range(i + 1)]


class Tile:

    def __init__(self, g, u, k):
        self.k = k
        self.n = k if g is None else g * u + k
        self.group = k // TB if g is None else (g + k // TB if u == TB else None)

    def slot(self, m):
        return self.k % m


def skewed_loop(eng, steps, total, unroll):
    deep = max(lag for _, lag in steps)
    turns = (total - deep) // unroll
    t = 0
    while t < total + deep:
        if t == deep and turns > 1:
            with eng.Fori(0, turns) as g:
                for i in range(unroll):
                    for f, lag in steps:
                        f(Tile(g, unroll, t + i - lag))
            t += turns * unroll
        else:
            for f, lag in steps:
                if 0 <= t - lag < total:
                    f(Tile(None, unroll, t - lag))
            t += 1


class Chain:

    def __init__(self, eng, sem, base=0):
        self.eng, self.sem, self.base, self.k = eng, sem, base, 0

    def link(self, ins):
        self.k += 1
        ins.then_inc(self.sem, 1)
        self.eng.wait_ge(self.sem, self.base + self.k)


GROUPS = {
    "a": [("ident", P), ("hm", H), ("desc", E), ("gates", 8), ("ctxT", CK),
          ("0wq", D), ("0wk", D), ("0wv", D), ("0wo", D), ("0b", 3), ("0bo", D)],
    "b": [("0we", E * D), ("0eb", D), ("0rw", E), ("0rb", E),
          ("1wq", D), ("1wkv", 2 * D), ("1gb", 6), ("1gw", E), ("1bo", D)],
    "c": [("2wqT", 8 * D), ("2wk", 8 * D), ("2wv", 8 * D), ("2wo", 8 * D), ("2b", 24), ("2bo", D), ("2cm", KEYS)],
    "d": [("mwq", D), ("mwd", LAT), ("mwuk", D), ("mwuv", D), ("mwo", D), ("mg", 2), ("mgw", E), ("mcm", P)],
    "e": [("3wq", D), ("3wk", D), ("3wv", D), ("3wo", D), ("3b", 3), ("3bo", D), ("rot", P),
          ("wp1", D), ("bp1", 1), ("wp2", E), ("bp2", E), ("3fwo", D), ("3fbo", D)],
}
PLACE = {}
WIDTH = {}
_at = 0
for _g, _items in GROUPS.items():
    _start = _at
    for _n, _w in _items:
        PLACE[_n] = (_at, _w)
        _at += _w
    WIDTH[_g] = (_start, _at)
PACKED = _at


def build(nc, x_in, packed, w_ffn1, w_moe, w_ffn3, rope, mask1, mask3, out):
    ctx = ExitStack()
    with ctx:
        def sb(name, shape, dt=F32):
            return ctx.enter_context(nc.sbuf_tensor(name, shape, dt))

        def sem(name):
            return ctx.enter_context(nc.semaphore(name))

        W = sb("W", [P, PACKED])

        def w(name, rows=P):
            a, n = PLACE[name]
            return W[0:rows, a:a + n]

        x = sb("x", [P, NT, D])
        FT = sb("FT", [P, B * S])
        xn_s = sb("xn_s", [P, TB, D])
        xnT_s = sb("xnT_s", [P, S])
        q1_s = sb("q1_s", [P, S])
        oT_s = (q1_s, xnT_s)
        qs = sb("qs", [P, 2, P])
        KBD = sb("KBD", [P, B, HK])
        VW = sb("VW", [P, B, NC, D])
        VBD = sb("VBD", [P, HK])
        att = sb("att", [P, 4, HK])
        PT = sb("PT", [P, 2, NC, P])
        C = sb("C", [P, B * HK])
        U = sb("U", [P, 3 * E * HID1])
        mask_u8 = sb("mask_u8", [P, NT * KEYS], U8)
        mask3_u8 = sb("mask3_u8", [P, CK], U8)
        bo3 = sb("bo3", [P, D])
        identb = sb("identb", [P, P], BF16)
        cmaskb = sb("cmaskb", [P, HK], BF16)
        diagb = sb("diagb", [P, P], BF16)
        tg = sb("tg", [P, 8])
        stats = sb("stats", [P, NT, 6])
        mv = sb("mv", [P, NT, 2])
        ve = sb("ve", [P, NT])
        msq = sb("msq", [P, NT])
        rstd = sb("rstd", [P, NT])
        rrms = sb("rrms", [P, NT])
        minus_half = sb("minus_half", [P, TB])
        mx = sb("mx", [P, 2, H])
        rs = sb("rs", [P, 2, H])
        ri = sb("ri", [P, 2, H])
        negm = sb("negm", [P, 2, TB])
        rec = sb("rec", [P, TB])
        o_sum = sb("o_sum", [P, TB, VE])
        w_all = sb("w_all", [P, NT, E])
        w_c = sb("w_c", [P, TB, E])
        G3 = sb("G3", [P, 6, B, E])
        hp_s = sb("hp_s", [P, B])
        chosen = sb("chosen", [P, B], I32)

        r_s = PT[:, 0, 0:TB, :]
        att_flat = att[:, :, :].rearrange("p a n -> p (a n)")
        wT_s = att_flat[0:E, 2 * HK:2 * HK + B * S].rearrange("e (i p) -> e i p", p=P)
        wT_c = PT[0:E, 0, 0:TB, :]
        G = att[:, :, :].rearrange("p a n -> p (a n)")[:, 0:12 * NT * E].rearrange("p (k t e) -> p k t e", k=12, e=E)
        xn_at = (xn_s, PT[:, 1, 4:8, :])
        VBD_at = (VBD[:, :], att[:, 3, :])
        mask3_f = att[:, 1, 0:CK]
        kT_s = att[:, 0, 0:CK]
        vT_s = PT[:, 0, 0:4, :].rearrange("p c n -> p (c n)")[:, 0:CK]
        kA_s = att[:, 0, 2 * CK:3 * CK]
        kB_s = att[:, 0, 3 * CK:4 * CK]
        kT2 = att[:, 0:2, :].rearrange("p a n -> p (a n)").rearrange("p (c n) -> p c n", n=CK)
        vT2 = att[:, 2:4, :].rearrange("p a n -> p (a n)").rearrange("p (c n) -> p c n", n=CK)
        VWT = U[:, 4096:4096 + B * HK].rearrange("p (b n) -> p b n", b=B)
        y = U[:, 9100:9100 + NT * D].rearrange("p (t d) -> p t d", d=D)
        cosT = U[:, 11264:11264 + S]
        sinT = U[:, 11264 + S:11264 + 2 * S]
        WG1 = U[:, 0:E * HID1].rearrange("p (e n) -> p e n", e=E)
        WI1 = U[:, E * HID1:2 * E * HID1].rearrange("p (e n) -> p e n", e=E)
        WO1 = U[:, 2 * E * HID1:3 * E * HID1].rearrange("p (e j d) -> p e j d", e=E, d=D)
        bgi = sb("bgi", [P, 2, E, J1])
        W1M = U[:, 0:E * HID2].rearrange("p (e n) -> p e n", e=E)
        W2M = U[:, E * HID2:2 * E * HID2].rearrange("p (e j d) -> p e j d", e=E, d=D)
        W3F = U[:, 4096:4096 + E * SEL].rearrange("p (e n) -> p e n", e=E)
        mneg = C[:, 0:NT * KEYS].rearrange("p (t k) -> p t k", k=KEYS)
        KT = C[:, 0:B * S]
        VP = KBD[:, :, :].rearrange("p b n -> p (b n)")[:, 0:NT * H * PIECES * VE // 2].bitcast(BF16)\
            .rearrange("p (t h c d) -> p t h c d", h=H, c=PIECES, d=VE)
        v_rest = PT[:, 0, 0:4, :].rearrange("p c n -> p (c n)")
        PH = PT[:, :, :, :].rearrange("p a c n -> p (a c n)").bitcast(F16)\
            .rearrange("p (a l c n) -> p a l c n", a=2, l=2, n=P)
        rope_a, rope_b = PT[:, 0, 4:8, :].rearrange("p c n -> p (c n)"), PT[:, 1, 0:4, :].rearrange("p c n -> p (c n)")
        nb3 = C[:, 0:B * HK // 2].bitcast(BF16).rearrange("p (b n) -> p b n", b=B)
        qh = VBD[:, 0:2 * S].rearrange("p (a n) -> p a n", a=2)
        Pm = att[:, :, :].rearrange("p a n -> p (a n)")[:, 0:2 * TB * S].rearrange("p (a i n) -> p a i n", a=2, i=TB)
        o_s = C[:, B * S:2 * B * S].rearrange("p (t d) -> p t d", d=D)
        c_s = C[:, B * S:2 * B * S]
        R0 = 12 * NT * E
        sg = att_flat[:, R0:R0 + 2 * S].rearrange("p (a n) -> p a n", a=2)
        hh = att_flat[:, R0 + 2 * S:R0 + 4 * S].rearrange("p (a n) -> p a n", a=2)
        sel = att[:, 0:2, 0:SEL]
        hh3 = att_flat[:, 2 * HK:2 * HK + 2 * J2 * S].rearrange("p (a f n) -> p a f n", a=2, f=J2)
        wide = PT[:, :, 0:E, :]
        hsum = PT[:, :, E, :]

        ps = ctx.enter_context(nc.psum_tensor("ps", [P, 8, BANK], F32))
        flat = ps[:, :, :].rearrange("p b n -> p (b n)")

        ld = {g: sem(f"loaded_{g}") for g in list(GROUPS) + ["x", "f1", "bgi", "moe", "f3", "rope", "m1", "m3"]}
        consts = sem("consts")
        tanh_done = sem("tanh_done")
        bf_done = sem("bf_done")
        s_stats, s_aggr, s_ve, s_rstd, s_xn = map(sem, ("stats_done", "aggregated", "var_eps", "rstd_done", "normed"))
        turned, turned_sb = sem("turned"), sem("turned_copied")
        x_new = sem("x_new")
        gate_chain, exp_gate = sem("gate_chain"), sem("exp_gate")
        router_ps = sem("router_ps")
        w_ready, wT_ps, wT_sb, wb_ps = sem("w_ready"), sem("wT_ps"), sem("wT_sb"), sem("wb_ps")
        q_ps, q_sb = sem("q_ps"), sem("q_sb")
        rot_ps, rope_chain, roped = sem("rot_ps"), sem("rope_chain"), sem("roped")
        y_set, nb_set, mneg_set, scratch = sem("y_set"), sem("nb_set"), sem("mneg_set"), sem("scratch")
        kv_ps, kv_sb, kv_chain = sem("kv_ps"), sem("kv_sb"), sem("kv_chain")
        kbd, vbd, vw_ps, vw_sb, vw_bo = map(sem, ("kbd_done", "vbd_done", "vw_ps", "vw_sb", "vw_bo"))
        fold_ps, fold_act, fold_dve = sem("fold_ps"), sem("fold_act"), sem("fold_dve")
        staged, scores, scores_read, rowmax, shifted = map(sem, ("q_staged", "scores", "scores_read", "rowmax", "shifted"))
        expd, rowsum, recip, probs, probsT_ps, probsT, attn_out = map(
            sem, ("exp_done", "rowsum", "recip", "probs", "probsT_ps", "probsT", "attn_out"))
        m_scores, m_rowmax, m_expd, m_probsT_ps, m_probsT, m_attn, m_rec, m_normed = map(
            sem, ("m_scores", "m_rowmax", "m_expd", "m_probsT_ps", "m_probsT", "m_attn", "m_rec", "m_normed"))
        ones_set, ot_ps, ot_sb, yo_ps = map(sem, ("ones_set", "ot_ps", "ot_sb", "yo_ps"))
        head_q = sem("head_q")
        m_high, m_summed = sem("m_high"), sem("m_summed")
        v_chain, v_split = sem("v_chain"), sem("v_split")
        mla_ps, v_ps, mla_sb = sem("mla_ps"), sem("v_ps"), sem("mla_sb")
        e0_staged, e0_ps, e0_read, e0_summed = map(sem, ("e0_staged", "e0_ps", "e0_read", "e0_summed"))
        up_ps, silu, gated, down_ps = map(sem, ("up_ps", "silu", "gated", "down_ps"))
        pol, pol_sb, sel_done, sel_chain = sem("pol"), sem("pol_sb"), sem("sel_done"), sem("sel_chain")
        h3_ps, h3_sb, r3_ps, r3_sb, o3_ps = map(sem, ("h3_ps", "h3_sb", "r3_ps", "r3_sb", "o3_ps"))
        stored, scratch_w = sem("stored"), sem("w_staged")

        CREDITS = [(turned, 1), (turned_sb, 1), (vw_ps, 2), (vw_sb, 1), (e0_ps, 2), (e0_read, 2), (e0_summed, 2), (gated, 2), (down_ps, 2),
                   (m_expd, 4), (m_probsT, 3), (m_normed, 1), (m_summed, 1), (m_scores, 8), (m_probsT_ps, 6), (m_attn, 2),
                   (x_new, 2), (scores, 2), (scores_read, 1), (shifted, 1), (expd, 2), (probs, 2), (probsT_ps, 6),
                   (probsT, 3), (attn_out, 2)]

        def tiles_before(s):
            return LAYER[s] * NT

        def wait(eng, sm, value):
            if isinstance(value, int) and value <= 0:
                return
            eng.wait_ge(sm, value)

        def fold_bank(s, b):
            return 3 if s != X2 and b >= 2 else 0

        def turn_bank(s, b):
            return 5 if s in (X0, F0, F1, MOE) and b % 2 == 1 else 7

        def tok(b, i, n=1):
            return bass.ds(b * TB + i, n)

        def cols(b, n=S):
            return bass.ds(b * n, n)

        def batch(t, b):
            v = t[:, bass.ds(b, 1)]
            return v.rearrange("p b n -> p (b n)") if len(v.shape) == 3 else v.rearrange("p b c n -> p (b c n)")

        def heads(a):
            return a.rearrange("p (h k) -> p h k", k=KEYS)

        def over_keys(a):
            return a.unsqueeze(2).to_broadcast([P, H, KEYS])

        def folded(u):
            h, k = divmod(u, 3)
            return (KBD[:, :, :], C[:, :].rearrange("p (b n) -> p b n", b=B), VWT)[k][:, :, h * KEYS:(h + 1) * KEYS]

        def batch_and_head(t):
            return t.n // H, t.n % H

        def values_of(b, j, h):
            return VP[:, tok(b, j), bass.ds(h, 1), :, :].rearrange("p t h c d -> p (t h c d)")

        def starts(eng, s):
            if s > X0:
                eng.wait_ge(x_new, XNEW0[s])

        block = ctx.enter_context(nc.Block())

        @block.sync
        def _(sp):
            for sm, n in CREDITS:
                sp.sem_inc(sm, n)

            def load(dst, src, g):
                sp.dma_start(dst, src).then_inc(ld[g], 16)

            a, z = WIDTH["a"]
            load(W[:, a:z], packed[:, a:z], "a")
            load(x[:, :, :], x_in.rearrange("(t p) d -> p t d", p=P), "x")
            for g in "bcde":
                a, z = WIDTH[g]
                load(W[:, a:z], packed[:, a:z], g)
                if g == "b":
                    load(mask_u8[:, :].rearrange("p (t k) -> p t k", k=KEYS),
                         mask1.bitcast(U8).rearrange("(t p k) -> p t k", p=P, k=KEYS), "m1")
                    load(U[:, :], w_ffn1[:, 0:3 * E * HID1], "f1")
                    load(bgi[:, :, :, :].rearrange("p a e j -> p (a e j)"), w_ffn1[:, 3 * E * HID1:], "bgi")
            load(mask3_u8[:, :], mask3, "m3")
            sp.wait_ge(x_new, XNEW0[X2])
            load(U[:, 0:2 * E * HID2], w_moe, "moe")
            load(U[:, 11264:11264 + 2 * S], rope, "rope")
            sp.wait_ge(x_new, XNEW0[MLA])
            load(U[:, 4096:4096 + E * SEL], w_ffn3, "f3")
            for b in range(B):
                sp.wait_ge(x_new, XNEW0[F3] + b + 1)
                sp.dma_start(out[b * S:(b + 1) * S, :].rearrange("(t p) d -> p t d", p=P),
                             x[:, b * TB:(b + 1) * TB, :]).then_inc(stored, 16)
            sp.wait_ge(stored, 16 * B)

        @block.tensor
        def _(pe):
            mm = pe.matmul
            ident = w("ident")
            pe.wait_ge(ld["a"], 16)

            def keep_warm(turns, bank=7):
                with pe.Fori(0, turns):
                    for _ in range(8):
                        mm(ps[:, bank, 0:P], identb[:, :], identb[:, :], start=True, stop=True)

            def turn(nth, rounds, rows=P, s=None, b=0):
                pe.wait_ge(s_xn, TB * rounds)
                two = s is not None and turn_bank(s, 1) != 7
                pe.wait_ge(turned_sb, nth if two else nth + 1)
                bank = 7 if s is None else turn_bank(s, b)
                for i in range(TB):
                    t = pe.transpose(ps[:, bank, i * rows:(i + 1) * rows], xn_at[nth % 2][0:rows, i, :],
                                     ident[0:rows, 0:rows])
                t.then_inc(turned, 1)

            def prepare(s, after):
                starts(pe, s)
                first = B if s == MLA else 0
                ahead = 1 if turn_bank(s, 1) != 7 else 0
                if s in WARM:
                    pe.wait_ge(turned_sb, TURN0[s] + 1)
                    keep_warm(WARM[s])
                for b in range(B + ahead):
                    if b < B:
                        if b == 0 and ahead:
                            pe.wait_ge(turned_sb, TURN0[s] + 1)
                        turn(TURN0[s] + b, ROUND0[s] + first + b + 1, s=s, b=b)
                    if after is not None and b >= ahead:
                        after(b - ahead)

            def turned_copied(s, b):
                pe.wait_ge(turned_sb, TURN0[s] + b + 2)

            def route(s, b, weight):
                turned_copied(s, b)
                for i in range(TB):
                    t = mm(ps[:, 6, (b * TB + i) * E:(b * TB + i + 1) * E],
                           FT[:, (b * TB + i) * P:(b * TB + i + 1) * P], weight, start=True, stop=True)
                t.then_inc(router_ps, 1)

            def weighted_bias(n, rows):
                pe.wait_ge(w_ready, n + 1)
                for b in range(B):
                    for i in range(TB):
                        t = pe.transpose(ps[0:E, 2 + b, i * P:(i + 1) * P], w_all[:, b * TB + i, :], ident)
                    t.then_inc(wT_ps, 1)
                for b in range(B):
                    pe.wait_ge(wT_sb, n * B + b + 1)
                    for i in range(TB):
                        t = mm(ps[:, 2 + b, i * D:(i + 1) * D], wT_s[:, b * TB + i, :], rows, start=True, stop=True)
                    t.then_inc(wb_ps, 1)

            def fold_values(s, wo, b):
                n = FOLD[s] * B + b
                pe.wait_ge(vbd, n + 1)
                pe.wait_ge(vw_sb, n + 1)
                for c in range(NC):
                    m = P if c < NC - 1 else LAST
                    t = mm(ps[0:m, fold_bank(s, b) + c // 4, (c % 4) * D:(c % 4 + 1) * D], VBD_at[b % 2][:, c * P:c * P + m], wo,
                           start=True, stop=True)
                t.then_inc(vw_ps, 1)

            def keys_values(s):
                starts(pe, s)
                if s in (X0, X3):
                    l = LAYER[s]
                    pe.wait_ge(ld["a" if s == X0 else "e"], 16)
                    mm(ps[:, 0, 0:CK], w(f"{l}wk"), w("ctxT"), start=True, stop=True).then_inc(kv_ps, 1)
                    mm(ps[:, 1, 0:CK], w(f"{l}wv"), w("ctxT"), start=True, stop=True).then_inc(kv_ps, 1)
                    pe.wait_ge(kv_sb, KV_SB0[s] + 2)
                    if s == X3:
                        mm(ps[:, 2, 0:CK], w("rot"), kT_s, start=True, stop=True).then_inc(kv_ps, 1)
                        pe.wait_ge(kv_chain, 3)
                    fold_values(s, w(f"{l}wo"), 0)
                elif s == X1:
                    for b in range(B):
                        t = mm(ps[0:KEYS, b // 2, (b % 2) * 2 * D:(b % 2 + 1) * 2 * D],
                               w("ctxT")[:, b * KEYS:(b + 1) * KEYS], w("1wkv"), start=True, stop=True)
                    t.then_inc(kv_ps, 1)
                    for r in range(KV1):
                        turn(TURN0[X1] - KV1 + r, ROUND0[X1] - KV1 + r + 1, rows=KEYS)
                    fold_values(s, ident, 0)
                else:
                    pe.wait_ge(ld["c"], 16)
                    for u in range(H):
                        if u >= 6:
                            pe.wait_ge(kv_sb, KV_SB0[X2] + u - 5)
                        wt = w("2wk") if u % 2 == 0 else w("2wv")
                        c = u // 2
                        mm(ps[:, u % 6, 0:CK], wt[:, c * D:(c + 1) * D], w("ctxT"), start=True, stop=True)\
                            .then_inc(kv_ps, 1)
                    keep_warm(WARM_FOLD)
                    pe.wait_ge(kv_sb, KV_SB0[X2] + H)
                    for u in range(3 * H):
                        if u >= 6:
                            pe.wait_ge(fold_act if u % 2 == 0 else fold_dve, (u - 6) // 2 + 1)
                        h, k = divmod(u, 3)
                        c, r = h // 2, HD2 * (h % 2)
                        rows = slice(r, r + HD2)
                        lhs = (w("2wqT")[rows, c * D:(c + 1) * D],
                               w("2b")[rows, c:c + 1].to_broadcast([HD2, P]),
                               w("2wo")[rows, c * D:(c + 1) * D])[k]
                        rhs = (kT2, kT2, vT2)[k][rows, c, :]
                        mm(ps[:, u % 6, 0:CK], lhs, rhs, start=True, stop=True).then_inc(fold_ps, 1)
                    pe.wait_ge(fold_act, 3 * H // 2)
                    pe.wait_ge(fold_dve, 3 * H // 2)
                    for b in range(B):
                        if b >= 2:
                            pe.wait_ge(fold_act, 3 * H // 2 + b - 1)
                        for c in range(NC):
                            m = P if c < NC - 1 else LAST
                            k = 3 * (b % 2) + c // 4
                            t = pe.transpose(ps[0:m, k, (c % 4) * D:(c % 4 + 1) * D], VWT[:, b, c * P:c * P + m],
                                             ident)
                        t.then_inc(fold_ps, 1)

            def cross(s):
                n0 = tiles_before(s)

                def score(t):
                    pe.wait_ge(staged, t.n + n0 + 1)
                    if s in (X1, X2):
                        pe.wait_ge(scores_read, t.n + (LAYER[s] - 1) * NT + 1)
                    else:
                        pe.wait_ge(shifted, t.n + n0 + 1)
                    causal = s == X2 and t.k % TB == 0
                    for c in range(3):
                        a, z = c * BANK, min((c + 1) * BANK, HK)
                        m = mm(flat[:, a:z], qs[:, t.slot(2), :], batch(KBD, t.group)[:, a:z],
                               start=True, stop=not (causal or s == X3))
                        if causal:
                            m = mm(flat[:, a:z], identb[:, :], cmaskb[:, a:z], start=False, stop=True)
                        if s == X3:
                            m = mm(flat[:, a:z], identb[:, :], batch(nb3, t.group)[:, a:z], start=False, stop=True)
                    m.then_inc(scores, 1)

                def turn_probs(t):
                    pe.wait_ge(probs, t.n + n0 + 3)
                    if isinstance(t.n, int) and t.n == 0 and s != X2:
                        pe.wait_ge(vw_sb, (FOLD[s] + 1) * B + 1)
                    for k in range(3):
                        pe.wait_ge(probsT, t.n * 3 + 3 * n0 + k + 1)
                        for c in range(4 * k, min(4 * k + 4, NC)):
                            m = P if c < NC - 1 else LAST
                            q = pe.transpose(ps[0:m, 3 + k, (c % 4) * P:(c % 4 + 1) * P],
                                             att[:, 2 + t.slot(2), c * P:c * P + m], ident)
                        q.then_inc(probsT_ps, 1)
                    if isinstance(t.n, int) and t.n == 0 and s in (X0, X3):
                        pe.wait_ge(vw_bo, {X0: 1, X3: 3}[s])

                def late_fold(t):
                    if s != X2 and isinstance(t.n, int) and t.n + 2 < B:
                        fold_values(s, ident if s == X1 else w(f"{LAYER[s]}wo"), t.n + 2)

                def product(t):
                    pe.wait_ge(x_new, t.n + XNEW0[s] + (B if s == X3 else 0) - 1)
                    for k in range(3):
                        pe.wait_ge(probsT, t.n * 3 + 3 * n0 + k + 4)
                        for c in range(4 * k, min(4 * k + 4, NC)):
                            m = P if c < NC - 1 else LAST
                            q = mm(ps[:, 6 + t.slot(2), 0:D], PT[0:m, t.slot(2), c, :],
                                   batch(VW, t.group)[0:m, c * D:(c + 1) * D], start=(c == 0), stop=(c == NC - 1))
                    q.then_inc(attn_out, 1)

                if s != X2:
                    pe.wait_ge(kbd, FOLD[s] + 1)
                if s == X2:
                    pe.wait_ge(vw_bo, 2)
                else:
                    pe.wait_ge(vw_sb, FOLD[s] * B + 3)
                if s == X2:
                    pe.wait_ge(bf_done, 3)
                if s == X3:
                    pe.wait_ge(nb_set, 1)
                skewed_loop(pe, [(score, 0), (late_fold, 0), (product, 3), (turn_probs, 2)], NT, TB)

            def experts(s, J, wg, wi, wo):
                units = E * J
                u0 = UNIT0[s]
                bias = 1 if s == F1 else 0
                per = E * TB + bias
                x0 = XNEW0[s]
                pe.wait_ge(x_new, x0)

                def chunk(c):
                    def up(u):
                        e, j = divmod(u, J)
                        if s == F1:
                            pe.wait_ge(gated, c * units + u0 + u + 1)
                        else:
                            pe.wait_ge(silu, c * units + u0 + u - 1)
                        t = mm(ps[:, u % 2, :], wg[:, e, j * P:(j + 1) * P], FT[:, cols(c)], start=True, stop=True)
                        if wi is not None:
                            t = mm(ps[:, 2 + u % 2, :], wi[:, e, j * P:(j + 1) * P], FT[:, cols(c)],
                                   start=True, stop=True)
                        t.then_inc(up_ps, 1)

                    def down(u):
                        e, j = divmod(u, J)
                        if s == F1:
                            pe.wait_ge(gated, c * units + u0 + u + 3)
                        else:
                            pe.wait_ge(silu, c * units + u0 + u + 1)
                        if j == 0:
                            pe.wait_ge(x_new, c * per + (bias if e >= 2 else 0) + (e - 1) * TB + x0)
                        for i in range(TB):
                            t = mm(ps[:, 4 + e % 2, i * D:(i + 1) * D], hh[:, u % 2, i * P:(i + 1) * P], wo[:, e, j, :],
                                   start=(j == 0 and i == 0), stop=(j == J - 1 and i == TB - 1))
                        t.then_inc(down_ps, 1)

                    up(0)
                    for u in range(1, units):
                        up(u)
                        if s == F1 and u == 1:
                            pe.wait_ge(scratch_w, c + 1)
                            for i in range(TB):
                                t = pe.transpose(ps[0:E, 6, i * P:(i + 1) * P], w_c[:, i, :], ident)
                            t.then_inc(wT_ps, 1)
                        down(u - 1)
                        if s == F1 and u == 2:
                            pe.wait_ge(wT_sb, c + B + 1)
                            for i in range(TB):
                                t = mm(ps[:, 7, i * D:(i + 1) * D], wT_c[:, i, :], w("1bo", E), start=True, stop=True)
                            t.then_inc(wb_ps, 1)
                    down(units - 1)
                with pe.Fori(0, B) as c:
                    chunk(c)

            keys_values(X0)

            def q0(b):
                turned_copied(X0, b)
                mm(ps[:, 6, :], w("0wq"), xnT_s[:, :], start=True, stop=True).then_inc(q_ps, 1)
            prepare(X0, q0)
            fold_values(X0, w("0wo"), 1)
            cross(X0)

            pe.wait_ge(ld["b"], 16)

            prepare(F0, lambda b: route(F0, b, w("0rw")))
            weighted_bias(0, w("0eb", E))

            def experts0(t):
                pe.wait_ge(e0_staged, t.n + 1)
                pe.wait_ge(e0_read, t.n + 1)
                for c in range(2):
                    m = mm(ps[:, 6 * t.slot(2) + c, :], qs[:, t.slot(2), :], w("0we")[:, c * BANK:(c + 1) * BANK],
                           start=True, stop=True)
                m.then_inc(e0_ps, 1)
            skewed_loop(pe, [(experts0, 0)], NT, TB)

            keys_values(X1)

            def q1(b):
                turned_copied(X1, b)
                for i in range(TB):
                    t = mm(ps[:, 3 + b, i * D:(i + 1) * D], xnT_s[:, i * P:(i + 1) * P], w("1wq"), start=True, stop=True)
                t.then_inc(q_ps, 1)
            prepare(X1, q1)
            fold_values(X1, ident, 1)
            for b in range(B):
                turn(TURN0[X1] + B + b, ROUND0[X1] + B + b + 1)
            cross(X1)

            prepare(F1, lambda b: route(F1, b, w("1gw")))
            pe.wait_ge(ld["f1"], 16)
            experts(F1, J1, WG1, WI1, WO1)

            keys_values(X2)
            prepare(X2, None)
            cross(X2)

            pe.wait_ge(ld["d"], 16)

            def latents(b):
                turned_copied(MLA, b)
                mm(ps[:, 6, :], w("mwq"), xnT_s[:, :], start=True, stop=True).then_inc(mla_ps, 1)
                mm(ps[0:LAT, 5, :], w("mwd"), xnT_s[:, :], start=True, stop=True).then_inc(mla_ps, 1)
            prepare(MLA, latents)
            for b in range(B):
                pe.wait_ge(mla_sb, b * 2 + 2)
                for i in range(TB):
                    t = mm(ps[:, b, i * D:(i + 1) * D], c_s[0:LAT, b * S + i * P:b * S + (i + 1) * P], w("mwuv", LAT),
                           start=True, stop=True)
                t.then_inc(v_ps, 1)
                pe.wait_ge(mla_sb, 2 * B)
                if b >= 2:
                    pe.wait_ge(mla_sb, 2 * B + b - 1)
                mm(ps[:, 4 + 2 * (b % 2), :], w("mwuk", LAT), c_s[0:LAT, b * S:(b + 1) * S], start=True, stop=True)\
                    .then_inc(mla_ps, 1)

            pe.wait_ge(mla_sb, 3 * B)
            pe.wait_ge(v_split, B)
            pe.wait_ge(ones_set, 2)
            pe.wait_ge(bf_done, 3)

            def score(t):
                n = t.n
                b, _ = batch_and_head(t)
                pe.wait_ge(head_q, n + 1)
                for i in range(TB):
                    pe.wait_ge(m_expd, n * 4 + i + 1)
                    z = (i + 1) * P
                    mm(ps[:, i, i * P:z], identb[:, :], diagb[:, :], start=True, stop=False, skip_group_check=True)
                    mm(ps[:, i, 0:z], qh[:, t.slot(2), i * P:(i + 1) * P], KT[:, bass.ds(b * S, z)], start=False, stop=True,
                       skip_group_check=True).then_inc(m_scores, 1)

            def turn_probs(t):
                n = t.n
                for k in range(3):
                    pe.wait_ge(m_probsT, n * 3 + k + 1)
                    for c in range(4 * k, min(4 * k + 4, len(BLOCKS))):
                        i, j = BLOCKS[c]
                        if j == 0:
                            pe.wait_ge(m_expd, n * 4 + i + 5)
                        q = pe.transpose(ps[:, 4 + k, (c % 4) * P:(c % 4 + 1) * P],
                                         Pm[:, t.slot(2), i, j * P:(j + 1) * P], ident)
                    q.then_inc(m_probsT_ps, 1)

            def weigh(t):
                n = t.n
                b, h = batch_and_head(t)
                pe.wait_ge(m_summed, n + 1)
                for c, (i, j) in enumerate(BLOCKS):
                    if c % 4 == 0:
                        pe.wait_ge(m_probsT, n * 3 + c // 4 + 4)
                    for half in range(2):
                        q = mm(ps[:, 7, i * PIECES * VE:(i + 1) * PIECES * VE], PH[:, t.slot(2), half, c, :],
                               values_of(b, j, h), start=(j == 0 and half == 0), stop=(j == i and half == 1))
                q.then_inc(m_attn, 1)

            skewed_loop(pe, [(score, 0), (turn_probs, 1), (weigh, 2)], B * H, 2)
            pe.wait_ge(m_normed, B * H + 1)
            for b in range(B):
                for i in range(TB):
                    t = pe.transpose(ps[:, b, i * P:(i + 1) * P], o_s[:, b * TB + i, :], ident)
                t.then_inc(ot_ps, 1)
            for b in range(B):
                pe.wait_ge(ot_sb, b + 1)
                for i in range(TB):
                    t = mm(ps[:, 4 + b, i * D:(i + 1) * D], oT_s[b % 2][:, i * P:(i + 1) * P], w("mwo"),
                           start=True, stop=True)
                t.then_inc(yo_ps, 1)

            prepare(MOE, lambda b: route(MOE, b, w("mgw")))
            pe.wait_ge(ld["moe"], 16)
            experts(MOE, J2, W1M, None, W2M)

            keys_values(X3)

            def rotate(b):
                pe.wait_ge(q_sb, b + B + 1)
                if b >= 3:
                    pe.wait_ge(roped, b - 2)
                mm(ps[:, 3 + b % 3, :], w("rot"), FT[:, b * S:(b + 1) * S], start=True, stop=True).then_inc(rot_ps, 1)

            def q3(b):
                turned_copied(X3, b)
                pe.wait_ge(q_sb, b + B)
                mm(ps[:, 6, :], w("3wq"), xnT_s[:, :], start=True, stop=True).then_inc(q_ps, 1)
                if b >= 1:
                    rotate(b - 1)
            prepare(X3, q3)
            rotate(B - 1)
            fold_values(X3, w("3wo"), 1)
            cross(X3)

            prepare(F3, None)
            pe.wait_ge(turned_sb, TURN0[F3] + B + 1)
            mm(ps[:, 6, 0:B], w("wp1"), FT[:, S - 1:B * S:S], start=True, stop=True).then_inc(pol, 1)
            pe.wait_ge(pol_sb, 1)
            for b in range(B):
                t = mm(ps[:, 7, b * E:(b + 1) * E], hp_s[:, b:b + 1].to_broadcast([P, P]), w("wp2"),
                       start=True, stop=True)
            t.then_inc(pol, 1)
            keep_warm(8, bank=6)

            def up3(t):
                pe.wait_ge(sel_done, t.n + 1)
                for f in range(J2):
                    mm(ps[:, 4 * t.slot(2) + f, :], sel[:, t.slot(2), f * P:(f + 1) * P], FT[:, cols(t.n)],
                       start=True, stop=True).then_inc(h3_ps, 1)

            def down3(t):
                for f in range(J2):
                    pe.wait_ge(h3_sb, t.n * J2 + f + 1)
                    a = HID2 + J2 + f * D
                    m = mm(ps[:, 2, :], sel[:, t.slot(2), a:a + D], hh3[:, t.slot(2), f, :],
                           start=(f == 0), stop=(f == J2 - 1))
                m.then_inc(r3_ps, 1)
                pe.wait_ge(r3_sb, t.n + 1)
                pe.wait_ge(x_new, t.n + XNEW0[F3])
                for i in range(TB):
                    m = mm(ps[:, 3, i * D:(i + 1) * D], r_s[:, i, :], w("3fwo"), start=True, stop=True)
                m.then_inc(o3_ps, 1)
            skewed_loop(pe, [(up3, 0), (down3, 1)], B, 2)

        @block.scalar
        def _(act):
            go = act.activation
            act.wait_ge(ld["a"], 16)
            go(tg[:, :], w("gates"), ACT.Tanh).then_inc(tanh_done, 1)

            def turned_copy(s, b, k, copies):
                act.wait_ge(turned, TURN0[s] + k * B + b + 2)
                for dst, scale, bias in copies:
                    if bias is not None:
                        t = go(dst, ps[:, turn_bank(s, b), :], ACT.Identity, scale=scale, bias=bias)
                    elif scale is not None:
                        t = go(dst, ps[:, turn_bank(s, b), :], ACT.Copy, scale=scale)
                    else:
                        t = go(dst, ps[:, turn_bank(s, b), :], ACT.Copy)
                t.then_inc(turned_sb, 1)

            def copy_vw(b, k0):
                vw = VW[:, b, :, :].rearrange("p c n -> p (c n)")
                go(vw[:, 0:4 * D], ps[:, k0, :], ACT.Copy)
                go(vw[:, 4 * D:8 * D], ps[:, k0 + 1, :], ACT.Copy)
                go(vw[:, 8 * D:9 * D], ps[:, k0 + 2, 0:D], ACT.Copy)
                return go(vw[0:LAST, 9 * D:10 * D], ps[0:LAST, k0 + 2, D:2 * D], ACT.Copy)

            def fold_values(s, b):
                n = b + FOLD[s] * B
                act.wait_ge(vw_ps, n + 3)
                copy_vw(b, fold_bank(s, b)).then_inc(vw_sb, 1)

            def keys_values(s):
                starts(act, s)
                if s in (X0, X3):
                    b_ = w(f"{LAYER[s]}b")
                    act.wait_ge(ld["a" if s == X0 else "e"], 16)
                    act.wait_ge(kv_ps, KV_PS0[s] + 1)
                    go(kT_s, ps[:, 0, 0:CK], ACT.Identity, bias=b_[:, 1:2]).then_inc(kv_sb, 1)
                    act.wait_ge(kv_ps, KV_PS0[s] + 2)
                    go(vT_s, ps[:, 1, 0:CK], ACT.Identity, bias=b_[:, 2:3]).then_inc(kv_sb, 1)
                    fold_values(s, 0)
                elif s == X1:
                    act.wait_ge(ld["b"], 16)
                    gb = w("1gb")
                    for r, dst in enumerate((kT_s, vT_s)):
                        act.wait_ge(turned, TURN0[X1] - KV1 + r + 2)
                        go(dst, ps[:, 7, 0:CK], ACT.Identity, scale=gb[:, 2 + 2 * r:3 + 2 * r],
                           bias=gb[:, 3 + 2 * r:4 + 2 * r]).then_inc(turned_sb, 1)
                    fold_values(s, 0)
                else:
                    act.wait_ge(ld["c"], 16)
                    for u in range(H):
                        c = u // 2
                        act.wait_ge(kv_ps, KV_PS0[X2] + u + 1)
                        k = 8 if u % 2 == 0 else 16
                        go((kT2 if u % 2 == 0 else vT2)[:, c, :], ps[:, u % 6, 0:CK], ACT.Identity,
                           bias=w("2b")[:, k + c:k + c + 1]).then_inc(kv_sb, 1)
                    for u in range(0, 3 * H, 2):
                        act.wait_ge(fold_ps, u + 1)
                        go(folded(u), ps[:, u % 6, 0:CK].rearrange("p (b k) -> p b k", k=KEYS), ACT.Copy)\
                            .then_inc(fold_act, 1)
                    for b in range(B):
                        act.wait_ge(fold_ps, 3 * H + b + 1)
                        copy_vw(b, 3 * (b % 2)).then_inc(fold_act, 1)

            def cross(s, scale):
                n0 = tiles_before(s)

                def stage(t):
                    act.wait_ge(scores, t.n + n0 + 1)
                    go(qs[:, t.slot(2), :], FT[:, bass.ds(t.n * P, P)], ACT.Copy).then_inc(staged, 1)

                def exponent(t):
                    act.wait_ge(shifted, t.n + n0 + 2)
                    act.wait_ge(probsT_ps, t.n * 3 + 3 * n0 + 3)
                    go(att[:, 2 + t.slot(2), :], att[:, t.slot(2), :], ACT.Exp, scale=scale).then_inc(expd, 1)

                def evacuate(t):
                    act.wait_ge(attn_out, t.n + n0 + 1)
                    for k in range(3):
                        act.wait_ge(probsT_ps, t.n * 3 + 3 * n0 + k + 7)
                        if k < 2:
                            go(PT[:, t.slot(2), 4 * k:4 * k + 4, :].rearrange("p c n -> p (c n)"), ps[:, 3 + k, :],
                               ACT.Copy).then_inc(probsT, 1)
                        else:
                            go(PT[:, t.slot(2), 8, :], ps[:, 5, 0:P], ACT.Copy)
                            go(PT[0:LAST, t.slot(2), 9, :], ps[0:LAST, 5, P:2 * P], ACT.Copy).then_inc(probsT, 1)

                def late_fold(t):
                    if s != X2 and isinstance(t.n, int) and t.n + 2 < B:
                        fold_values(s, t.n + 2)

                skewed_loop(act, [(stage, 0), (evacuate, 3), (exponent, 1), (late_fold, 0)], NT, TB)

            def gate_exp(n, chain, src, dst):
                act.wait_ge(gate_chain, chain)
                go(dst, src, ACT.Exp).then_inc(exp_gate, 1)

            def copy_wT(n):
                for b in range(B):
                    act.wait_ge(wT_ps, n * B + b + 1)
                    go(wT_s[:, b * TB:(b + 1) * TB, :].rearrange("e i p -> e (i p)"), ps[0:E, 2 + b, :], ACT.Copy)\
                        .then_inc(wT_sb, 1)

            def hidden(s, J, dst):
                units = E * J
                u0 = UNIT0[s]
                with act.Fori(0, B) as c:
                    for u in range(units):
                        e, j = divmod(u, J)
                        if s == F1 and u == 2:
                            act.wait_ge(wT_ps, c + B + 1)
                            go(wT_c.rearrange("e i p -> e (i p)"), ps[0:E, 6, :], ACT.Copy).then_inc(wT_sb, 1)
                        act.wait_ge(up_ps, c * units + u0 + u + 1)
                        if s == F1:
                            act.wait_ge(gated, c * units + u0 + u + 1)
                            go(dst[:, u % 2, :], ps[:, u % 2, :], ACT.Silu, bias=bgi[:, 0, e, j:j + 1]).then_inc(silu, 1)
                        else:
                            act.wait_ge(down_ps, c * units + u0 + u + 1)
                            go(dst[:, u % 2, :], ps[:, u % 2, :], ACT.Silu).then_inc(silu, 1)

            keys_values(X0)
            for b in range(B):
                turned_copy(X0, b, 0, [(xnT_s[:, :], None, None)])
                act.wait_ge(q_ps, b + 1)
                go(FT[:, cols(b)], ps[:, 6, :], ACT.Identity, bias=w("0b")[:, 0:1]).then_inc(q_sb, 1)
            fold_values(X0, 1)
            act.wait_ge(q_sb, B)
            cross(X0, HD ** -0.5)

            starts(act, F0)
            for b in range(B):
                turned_copy(F0, b, 0, [(FT[:, cols(b)], None, None)])
            gate_exp(0, 3, G[:, 1, :, :], G[:, 2, :, :])
            copy_wT(0)

            def stage0(t):
                act.wait_ge(e0_ps, t.n + 1)
                go(qs[:, t.slot(2), :], FT[:, bass.ds(t.n * P, P)], ACT.Copy).then_inc(e0_staged, 1)
            act.wait_ge(turned_sb, TURN0[F0] + B + 1)
            skewed_loop(act, [(stage0, 0)], NT, TB)

            keys_values(X1)
            for b in range(B):
                turned_copy(X1, b, 0, [(xnT_s[:, :], None, None)])
            fold_values(X1, 1)
            for b in range(B):
                turned_copy(X1, b, 1, [(FT[:, cols(b)], w("1gb")[:, 0:1], w("1gb")[:, 1:2])])
            act.wait_ge(turned_sb, TURN0[X1] + 2 * B + 1)
            cross(X1, 1.0)

            starts(act, F1)
            for b in range(B):
                turned_copy(F1, b, 0, [(FT[:, cols(b)], None, None)])
            gate_exp(1, TOP1 + 12, G[:, 10, :, 0:1], G[:, 11, :, 0:1])
            act.wait_ge(ld["bgi"], 16)
            hidden(F1, J1, sg)

            keys_values(X2)
            for b in range(B):
                turned_copy(X2, b, 0, [(FT[:, cols(b)], None, None)])
            act.wait_ge(turned_sb, TURN0[X2] + B + 1)
            cross(X2, HD2 ** -0.5)

            starts(act, MLA)
            act.wait_ge(ld["d"], 16)
            for b in range(B):
                turned_copy(MLA, b, 0, [(xnT_s[:, :], w("mg")[:, 0:1], None)])
                act.wait_ge(mla_ps, b * 2 + 1)
                go(FT[:, cols(b)], ps[:, 6, :], ACT.Copy, scale=HD ** -0.5).then_inc(mla_sb, 1)
                act.wait_ge(mla_ps, b * 2 + 2)
                go(c_s[0:LAT, cols(b)], ps[0:LAT, 5, :], ACT.Copy).then_inc(mla_sb, 1)
            for b in range(B):
                act.wait_ge(mla_ps, 2 * B + b + 1)
                go(KT[:, cols(b)], ps[:, 4 + 2 * (b % 2), :], ACT.Copy).then_inc(mla_sb, 1)
            act.wait_ge(mla_sb, 3 * B)

            def exponents(t, tiles):
                n = t.n
                if 0 in tiles:
                    act.wait_ge(m_probsT_ps, n * 3 + 3)
                for i in tiles:
                    act.wait_ge(m_rowmax, n * 4 + i + 1)
                    z = (i + 1) * P
                    go(Pm[:, t.slot(2), i, 0:z], ps[:, i, 0:z], ACT.Exp, bias=negm[:, t.slot(2), i:i + 1])\
                        .then_inc(m_expd, 1)

            def first_exponents(t):
                exponents(t, range(TB - 1))

            def last_exponent(t):
                exponents(t, [TB - 1])

            def high_half(t):
                n = t.n
                act.wait_ge(m_attn, n + 1)
                for k in range(3):
                    act.wait_ge(m_probsT_ps, n * 3 + k + 7)
                    m = min(4, len(BLOCKS) - 4 * k)
                    go(PH[:, t.slot(2), 0, 4 * k:4 * k + m, :].rearrange("p c n -> p (c n)"), ps[:, 4 + k, 0:m * P],
                       ACT.Copy, scale=PSCALE).then_inc(m_high, 1)
            skewed_loop(act, [(first_exponents, 0), (high_half, 1), (last_exponent, 0)], B * H, 2)
            for b in range(B):
                act.wait_ge(ot_ps, b + 1)
                if b >= 2:
                    act.wait_ge(yo_ps, b - 1)
                go(oT_s[b % 2][:, :], ps[:, b, :], ACT.Copy).then_inc(ot_sb, 1)

            starts(act, MOE)
            for b in range(B):
                turned_copy(MOE, b, 0, [(FT[:, cols(b)], w("mg")[:, 1:2], None)])
            gate_exp(2, TOP1 + TOP2 + 12, G[:, 10, :, 0:1], G[:, 11, :, 0:1])
            hidden(MOE, J2, hh)

            keys_values(X3)
            for b in range(B):
                turned_copy(X3, b, 0, [(xnT_s[:, :], None, None)])
                act.wait_ge(q_ps, b + 2 * B + 1)
                go(FT[:, cols(b)], ps[:, 6, :], ACT.Identity, bias=w("3b")[:, 0:1]).then_inc(q_sb, 1)
            fold_values(X3, 1)
            act.wait_ge(roped, B)
            cross(X3, HD ** -0.5)

            starts(act, F3)
            for b in range(B):
                turned_copy(F3, b, 0, [(FT[:, cols(b)], None, None)])
            act.wait_ge(pol, 1)
            go(hp_s[:, :], ps[:, 6, 0:B], ACT.Gelu, bias=w("bp1")).then_inc(pol_sb, 1)

            def gelu3(t):
                sl = t.slot(2)
                wait(act, r3_ps, t.n - 1)
                for f in range(J2):
                    act.wait_ge(h3_ps, t.n * J2 + f + 1)
                    go(hh3[:, sl, f, :], ps[:, 4 * sl + f, :], ACT.Gelu, bias=sel[:, sl, HID2 + f:HID2 + f + 1])\
                        .then_inc(h3_sb, 1)

            def result3(t):
                act.wait_ge(r3_ps, t.n + 1)
                wait(act, o3_ps, t.n)
                go(r_s[:, :, :].rearrange("p i d -> p (i d)"), ps[:, 2, :], ACT.Identity,
                   bias=sel[:, t.slot(2), SEL - 1:SEL]).then_inc(r3_sb, 1)
            skewed_loop(act, [(gelu3, 0), (result3, 1)], B, 2)

        @block.gpsimd
        def _(pool):
            tt = pool.tensor_tensor
            pool.memset(minus_half[:, :], -0.5).then_inc(consts, 1)
            pool.wait_ge(consts, 1)

            def root(n, b, var=ve, out=rstd):
                pool.wait_ge(s_ve, n + 1)
                at = slice(b * TB, (b + 1) * TB)
                tt(out[:, at], var[:, at], minus_half[:, :], ALU.pow).then_inc(s_rstd, 1)

            def roots(s, k=0):
                for b in range(B):
                    root(ROUND0[s] + k * B + b, b)

            def block_values(s, b):
                pool.wait_ge(vw_ps, b + FOLD[s] * B + 1)
                tt(heads(VBD_at[b % 2]), vT_s[:, b * KEYS:(b + 1) * KEYS].unsqueeze(1).to_broadcast([P, H, KEYS]),
                   over_keys(w("hm")), ALU.mult).then_inc(vbd, 1)

            def values_and_roots(s):
                starts(pool, s)
                if s == X1:
                    for r in range(KV1):
                        root(ROUND0[X1] - KV1 + r, r)
                    pool.wait_ge(turned_sb, TURN0[X1] + 1)
                else:
                    pool.wait_ge(kv_sb, KV_SB0[s] + 2)
                block_values(s, 0)
                roots(s)
                for b in range(1, B):
                    block_values(s, b)

            def cross(s):
                n0 = tiles_before(s)

                def normalize(t):
                    pool.wait_ge(recip, t.n + n0 + 1)
                    p = heads(att[:, 2 + t.slot(2), :])
                    tt(p, p, over_keys(ri[:, t.slot(2), :]), ALU.mult).then_inc(probs, 1)
                skewed_loop(pool, [(normalize, 0)], NT, TB)

            pool.wait_ge(ld["a"], 16)
            values_and_roots(X0)
            cross(X0)
            pool.wait_ge(ld["m1"], 16)
            pool.tensor_scalar(C[:, 0:NT * KEYS], mask_u8[:, :], 1.0e9, -1.0e9, ALU.mult, ALU.add).then_inc(mneg_set, 1)
            roots(F0)
            values_and_roots(X1)
            roots(X1, 1)
            cross(X1)
            roots(F1)
            roots(X2)
            cross(X2)
            starts(pool, MLA)
            roots(MLA)
            for b in range(B):
                root(ROUND0[MLA] + B + b, b, msq, rrms)
            pool.memset(VP[:, :, :, 0, HD:VE], 1.0).then_inc(ones_set, 1)
            pool.memset(VP[:, :, :, 1:PIECES, HD:VE], 0.0).then_inc(ones_set, 1)
            pool.wait_ge(mla_sb, 3 * B)

            def head_queries(t):
                b, h = batch_and_head(t)
                pool.wait_ge(m_scores, t.n * 4 + 4)
                tt(qh[:, t.slot(2), :], FT[:, cols(b)], w("hm")[:, bass.ds(h, 1)].to_broadcast([P, S]), ALU.mult)\
                    .then_inc(head_q, 1)
            skewed_loop(pool, [(head_queries, 0)], B * H, 2)
            starts(pool, MOE)
            roots(MOE)
            pool.wait_ge(ld["m3"], 16)
            for b in range(B):
                t = pool.tensor_scalar(heads(nb3[:, b, :]),
                                       mask3_u8[:, b * KEYS:(b + 1) * KEYS].unsqueeze(1).to_broadcast([P, H, KEYS]),
                                       -NEG, NEG, ALU.mult, ALU.add)
            t.then_inc(nb_set, 1)
            values_and_roots(X3)
            cross(X3)
            roots(F3)

        @block.vector
        def _(dve):
            v = nc.vector
            tt, ts, stt = v.tensor_tensor, v.tensor_scalar, v.scalar_tensor_tensor

            def moments(n, src, b, rms=None, rows=P):
                counted = n - (B if n >= ROUND0[MLA] + B else 0)
                for i in range(TB):
                    v.bn_stats(stats[0:rows, b * TB + i, :], src(i)).then_inc(s_stats, 1)
                dve.wait_ge(s_stats, TB * (counted + 1))
                for i in range(TB):
                    v.bn_aggr(mv[0:rows, b * TB + i, :], stats[0:rows, b * TB + i, :]).then_inc(s_aggr, 1)
                dve.wait_ge(s_aggr, TB * (counted + 1))
                at = slice(b * TB, (b + 1) * TB)
                mean, var = mv[0:rows, at, 0], mv[0:rows, at, 1]
                if rms is not None:
                    tt(msq[0:rows, at], mean, mean, ALU.mult).then_inc(scratch, 1)
                    dve.wait_ge(scratch, rms)
                    stt(ve[0:rows, at], msq[0:rows, at], RMS_EPS, var, ALU.add, ALU.add).then_inc(s_ve, 1)
                else:
                    ts(ve[0:rows, at], var, LN_EPS, None, ALU.add).then_inc(s_ve, 1)

            def normed(n, n_turn, src, dst, b, rms=None, rows=P):
                dve.wait_ge(s_rstd, n + 1)
                if n_turn is not None:
                    wait(dve, turned, n_turn)
                for i in range(TB):
                    k = b * TB + i
                    if rms is not None:
                        ts(dst(i), src(i), rms[0:rows, k:k + 1], None, ALU.mult).then_inc(s_xn, 1)
                    else:
                        ts(dst(i), src(i), mv[0:rows, k, 0:1], rstd[0:rows, k:k + 1], ALU.subtract, ALU.mult)\
                            .then_inc(s_xn, 1)

            def xn_of(nth, rows=P):
                return lambda i: xn_at[nth % 2][0:rows, i, :]

            def rows_of(t, b):
                return lambda i: t[:, b * TB + i, :]

            def moments_of_x(s, first=0):
                for b in range(first, B):
                    moments(ROUND0[s] + b, rows_of(x, b), b)

            def norm_x(s, first=0):
                moments_of_x(s, first)
                for b in range(B):
                    normed(ROUND0[s] + b, TURN0[s] + b, rows_of(x, b), xn_of(TURN0[s] + b), b)

            def norm_y(s, n, rms):
                for b in range(B):
                    normed(n + b, TURN0[s] + b, rows_of(y, b), xn_of(TURN0[s] + b), b, rms=rms)

            def row(t, b, i):
                return t[:, tok(b, i), :].rearrange("p t d -> p (t d)")

            def block_keys(s):
                starts(dve, s)
                dst = KBD[:, :, :].rearrange("p b (h k) -> p b h k", k=KEYS)
                if s == X1:
                    dve.wait_ge(turned_sb, TURN0[X1])
                elif s == X0:
                    dve.wait_ge(kv_sb, 1)
                for b in range(B):
                    t = tt(dst[:, b], kT_s[:, b * KEYS:(b + 1) * KEYS].unsqueeze(1).to_broadcast([P, H, KEYS]),
                           over_keys(w("hm")), ALU.mult)
                t.then_inc(kbd, 1)

            def add_output_bias(s):
                if s == X2:
                    dve.wait_ge(fold_act, 3 * H // 2 + B)
                else:
                    dve.wait_ge(vw_sb, (FOLD[s] + 1) * B + 1)
                tt(VW[:, :, 0, :], VW[:, :, 0, :], w(f"{LAYER[s]}bo").unsqueeze(1).to_broadcast([P, B, D]), ALU.add)\
                    .then_inc(vw_bo, 1)

            def cross(s):
                n0 = tiles_before(s)

                def add_to_scores(t):
                    dve.wait_ge(scores, t.n + n0 + 3)
                    dve.wait_ge(expd, t.n + n0 + 1)
                    if s == X1:
                        m = mneg[:, bass.ds(t.n, 1), :].to_broadcast([P, H, KEYS])
                        stt(heads(att[:, t.slot(2), :]), heads(flat[:, 0:HK]), HD ** -0.5, m, ALU.mult, ALU.add)\
                            .then_inc(scores_read, 1)
                    else:
                        tt(att[:, t.slot(2), :], flat[:, 0:HK], batch(C[:, :].rearrange("p (b n) -> p b n", b=B), t.group),
                           ALU.add).then_inc(scores_read, 1)

                def largest(t):
                    if s in (X1, X2):
                        src = heads(att[:, t.slot(2), :])
                        dve.wait_ge(scores_read, t.n + (LAYER[s] - 1) * NT + 2)
                    else:
                        src = heads(flat[:, 0:HK])
                        dve.wait_ge(scores, t.n + n0 + 3)
                        dve.wait_ge(expd, t.n + n0 + 1)
                    v.tensor_reduce(mx[:, t.slot(2), :], src, AX.X, ALU.max).then_inc(rowmax, 1)

                def shift(t):
                    a = heads(att[:, t.slot(2), :])
                    dve.wait_ge(rowmax, t.n + n0 + 1)
                    tt(a, a if s in (X1, X2) else heads(flat[:, 0:HK]), over_keys(mx[:, t.slot(2), :]), ALU.subtract)\
                        .then_inc(shifted, 1)

                def total(t):
                    dve.wait_ge(expd, t.n + n0 + 3)
                    v.tensor_reduce(rs[:, t.slot(2), :], heads(att[:, 2 + t.slot(2), :]), AX.X, ALU.add)\
                        .then_inc(rowsum, 1)

                def invert(t):
                    dve.wait_ge(rowsum, t.n + n0 + 1)
                    dve.wait_ge(probs, t.n + n0 + 1)
                    v.reciprocal(ri[:, t.slot(2), :], rs[:, t.slot(2), :]).then_inc(recip, 1)

                def early_moments(t):
                    if isinstance(t.n, int) and 0 <= t.n - (NT - TB) < EARLY:
                        b = t.n - (NT - TB)
                        dve.wait_ge(x_new, XNEW0[s] + (B if s == X3 else 0) + (b + 1) * TB)
                        moments(ROUND0[s + 1] + b, rows_of(x, b), b)

                def update(t):
                    dve.wait_ge(attn_out, t.n + n0 + 3)
                    xt = x[:, bass.ds(t.n, 1), :].rearrange("p t d -> p (t d)")
                    stt(xt, ps[:, 6 + t.slot(2), 0:D], tg[:, LAYER[s]:LAYER[s] + 1], xt, ALU.mult, ALU.add)\
                        .then_inc(x_new, 1)

                def late_bias(t):
                    if s in (X0, X3) and isinstance(t.n, int) and t.n == 1:
                        add_output_bias(s)

                if s in (X1, X2):
                    steps = [(add_to_scores, 0), (total, 1), (largest, 0), (invert, 1), (shift, 0)]
                else:
                    steps = [(largest, 0), (shift, 0), (total, 1), (invert, 1)]
                skewed_loop(dve, steps + [(late_bias, 0), (update, 3), (early_moments, 3)], NT, TB)

            def gate(s, n, base, tanh):
                c = Chain(dve, gate_chain, base)
                g = lambda k: G[:, k, :, :]
                one = lambda k: G[:, 3, :, k:k + 1]
                wide_ = lambda a: a.to_broadcast([P, NT, E])
                desc = w("desc").unsqueeze(1).to_broadcast([P, NT, E])
                lg = ps[:, 6, 0:NT * E].rearrange("p (i e) -> p i e", e=E)
                dve.wait_ge(router_ps, (n + 1) * B)

                def first_largest(src, k, m, m2):
                    c.link(v.tensor_reduce(one(m), src, AX.X, ALU.max))
                    c.link(tt(g(k), src, wide_(one(m)), ALU.subtract))
                    c.link(stt(g(k + 1), g(k), 0.0, desc, ALU.is_ge, ALU.mult))
                    c.link(v.tensor_reduce(one(m2), g(k + 1), AX.X, ALU.max))
                    c.link(tt(g(k + 1), g(k + 1), wide_(one(m2)), ALU.is_equal))
                    return g(k + 1)

                if s == F0:
                    c.link(tt(g(0), lg, w("0rb").unsqueeze(1).to_broadcast([P, NT, E]), ALU.add))
                    c.link(v.tensor_reduce(one(0), g(0), AX.X, ALU.max))
                    c.link(tt(g(1), g(0), wide_(one(0)), ALU.subtract))
                    c.link(stt(g(5), g(1), 0.0, desc, ALU.is_ge, ALU.mult))
                    c.link(v.tensor_reduce(one(1), g(5), AX.X, ALU.max))
                    c.link(tt(g(5), g(5), wide_(one(1)), ALU.is_equal))
                    dve.wait_ge(exp_gate, n + 1)
                    c.link(v.tensor_reduce(one(2), g(2), AX.X, ALU.add))
                    c.link(v.reciprocal(one(3), one(2)))
                    stt(w_all[:, :, :], g(5), tanh, wide_(one(3)), ALU.mult, ALU.mult).then_inc(w_ready, 1)
                    dve.wait_ge(w_ready, n + 1)
                    assert c.k == TOP1, c.k
                    return
                c.link(v.tensor_copy(g(0), lg))
                oh1 = first_largest(g(0), 4, 0, 1)
                c.link(stt(g(6), oh1, NEG, g(0), ALU.mult, ALU.add))
                c.link(v.tensor_reduce(one(2), g(6), AX.X, ALU.max))
                c.link(tt(g(7), g(6), wide_(one(2)), ALU.subtract))
                c.link(stt(g(8), g(7), 0.0, desc, ALU.is_ge, ALU.mult))
                c.link(v.tensor_reduce(one(3), g(8), AX.X, ALU.max))
                c.link(tt(G[:, 10, :, 0:1], one(2), one(0), ALU.subtract))
                c.link(tt(g(8), g(8), wide_(one(3)), ALU.is_equal))
                dve.wait_ge(exp_gate, n + 1)
                ex = G[:, 11, :, 0:1]
                c.link(ts(one(4), ex, 1.0, None, ALU.add))
                c.link(v.reciprocal(one(5), one(4)))
                if tanh is not None:
                    c.link(ts(one(5), one(5), tanh, None, ALU.mult))
                c.link(tt(one(6), ex, one(5), ALU.mult))
                c.link(tt(g(7), oh1, wide_(one(5)), ALU.mult))
                c.link(tt(g(8), g(8), wide_(one(6)), ALU.mult))
                tt(w_all[:, :, :], g(7), g(8), ALU.add).then_inc(w_ready, 1)
                dve.wait_ge(w_ready, n + 1)
                assert c.k == (TOP2 if s == F1 else TOP2N), c.k

            def add_weighted_bias(n):
                for b in range(B):
                    dve.wait_ge(wb_ps, n * B + b + 1)
                    xb = x[:, tok(b, 0, TB), :]
                    tt(xb, xb, ps[:, 2 + b, :].rearrange("p (i d) -> p i d", d=D), ALU.add).then_inc(x_new, 1)

            def experts(s, J, acc):
                units = E * J
                u0 = UNIT0[s]
                bias = 1 if s == F1 else 0
                per = E * TB + bias
                x0 = XNEW0[s]
                w0 = 0 if s == F1 else B
                dve.wait_ge(w_ready, 3 if s == MOE else 2)
                with dve.Fori(0, B) as c:
                    dve.wait_ge(x_new, c * per + x0)
                    v.tensor_copy(w_c[:, :, :], w_all[:, tok(c, 0, TB), :]).then_inc(scratch_w, 1)
                    dve.wait_ge(scratch_w, c + w0 + 1)

                    def gate_unit(u):
                        e, j = divmod(u, J)
                        dve.wait_ge(silu, c * units + u0 + u + 1)
                        dve.wait_ge(down_ps, c * units + u0 + u + 1)
                        stt(hh[:, u % 2, :], ps[:, 2 + u % 2, :], bgi[:, 1, e, j:j + 1], sg[:, u % 2, :],
                            ALU.add, ALU.mult).then_inc(gated, 1)

                    def add_expert(e):
                        dve.wait_ge(down_ps, c * units + u0 + (e + 1) * J + 2)
                        if s == F1 and e == 0:
                            dve.wait_ge(wb_ps, c + B + 1)
                            xb = x[:, tok(c, 0, TB), :]
                            tt(xb, xb, ps[:, 7, :].rearrange("p (i d) -> p i d", d=D), ALU.add).then_inc(x_new, 1)
                        if e + bias >= 1:
                            dve.wait_ge(x_new, c * per + bias + e * TB + x0)
                        for i in range(TB):
                            a = row(acc, c, i)
                            stt(a, ps[:, 4 + e % 2, i * D:(i + 1) * D], w_c[:, i, e:e + 1], a, ALU.mult, ALU.add)\
                                .then_inc(x_new, 1)
                    for e in range(E):
                        for j in range(J):
                            if s == F1:
                                gate_unit(e * J + j)
                            if j == 0 and e > 0:
                                add_expert(e - 1)
                    add_expert(E - 1)

            dve.wait_ge(ld["a"], 16)
            v.tensor_copy(identb[:, :], w("ident")).then_inc(bf_done, 1)
            dve.wait_ge(ld["x"], 16)
            norm_x(X0)
            block_keys(X0)
            dve.wait_ge(tanh_done, 1)
            cross(X0)

            starts(dve, F0)
            dve.wait_ge(ld["b"], 16)
            norm_x(F0, EARLY)
            gate(F0, 0, 0, tg[:, 4:5])
            add_weighted_bias(0)

            def weigh_experts(t):
                dve.wait_ge(e0_ps, t.n + 3)
                dve.wait_ge(e0_summed, t.n + 1)
                ys = flat[:, 6 * BANK * t.slot(2):(6 * t.slot(2) + 2) * BANK].rearrange("p (e d) -> p e d", d=D)
                wt = w_all[:, bass.ds(t.n, 1), :].rearrange("p t e -> p (t e)").unsqueeze(2).to_broadcast([P, E, D])
                tt(wide[:, t.slot(2)], ys, wt, ALU.mult).then_inc(e0_read, 1)

            def sum_experts(t):
                dve.wait_ge(e0_read, t.n + 3)
                dve.wait_ge(x_new, t.n + XNEW0[F0] + B - 1)
                v.tensor_reduce(hsum[:, t.slot(2), :], wide[:, t.slot(2)].rearrange("p e d -> p d e"), AX.X, ALU.add)\
                    .then_inc(e0_summed, 1)

            def add_experts(t):
                dve.wait_ge(e0_summed, t.n + 3)
                xt = x[:, bass.ds(t.n, 1), :].rearrange("p t d -> p (t d)")
                tt(xt, xt, hsum[:, t.slot(2), :], ALU.add).then_inc(x_new, 1)
            dve.wait_ge(x_new, XNEW0[F0] + B)
            skewed_loop(dve, [(weigh_experts, 0), (sum_experts, 1), (add_experts, 2)], NT, TB)

            starts(dve, X1)
            dve.wait_ge(kv_ps, KV_PS0[X1] + 1)
            kv = [lambda i, r=r: ps[0:KEYS, i // 2, (2 * (i % 2) + r) * D:(2 * (i % 2) + r + 1) * D] for r in range(KV1)]
            n0, t0 = ROUND0[X1], TURN0[X1]
            for r in range(KV1):
                moments(n0 - KV1 + r, kv[r], r, rows=KEYS)
            for r in range(KV1):
                normed(n0 - KV1 + r, t0 - KV1 + r, kv[r], xn_of(t0 - KV1 + r, KEYS), r, rows=KEYS)
            dve.wait_ge(s_xn, TB * n0)
            norm_x(X1)
            block_keys(X1)
            for b in range(B):
                dve.wait_ge(q_ps, b + B + 1)
                moments(n0 + B + b, lambda i: ps[:, 3 + b, i * D:(i + 1) * D], b)
            for b in range(B):
                normed(n0 + B + b, t0 + B + b, lambda i: ps[:, 3 + b, i * D:(i + 1) * D], xn_of(t0 + B + b), b)
            dve.wait_ge(mneg_set, 1)
            cross(X1)

            starts(dve, F1)
            norm_x(F1, EARLY)
            gate(F1, 1, TOP1, tg[:, 5:6])
            dve.wait_ge(ld["bgi"], 16)
            experts(F1, J1, x)

            starts(dve, X2)
            moments_of_x(X2)
            dve.wait_ge(ld["c"], 16)
            for u in range(1, 3 * H, 2):
                dve.wait_ge(fold_ps, u + 1)
                v.tensor_copy(folded(u), ps[:, u % 6, 0:CK].rearrange("p (b k) -> p b k", k=KEYS)).then_inc(fold_dve, 1)
            dve.wait_ge(ld["d"], 16)
            v.tensor_copy(heads(cmaskb[:, :]), w("2cm").unsqueeze(1).to_broadcast([P, H, KEYS])).then_inc(bf_done, 1)
            v.tensor_copy(diagb[:, :], w("mcm")).then_inc(bf_done, 1)
            for b in range(B):
                normed(ROUND0[X2] + b, TURN0[X2] + b, rows_of(x, b), xn_of(TURN0[X2] + b), b)
            add_output_bias(X2)
            dve.wait_ge(fold_dve, 3 * H // 2)
            cross(X2)

            starts(dve, MLA)
            n0 = ROUND0[MLA]
            moments_of_x(MLA, EARLY)
            dve.wait_ge(s_rstd, n0 + B)
            tt(msq[:, :], rstd[:, :], rstd[:, :], ALU.mult).then_inc(scratch, 1)
            dve.wait_ge(scratch, 1)
            tt(msq[:, :], msq[:, :], mv[:, :, 1], ALU.mult).then_inc(scratch, 1)
            dve.wait_ge(scratch, 2)
            ts(msq[:, :], msq[:, :], RMS_EPS, None, ALU.add).then_inc(s_ve, B)
            for b in range(B):
                normed(n0 + b, None, rows_of(x, b), rows_of(y, b), b)
            dve.wait_ge(s_xn, TB * (n0 + B))
            norm_y(MLA, n0 + B, rrms)

            c = Chain(dve, v_chain)
            for b in range(B):
                dve.wait_ge(v_ps, b + 1)
                heads_of = lambda a: a.rearrange("p (t h d) -> p t h d", h=H, d=HD)
                piece = lambda k: VP[:, b * TB:(b + 1) * TB, :, k, 0:HD]
                c.link(v.tensor_copy(piece(0), heads_of(ps[:, b, :])))
                c.link(tt(heads_of(v_rest), heads_of(ps[:, b, :]), piece(0), ALU.subtract))
                c.link(v.tensor_copy(piece(1), heads_of(v_rest)))
                tt(piece(2), heads_of(v_rest), piece(1), ALU.subtract).then_inc(v_split, 1)
                dve.wait_ge(v_split, b + 1)
            def maxima(t, tiles):
                for i in tiles:
                    dve.wait_ge(m_scores, t.n * 4 + i + 9)
                    v.tensor_reduce(negm[:, t.slot(2), i:i + 1], ps[:, i, 0:(i + 1) * P], AX.X, ALU.max, negate=True)\
                        .then_inc(m_rowmax, 1)

            def low_half(t):
                n = t.n
                for k in range(3):
                    dve.wait_ge(m_high, n * 3 + k + 1)
                    m = min(4, len(BLOCKS) - 4 * k)
                    high, low = (PH[:, t.slot(2), half, 4 * k:4 * k + m, :].rearrange("p c n -> p (c n)")
                                 for half in range(2))
                    stt(low, ps[:, 4 + k, 0:m * P], PSCALE, high, ALU.mult, ALU.subtract).then_inc(m_probsT, 1)

            def sum_pieces(t):
                dve.wait_ge(m_attn, t.n + 3)
                dve.wait_ge(m_normed, t.n + 1)
                o = ps[:, 7, 0:TB * PIECES * VE].rearrange("p (i c d) -> p i d c", c=PIECES, d=VE)
                v.tensor_reduce(o_sum[:, :, :], o, AX.X, ALU.add).then_inc(m_summed, 1)

            def invert(t):
                dve.wait_ge(m_summed, t.n + 2)
                v.reciprocal(rec[:, :].unsqueeze(2), o_sum[:, :, HD:VE]).then_inc(m_rec, 1)

            def divide(t):
                b, h = batch_and_head(t)
                dve.wait_ge(m_rec, t.n + 1)
                tt(o_s[:, tok(b, 0, TB), bass.ds(h * HD, HD)], o_sum[:, :, 0:HD],
                   rec[:, :].unsqueeze(2).to_broadcast([P, TB, HD]), ALU.mult).then_inc(m_normed, 1)
            skewed_loop(dve, [(sum_pieces, 3), (lambda t: maxima(t, [0]), 0), (invert, 3), (lambda t: maxima(t, [1]), 0),
                              (divide, 3), (lambda t: maxima(t, [2, 3]), 0), (low_half, 1)], B * H, 2)
            for b in range(B):
                dve.wait_ge(yo_ps, b + 1)
                yb = y[:, tok(b, 0, TB), :]
                tt(yb, yb, ps[:, 4 + b, :].rearrange("p (i d) -> p i d", d=D), ALU.add).then_inc(x_new, 1)
                if b >= 1:
                    dve.wait_ge(x_new, XNEW0[MLA] + b)
                    moments(ROUND0[MOE] + b - 1, rows_of(y, b - 1), b - 1, rms=b + 2)

            starts(dve, MOE)
            moments(ROUND0[MOE] + B - 1, rows_of(y, B - 1), B - 1, rms=B + 2)
            norm_y(MOE, ROUND0[MOE], rstd)
            gate(MOE, 2, TOP1 + TOP2, None)
            experts(MOE, J2, y)

            starts(dve, X3)
            dve.wait_ge(ld["e"], 16)
            dve.wait_ge(ld["m3"], 16)
            dve.wait_ge(ld["rope"], 16)
            dve.wait_ge(kv_ps, KV_PS0[X3] + 3)
            c = Chain(dve, kv_chain)
            perb = lambda a: a.rearrange("p (b k) -> p b k", k=KEYS)
            table = lambda a: a[:, 0:KEYS].unsqueeze(1).to_broadcast([P, B, KEYS])
            c.link(v.tensor_copy(mask3_f[:, :], mask3_u8[:, :]))
            c.link(tt(perb(kA_s), perb(kT_s), table(cosT), ALU.mult))
            c.link(tt(perb(kB_s), perb(ps[:, 2, 0:CK]), table(sinT), ALU.mult))
            c.link(tt(kA_s, kA_s, kB_s, ALU.add))
            c.link(tt(kT_s, kA_s, mask3_f[:, :], ALU.mult))
            for b in range(B):
                xb, yb = x[:, tok(b, 0, TB), :], y[:, tok(b, 0, TB), :]
                stt(xb, yb, tg[:, 6:7], xb, ALU.mult, ALU.add).then_inc(x_new, 1)
            dve.wait_ge(x_new, XNEW0[X3] + B)
            norm_x(X3)
            block_keys(X3)
            c = Chain(dve, rope_chain)
            for b in range(B):
                dve.wait_ge(rot_ps, b + 1)
                c.link(tt(rope_a, FT[:, cols(b)], cosT, ALU.mult))
                c.link(tt(rope_b, ps[:, 3 + b % 3, :], sinT, ALU.mult))
                tt(FT[:, cols(b)], rope_a, rope_b, ALU.add).then_inc(roped, 1)
                dve.wait_ge(roped, b + 1)
            cross(X3)

            starts(dve, F3)
            ts(bo3[:, :], w("3fbo"), 0.3, None, ALU.mult).then_inc(y_set, 1)
            dve.wait_ge(y_set, 1)
            moments_of_x(F3, EARLY)
            for b in range(B):
                dve.wait_ge(y_set, max(b, 1))
                nth = TURN0[F3] + b
                normed(ROUND0[F3] + b, nth, rows_of(x, b), xn_of(nth), b)
                dve.wait_ge(s_xn, TB * (ROUND0[F3] + b + 1))
                tt(y[:, b * TB:(b + 1) * TB, :], xn_at[nth % 2][:, :, :],
                   bo3[:, :].unsqueeze(1).to_broadcast([P, TB, D]), ALU.add).then_inc(y_set, 1)
            dve.wait_ge(y_set, B + 1)
            dve.wait_ge(pol, 2)
            c = Chain(dve, sel_chain)
            lg = ps[:, 7, 0:B * E].rearrange("p (b e) -> p b e", e=E)
            of = lambda a: a.unsqueeze(1).to_broadcast([P, B, E])
            one = lambda k: G3[:, 3, :, k:k + 1]
            c.link(tt(G3[:, 0, :, :], lg, of(w("bp2")), ALU.add))
            c.link(v.tensor_reduce(one(0), G3[:, 0, :, :], AX.X, ALU.max))
            c.link(tt(G3[:, 1, :, :], G3[:, 0, :, :], one(0).to_broadcast([P, B, E]), ALU.subtract))
            c.link(stt(G3[:, 5, :, :], G3[:, 1, :, :], 0.0, of(w("desc")), ALU.is_ge, ALU.mult))
            c.link(v.tensor_reduce(one(1), G3[:, 5, :, :], AX.X, ALU.max))
            c.link(ts(G3[:, 4, :, 0:1], one(1), -1.0, float(E), ALU.mult, ALU.add))
            c.link(ts(chosen[:, :].unsqueeze(2), G3[:, 4, :, 0:1], float(E - 1), 0.0, ALU.min, ALU.max))
            expert = [nc.values_load(chosen[0:1, b:b + 1], engines=[mybir.EngineType.DVE], min_val=0, max_val=E - 1,
                                     skip_runtime_bounds_check_because="chosen is clamped to the experts above")
                      for b in range(B)]
            dve.wait_ge(ld["f3"], 16)

            def select(t):
                wait(dve, r3_ps, t.n - 1)
                wait(dve, r3_sb, t.n - 1)
                v.tensor_copy(sel[:, t.slot(2), :], W3F[:, bass.ds(expert[t.n], 1), :].rearrange("p e n -> p (e n)"))\
                    .then_inc(sel_done, 1)

            def finish(t):
                dve.wait_ge(o3_ps, t.n + 1)
                xb, yb = x[:, t.n * TB:(t.n + 1) * TB, :], y[:, t.n * TB:(t.n + 1) * TB, :]
                c.link(stt(yb, ps[:, 3, :].rearrange("p (i d) -> p i d", d=D), 0.3, yb, ALU.mult, ALU.add))
                stt(xb, yb, tg[:, 7:8], xb, ALU.mult, ALU.add).then_inc(x_new, 1)
            skewed_loop(dve, [(select, 0), (finish, 2)], B, 2)


def _columns(v):
    return v.reshape(-1, P).T


def _rows(v, n=P):
    out = np.zeros((P, v.size), v.dtype)
    out[:n] = v
    return out


def _pad(a):
    out = np.zeros((P, a.shape[1]), a.dtype)
    out[:a.shape[0]] = a
    return out


def _pack(i):
    f = np.float32
    ident = np.eye(P, dtype=f)
    rot = np.zeros((P, P), f)
    for k in range(0, P, 2):
        rot[k + 1, k] = -1.0
        rot[k, k + 1] = 1.0
    causal = np.where(np.arange(KEYS)[None, :] > np.arange(P)[:, None], f(-1e30), f(0)).astype(f)
    diag = np.where(np.arange(P)[None, :] > np.arange(P)[:, None], f(-1e30), f(0)).astype(f)
    two = lambda a: a.reshape(8, P, D).transpose(1, 0, 2).reshape(P, 8 * D)
    v = {
        "ident": ident,
        "hm": (np.arange(P)[:, None] // HD == np.arange(H)[None, :]).astype(f),
        "desc": np.tile(np.arange(E, 0, -1, dtype=f), (P, 1)),
        "gates": _rows(np.concatenate([i["g_xattn"], i["g_ffn"]])),
        "ctxT": i["ctx_1024"].reshape(CK, D).T,
        "0wq": i["L0_xattn_Wq"].T, "0wk": i["L0_xattn_Wk"].T, "0wv": i["L0_xattn_Wv"].T, "0wo": i["L0_xattn_Wo"].T,
        "0b": np.stack([i["L0_xattn_bq"], i["L0_xattn_bk"], i["L0_xattn_bv"]], 1),
        "0bo": _rows(i["L0_xattn_bo"], KEYS),
        "0we": i["L0_ffn_expert_w"].transpose(1, 0, 2).reshape(P, E * D),
        "0eb": _pad(i["L0_ffn_expert_b"]), "0rw": i["L0_ffn_router_w"], "0rb": _rows(i["L0_ffn_router_b"]),
        "1wq": i["L1_xattn_Wq"], "1wkv": np.concatenate([i["L1_xattn_Wk"], i["L1_xattn_Wv"]], 1),
        "1gb": np.stack([i["L1_xattn_" + k] for k in ("gq", "bq", "gk", "bk", "gv", "bv")], 1),
        "1gw": i["L1_ffn_gate_w"].T, "1bo": _pad(i["L1_ffn_bo"]),
        "2wqT": two(i["L2_xattn_Wq"].T), "2wk": i["L2_xattn_Wk"], "2wv": i["L2_xattn_Wv"], "2wo": two(i["L2_xattn_Wo"]),
        "2b": np.concatenate([_columns(i["L2_xattn_" + k]) for k in ("bq", "bk", "bv")], 1),
        "2bo": _rows(i["L2_xattn_bo"], KEYS), "2cm": causal,
        "mwq": i["L2_ffn_Wq"], "mwd": i["L2_ffn_Wdkv"], "mwuk": _pad(i["L2_ffn_Wuk"]), "mwuv": _pad(i["L2_ffn_Wuv"]),
        "mwo": i["L2_ffn_Wo"], "mg": np.stack([i["L2_ffn_g1"], i["L2_ffn_g2"]], 1), "mgw": i["L2_ffn_gate_w"],
        "mcm": diag,
        "3wq": i["L3_xattn_w_q"], "3wk": i["L3_xattn_w_k"], "3wv": i["L3_xattn_w_v"], "3wo": i["L3_xattn_w_o"],
        "3b": np.stack([i["L3_xattn_b_q"], i["L3_xattn_b_k"], i["L3_xattn_b_v"]], 1),
        "3bo": _rows(i["L3_xattn_b_o"], KEYS), "rot": rot,
        "wp1": i["L3_ffn_Wp1"], "bp1": i["L3_ffn_bp1"][:, None], "wp2": i["L3_ffn_Wp2"], "bp2": _rows(i["L3_ffn_bp2"]),
        "3fwo": i["L3_ffn_Wo"], "3fbo": _rows(i["L3_ffn_bo"]),
    }
    order = [n for items in GROUPS.values() for n, _ in items]
    for n in order:
        assert v[n].shape == (P, PLACE[n][1]), (n, v[n].shape)
    return np.ascontiguousarray(np.concatenate([v[n] for n in order], 1))


def _rope():
    f = np.float32
    inv = (f(10000.0) ** (np.arange(0, HD, 2, dtype=f) / f(HD))).astype(f)
    theta = (np.arange(S, dtype=f)[:, None] / inv).astype(f)
    theta = np.tile(np.repeat(theta, 2, axis=1), (1, H)).T
    return np.ascontiguousarray(np.concatenate([np.cos(theta), np.sin(theta)], 1).astype(f))


def kernel(**inputs):
    import concourse.bacc as _bacc
    from concourse.bass_utils import run_bass_kernel_spmd as _run

    i = {k: np.asarray(a) for k, a in inputs.items()}

    def up(a):
        return a.transpose(2, 0, 1).reshape(D, -1)

    def down(a):
        e, h, d = a.shape
        return a.reshape(e, h // P, P, d).transpose(2, 0, 1, 3).reshape(P, -1)

    def cols_of(a):
        e, h = a.shape
        return a.reshape(e, h // P, P).transpose(2, 0, 1)

    arrays = {
        "x": i["x"].reshape(B * S, D),
        "packed": _pack(i),
        "ffn1": np.concatenate([up(i["L1_ffn_wg"]), up(i["L1_ffn_wi"]), down(i["L1_ffn_wo"].transpose(0, 2, 1)),
                                cols_of(i["L1_ffn_bg"]).reshape(P, -1), cols_of(i["L1_ffn_bi"]).reshape(P, -1)], 1),
        "moe": np.concatenate([i["L2_ffn_w1"].transpose(1, 0, 2).reshape(D, -1), down(i["L2_ffn_w2"])], 1),
        "ffn3": np.concatenate([i["L3_ffn_W1"].transpose(1, 0, 2), cols_of(i["L3_ffn_b1"]),
                                down(i["L3_ffn_W2"]).reshape(P, E, J2 * D), i["L3_ffn_b2"].T[:, :, None]],
                               2).reshape(P, -1),
        "rope": _rope(),
        "mask1": np.ascontiguousarray(i["mask_BxSxS2_bk0"]).reshape(-1).view(np.uint32),
        "mask3": np.ascontiguousarray(np.broadcast_to(i["mask_Bx1x1xS2_bf1"].reshape(1, CK), (P, CK))).view(np.uint8),
    }
    arrays = {f"in_{k}": np.ascontiguousarray(a) for k, a in arrays.items()}
    nc = _bacc.Bacc("TRN2", target_bir_lowering=False, num_devices=1)
    args = {k: nc.dram_tensor(k, a.shape, mybir.dt.from_np(a.dtype), kind="ExternalInput").ap()
            for k, a in arrays.items()}
    out = nc.dram_tensor("out_x", (B * S, D), F32, kind="ExternalOutput").ap()
    build(nc, args["in_x"], args["in_packed"], args["in_ffn1"], args["in_moe"], args["in_ffn3"], args["in_rope"],
          args["in_mask1"], args["in_mask3"], out)
    r = _run(nc, [arrays], core_ids=[0])
    return r.results[0]["out_x"].reshape(B, S, D)
```
